# Optimizing a Trainium2 kernel written in Bass

```python
import numpy as np
import jax
import jax.numpy as jnp

def _softmax(x, axis=-1):
    return jax.nn.softmax(x, axis=axis)

def _gelu(x):
    return jax.nn.gelu(x, approximate=True)

def _silu(x):
    return jax.nn.silu(x)

def _sigmoid(x):
    return jax.nn.sigmoid(x)

def _layernorm(x, axis=-1, eps=1e-05):
    m = jnp.mean(x, axis=axis, keepdims=True)
    v = jnp.var(x, axis=axis, keepdims=True)
    return (x - m) / jnp.sqrt(v + eps)

def _scatter_add(tgt, idx, src, axis=0):
    return tgt.at[idx].add(src)

def _segment_sum(src, seg, n):
    return jax.ops.segment_sum(src, seg, n)
kernel_name = 'mk_seq_postln_d1_jaxref_r4_80f470'

def setup_inputs(seed: int=0):
    np.random.seed(seed)
    _w = jnp.asarray

    def _L0_attn_setup():
        import jax, jax.numpy as jnp
        import numpy as np
        import math
        H = 16
        LORA_SCALING = 16 / 8
        NEG_INF = -1e+30

        def _alibi_slopes(n_heads):
            start = 2.0 ** (-2.0 ** (-(math.log2(n_heads) - 3)))
            return jnp.asarray([start * start ** i for i in range(n_heads)], dtype=jnp.float32)

        def _lora(x, W, A, Bm):
            return x @ W.T + x @ Bm.T @ A.T * LORA_SCALING
        key = jax.random.key(seed)
        ks = jax.random.split(key, 11)
        B, T, E, r = (4, 512, 256, 8)
        d = {'x': jax.random.normal(ks[0], (B, T, E), jnp.float32), 'Wq': jax.random.normal(ks[1], (E, E), jnp.float32) * E ** (-0.5), 'Aq': jax.random.normal(ks[2], (E, r), jnp.float32) * 0.01, 'Bq': jax.random.normal(ks[3], (r, E), jnp.float32) * 0.01, 'Wk': jax.random.normal(ks[4], (E, E), jnp.float32) * E ** (-0.5), 'Ak': jax.random.normal(ks[5], (E, r), jnp.float32) * 0.01, 'Bk': jax.random.normal(ks[6], (r, E), jnp.float32) * 0.01, 'Wv': jax.random.normal(ks[7], (E, E), jnp.float32) * E ** (-0.5), 'Av': jax.random.normal(ks[8], (E, r), jnp.float32) * 0.01, 'Bv': jax.random.normal(ks[9], (r, E), jnp.float32) * 0.01, 'Wp': jax.random.normal(ks[10], (E, E), jnp.float32) * E ** (-0.5)}
        return d
    _L0_attn_in = _L0_attn_setup()

    def _L0_ffn_setup():
        import math
        import jax, jax.numpy as jnp
        import numpy as np
        B, S, D, H, E, K = (4, 512, 256, 1024, 8, 2)
        CAPACITY_RATIO = 1.05
        key = jax.random.key(seed)
        k0, k1, k2, k3 = jax.random.split(key, 4)
        x = jax.random.normal(k0, (B, S, D), jnp.float32)
        Wg = jax.random.normal(k1, (D, E), jnp.float32) * 0.02
        W1 = jax.random.normal(k2, (E, D, H), jnp.float32) * 0.02
        b1 = jnp.zeros((E, H), jnp.float32)
        W2 = jax.random.normal(k3, (E, H, D), jnp.float32) * 0.02
        b2 = jnp.zeros((E, D), jnp.float32)
        return {'x': x, 'Wg': Wg, 'W1': W1, 'b1': b1, 'W2': W2, 'b2': b2}
    _L0_ffn_in = _L0_ffn_setup()
    _d = {'L0_attn_x': _L0_attn_in['x'], 'L0_attn_Wq': _L0_attn_in['Wq'], 'L0_attn_Aq': _L0_attn_in['Aq'], 'L0_attn_Bq': _L0_attn_in['Bq'], 'L0_attn_Wk': _L0_attn_in['Wk'], 'L0_attn_Ak': _L0_attn_in['Ak'], 'L0_attn_Bk': _L0_attn_in['Bk'], 'L0_attn_Wv': _L0_attn_in['Wv'], 'L0_attn_Av': _L0_attn_in['Av'], 'L0_attn_Bv': _L0_attn_in['Bv'], 'L0_attn_Wp': _L0_attn_in['Wp'], 'L0_ffn_Wg': _L0_ffn_in['Wg'], 'L0_ffn_W1': _L0_ffn_in['W1'], 'L0_ffn_b1': _L0_ffn_in['b1'], 'L0_ffn_W2': _L0_ffn_in['W2'], 'L0_ffn_b2': _L0_ffn_in['b2']}
    _x0 = _d['L0_attn_x']
    _d['L0_attn_x'] = jax.random.normal(jax.random.fold_in(jax.random.key(seed), 1), (1, 4096, 256), dtype=_x0.dtype)
    del _x0
    return _d

def reference(L0_attn_x, L0_attn_Wq, L0_attn_Aq, L0_attn_Bq, L0_attn_Wk, L0_attn_Ak, L0_attn_Bk, L0_attn_Wv, L0_attn_Av, L0_attn_Bv, L0_attn_Wp, L0_ffn_Wg, L0_ffn_W1, L0_ffn_b1, L0_ffn_W2, L0_ffn_b2):

    def _L0_attn_ref(x, Wq, Aq, Bq, Wk, Ak, Bk, Wv, Av, Bv, Wp):
        import jax, jax.numpy as jnp
        import numpy as np
        import math
        H = 16
        LORA_SCALING = 16 / 8
        NEG_INF = -1e+30

        def _alibi_slopes(n_heads):
            start = 2.0 ** (-2.0 ** (-(math.log2(n_heads) - 3)))
            return jnp.asarray([start * start ** i for i in range(n_heads)], dtype=jnp.float32)

        def _lora(x, W, A, Bm):
            return x @ W.T + x @ Bm.T @ A.T * LORA_SCALING
        B, T, E = x.shape
        dh = E // H
        q = _lora(x, Wq, Aq, Bq).reshape(B, T, H, dh).transpose(0, 2, 1, 3)
        k = _lora(x, Wk, Ak, Bk).reshape(B, T, H, dh).transpose(0, 2, 1, 3)
        v = _lora(x, Wv, Av, Bv).reshape(B, T, H, dh).transpose(0, 2, 1, 3)
        s = jnp.einsum('bhqd,bhkd->bhqk', q, k) / jnp.sqrt(jnp.float32(dh))
        i = jnp.arange(T)[:, None]
        j = jnp.arange(T)[None, :]
        slopes = _alibi_slopes(H)
        bias = slopes[:, None, None] * (i - j).astype(jnp.float32)
        s = s + bias[None]
        s = jnp.where(j[None, None] <= i[None, None], s, NEG_INF)
        out = jnp.einsum('bhqk,bhkd->bhqd', jax.nn.softmax(s, axis=-1), v)
        out = out.transpose(0, 2, 1, 3).reshape(B, T, E)
        return out @ Wp.T

    def _L0_ffn_ref(x, Wg, W1, b1, W2, b2):
        import math
        import jax, jax.numpy as jnp
        import numpy as np
        B, S, D, H, E, K = (4, 512, 256, 1024, 8, 2)
        CAPACITY_RATIO = 1.05
        b, s, d = x.shape
        e = Wg.shape[1]
        n = b * s
        cap = int(math.ceil(n * K / e * CAPACITY_RATIO))
        xf = x.reshape(n, d)
        probs = jax.nn.softmax(xf @ Wg, axis=-1)
        topv, topi = jax.lax.top_k(probs, K)
        gates = topv / jnp.sum(topv, axis=-1, keepdims=True)
        eidx = topi.reshape(-1)
        oh = jax.nn.one_hot(eidx, e, dtype=jnp.int32)
        pos = jnp.sum(jnp.cumsum(oh, axis=0) * oh, axis=-1) - 1
        keep = pos < cap
        dest = jnp.where(keep, eidx * cap + pos, e * cap)
        xr = jnp.repeat(xf, K, axis=0)
        buf = jnp.zeros((e * cap + 1, d), x.dtype).at[dest].set(xr)
        expert_in = buf[:e * cap].reshape(e, cap, d)
        h = jax.nn.gelu(jnp.einsum('ecd,edh->ech', expert_in, W1) + b1[:, None, :])
        y = jnp.einsum('ech,ehd->ecd', h, W2) + b2[:, None, :]
        yf = jnp.concatenate([y.reshape(e * cap, d), jnp.zeros((1, d), y.dtype)], axis=0)
        gathered = yf[dest]
        w = (gates.reshape(-1) * keep.astype(gates.dtype))[:, None]
        out = (gathered * w).reshape(n, K, d).sum(axis=1).reshape(b, s, d)
        return out
    x = L0_attn_x
    x = _layernorm(x + _L0_attn_ref(x, L0_attn_Wq, L0_attn_Aq, L0_attn_Bq, L0_attn_Wk, L0_attn_Ak, L0_attn_Bk, L0_attn_Wv, L0_attn_Av, L0_attn_Bv, L0_attn_Wp), axis=-1)
    x = _layernorm(x + _L0_ffn_ref(x, L0_ffn_Wg, L0_ffn_W1, L0_ffn_b1, L0_ffn_W2, L0_ffn_b2), axis=-1)
    return x

_drawn_inputs = setup_inputs


def setup_inputs(seed=0):
    import zlib

    import numpy as np

    out = dict(_drawn_inputs(seed))
    spreads = {'L0_ffn_b1': (0.0, 0.328), 'L0_ffn_b2': (0.0, 0.1)}
    factors = {'L0_attn_Aq': 8.0,
     'L0_attn_Bq': 8.0,
     'L0_attn_Ak': 8.0,
     'L0_attn_Bk': 8.0,
     'L0_attn_Av': 7.919,
     'L0_attn_Bv': 8.0}
    for name, (base, spread) in spreads.items():
        noise = np.random.default_rng([zlib.crc32(name.encode()), seed]).standard_normal(out[name].shape)
        drawn = base * np.exp(spread * noise) if base else spread * noise
        out[name] = jnp.asarray(drawn.astype(out[name].dtype))
    for name, factor in factors.items():
        out[name] = (out[name] * factor).astype(out[name].dtype)
    return out
```

```python
import math
from contextlib import ExitStack

import numpy as np

import concourse.bass as bass
from concourse import mybir

F32 = mybir.dt.float32
BF16 = mybir.dt.bfloat16
I32 = mybir.dt.int32
U32 = mybir.dt.uint32
ACT = mybir.ActivationFunctionType
ALU = mybir.AluOpType
AX = mybir.AxisListType

P = 128
T = 4096
D = 256
H = 16
DH = D // H
G = 4
NG = H // G
QB = 512
NB = T // QB
KT = QB // P
R = 8
LORA_SCALE = 2.0
EPS = 1e-5

PAIRS = [(0, 0), (0, 1), (1, 0), (1, 1), (0, 2), (2, 0)]
NP_ROWS = 16 * len(PAIRS)
ROW_BIAS = NP_ROWS
ROW_SHIFT = NP_ROWS + 3
KROWS = NP_ROWS + 6
BOUND = 60.0
MASKED = -1e30

E = 8
HID = 1024
CAP = int(math.ceil(T * 2 / E * 1.05))
SLOTS = E * CAP
DROPPED = SLOTS
HC = HID // P
ST = -(-CAP // P)
LAST = CAP - (ST - 1) * P
ZERO_COLS = SLOTS * D // P // NB
assert ZERO_COLS * NB * P == SLOTS * D


def alone(eng):
    eng.sem_inc(PASSED["sem"], 1)


PASSED = {}


class Chain:

    def __init__(self, eng, sem, base, steps):
        self.eng, self.sem, self.base, self.steps, self.n = eng, sem, base, steps, 0

    def did(self, ins):
        self.n += 1
        ins.then_inc(self.sem, 1)

    def wait(self):
        self.eng.wait_ge(self.sem, self.base + self.n)

    def end(self):
        assert self.n == self.steps, (self.n, self.steps)


def tiles_before(g, b):
    return g * (2 * NB * (NB + 1)) + 2 * b * (b + 1)


def build(nc, io):
    with ExitStack() as ctx:
        def sb(name, shape, dt, c=ctx):
            return c.enter_context(nc.sbuf_tensor(name, shape, dt))

        def psum(name, shape, dt, c):
            return c.enter_context(nc.psum_tensor(name, shape, dt))

        def sem(name):
            return ctx.enter_context(nc.semaphore(name))

        def dram(name, shape, dt):
            return nc.dram_tensor(name, shape, dt, kind="Internal").ap()

        parts = {m: dram(f"parts_{m}", (3, D, T), BF16) for m in "qk"}
        shift = dram("shift", (H, 3, T), BF16)
        attnT = dram("attnT", (D, T), F32)
        slots_x = dram("slots_x", (SLOTS + 1, D), F32)
        slots_y = dram("slots_y", (SLOTS + 1, D), F32)

        flag = sb("flag", [1, 1], I32)
        x1_all = sb("x1_all", [P, NB, KT, D], F32)
        dest_all = sb("dest_all", [P, NB, KT * 2], U32)
        weight_all = sb("weight_all", [P, NB, KT * 2], F32)
        PASSED["sem"] = sem("passed")
        with ExitStack() as mid:
            r = Router(io, lambda n, sh, dt: sb(n, sh, dt, mid), sem, attnT, slots_x, x1_all, dest_all, weight_all)
            attention(nc, io, sb, psum, sem, parts, shift, attnT, flag, slots_x, slots_y, r)
            with ExitStack() as st:
                x = Experts(lambda n, sh, dt: sb(n, sh, dt, st), sem)
                route_last(nc, io, psum, r, x)
                experts(nc, io, psum, slots_x, slots_y, x, st)
        combine(nc, io, sb, psum, sem, x1_all, slots_y, dest_all, weight_all)


def attention(nc, io, sb, psum, sem, parts, shift, attnT, flag, slots_x, slots_y, r):
    with ExitStack() as big:
        v_sb = sb("v_sb", [P, T // P, D], F32, big)
        kop = sb("kop", [KROWS, 2, G, T], BF16, big)
        qop = sb("qop", [KROWS, 2, G, QB], BF16, big)
        ident_b = sb("ident_b", [P, P], BF16, big)
        cmask = sb("cmask", [P, P], BF16, big)
        v_stage = sb("v_stage", [P, KT, G, 32], F32, big)

        project(nc, io, sb, psum, sem, parts, shift, flag, v_sb, qop, ident_b, cmask, v_stage,
                slots_x, slots_y, r.x1[:].rearrange("p n t d -> p (n t d)"))
        exact_maxima(nc, io, sb, psum, sem, parts, shift, flag, kop, qop, ident_b)
        attend(nc, io, sb, psum, sem, parts, shift, attnT, kop, qop, ident_b, cmask, v_stage, v_sb, r)



def project(nc, io, sb, psum, sem, parts, shift, flag, v_sb, qop, ident_b, cmask, v_stage,
            slots_x, slots_y, spare):
    with ExitStack() as st:
        wT = sb("wT", [P, 3, 2, D], F32, st)
        loA = sb("loA", [R, 3, D], F32, st)
        loB = sb("loB", [R, 3, D], F32, st)
        weff = sb("weff", [P, 3, 2, D], F32, st)
        xT = sb("xT", [P, 2, 2, QB], F32, st)
        part = sb("part", [P, 4, 3, QB], BF16, st)
        resid = sb("resid", [P, 2, QB], F32, st)
        sq = sb("sq", [P, 2, QB], BF16, st)
        hsel = sb("hsel", [P, 8], BF16, st)
        ident8 = sb("ident8", [8, 8], F32, st)
        nmax = sb("nmax", [8, 4, NB], F32, st)
        nm = sb("nm", [8, 4], F32, st)
        bnd = sb("bnd", [8, 2], F32, st)
        bnd1 = sb("bnd1", [8, 1], F32, st)
        one = sb("one", [1, 2], F32, st)
        zeros = spare[:, 0:ZERO_COLS]
        warm = sb("warm", [1, 1], F32, st)
        zero_set = sem("zero_set")
        zero_out = sem("zero_out")
        ps_p = psum("ps_p", [P, 4, QB], F32, st)
        ps_v = psum("ps_v", [P, 2, 2, D], F32, st)
        ps_n = psum("ps_n", [P, 2, QB], F32, st)

        w_loaded = sem("w_loaded")
        small_loaded = sem("small_loaded")
        x_loaded = [sem(f"x_loaded{u}") for u in range(2)]
        lora_mm = sem("lora_mm")
        weff_done = sem("weff_done")
        proj_mm = sem("proj_mm")
        v_mm = sem("v_mm")
        v_out = sem("v_out")
        head_done = sem("head_done")
        sq_done = sem("sq_done")
        resid_done = sem("resid_done")
        mid_done = sem("mid_done")
        tail_done = sem("tail_done")
        norm_mm = sem("norm_mm")
        norm_max = sem("norm_max")
        stored = [sem(f"stored{m}") for m in range(4)]
        shift_out = sem("shift_out")
        bnd_step = sem("bnd_step")
        bnd_T = sem("bnd_T")
        ones_set = sem("ones_set")

        nc.sync.sem_inc(resid_done, 4)
        nc.sync.sem_inc(sq_done, 4)
        nc.sync.sem_inc(norm_mm, 2)
        nc.sync.sem_inc(norm_max, 2)
        nc.sync.sem_inc(tail_done, 2)
        nc.sync.sem_inc(v_out, 2)
        for s in stored:
            nc.sync.sem_inc(s, 16)

        xT_d = io["xT"].rearrange("(c p) t -> p c t", p=P)
        with nc.Block() as block:
            @block.sync
            def _(sp):
                for m, w in enumerate("qkv"):
                    sp.dma_start(loA[:, m, :], io["A" + w]).then_inc(w_loaded, 16)
                    sp.dma_start(loB[:, m, :], io["B" + w]).then_inc(w_loaded, 16)
                    sp.dma_start(wT[:, m], io["W" + w].rearrange("(c p) o -> p c o", p=P)).then_inc(w_loaded, 16)
                for u in range(2):
                    sp.dma_start(xT[:, u], xT_d[:, :, u * QB:(u + 1) * QB]).then_inc(x_loaded[u], 16)
                sp.dma_start(hsel[:], io["headsel"]).then_inc(small_loaded, 16)
                sp.dma_start(ident8[:], io["ident"][0:8, 0:8]).then_inc(small_loaded, 16)
                sp.dma_start(ident_b[:], io["ident_b"]).then_inc(small_loaded, 16)
                sp.dma_start(cmask[:], io["cmask"]).then_inc(small_loaded, 16)
                for s in range(2):
                    sp.dma_start(qop[ROW_BIAS:ROW_SHIFT, s], io["q_const"][0:3]).then_inc(small_loaded, 16)
                sp.dma_start(shift.rearrange("h a t -> h (a t)"), io["no_shift"]).then_inc(shift_out, 16)

                def store(m, tb):
                    sp.wait_ge(tail_done, tb * 4 + (m + 1 + 2))
                    dst = parts["qk"[m // 2]][:, (m % 2) * P:(m % 2 + 1) * P, bass.ds(tb * QB, QB)]
                    sp.dma_start(dst.rearrange("a p t -> p a t"), part[:, m]).then_inc(stored[m], 16)

                with sp.Fori(0, NB // 2 - 1) as i:
                    for u in range(2):
                        tb = 2 * i + u
                        for m in range(4):
                            store(m, tb)
                        sp.wait_ge(v_mm, tb * 2 + 2)
                        sp.dma_start(xT[:, u], xT_d[:, :, bass.ds((tb + 2) * QB, QB)]).then_inc(x_loaded[u], 16)
                for tb in range(NB - 2, NB):
                    for m in range(4):
                        store(m, tb)
                sp.wait_ge(small_loaded, 16 * 6)
                for m in range(4):
                    sp.wait_ge(stored[m], 16 * (NB + 1))
                sp.wait_ge(shift_out, 16)

            @block.tensor
            def _(pe):
                pe.wait_ge(w_loaded, 16 * 9)
                for m in range(3):
                    for c in range(2):
                        mm = pe.matmul(ps_p[:, m, c * D:(c + 1) * D], loB[:, m, c * P:(c + 1) * P], loA[:, m, :],
                                       start=True, stop=True)
                mm.then_inc(lora_mm, 1)
                pe.wait_ge(weff_done, 6)
                pe.wait_ge(small_loaded, 16 * 6)

                def norm(m, tb):
                    pe.wait_ge(sq_done, tb * 4 + (m + 1 + 4))
                    pe.wait_ge(norm_max, tb * 4 + (m + 1))
                    pe.matmul(ps_n[0:8, m % 2, :], hsel[:], sq[:, m % 2, :], start=True, stop=True).then_inc(norm_mm, 1)

                def block_of(tb, u, i):
                    pe.wait_ge(x_loaded[u], i * 16 + 16)
                    for m in range(4):
                        pe.wait_ge(resid_done, tb * 4 + (m + 1))
                        pe.wait_ge(sq_done, tb * 4 + (m + 1))
                        for c in range(2):
                            mm = pe.matmul(ps_p[:, m, :], weff[:, m // 2, c, (m % 2) * P:(m % 2 + 1) * P],
                                           xT[:, u, c, :], start=(c == 0), stop=(c == 1))
                        mm.then_inc(proj_mm, 1)
                        if m >= 1:
                            norm(m - 1, tb)
                    for j in range(2):
                        pe.wait_ge(v_out, tb * 2 + (j + 1))
                        for s in range(2):
                            for c in range(2):
                                mm = pe.matmul(ps_v[:, j, s, :], xT[:, u, c, (2 * j + s) * P:(2 * j + s + 1) * P],
                                               weff[:, 2, c, :], start=(c == 0), stop=(c == 1))
                        mm.then_inc(v_mm, 1)
                        if j == 0:
                            norm(3, tb)

                with pe.Fori(0, NB // 2) as i:
                    for u in range(2):
                        block_of(2 * i + u, u, i)
                pe.wait_ge(bnd_step, 3)
                pe.transpose(ps_n[0:1, 0, 0:8], bnd1[:], ident8[:]).then_inc(bnd_T, 1)

            @block.scalar
            def _(act):
                def tile(m, tb):
                    scale = 0.25 if m < 2 else 1.0
                    act.wait_ge(proj_mm, tb * 4 + (m + 1))
                    act.wait_ge(stored[m], tb * 16 + 16)
                    act.activation(part[:, m, 0, :], ps_p[:, m, :], ACT.Identity, scale=scale).then_inc(head_done, 1)
                    act.wait_ge(norm_mm, tb * 4 + (m + 1))
                    act.activation(sq[:, m % 2, :], ps_p[:, m, :], ACT.Square, scale=scale).then_inc(sq_done, 1)

                act.wait_ge(ones_set, 1)
                act.activation(warm[:], v_stage[0:1, 0, 0, 0:1], ACT.Exp)
                with act.Fori(0, NB) as tb:
                    for m in range(4):
                        tile(m, tb)
                    for j in range(2):
                        act.wait_ge(v_mm, tb * 2 + (j + 1))
                        alone(act)
                        act.activation(v_sb[:, bass.ds(tb * 4 + 2 * j, 2), :], ps_v[:, j], ACT.Identity).then_inc(v_out, 1)

            @block.vector
            def _(dve):
                dve.memset(v_stage[:], 1.0).then_inc(ones_set, 1)
                dve.wait_ge(lora_mm, 1)
                for m in range(3):
                    for c in range(2):
                        dve.scalar_tensor_tensor(out=weff[:, m, c, :], in0=ps_p[:, m, c * D:(c + 1) * D],
                                                 scalar=LORA_SCALE, in1=wT[:, m, c, :], op0=ALU.mult,
                                                 op1=ALU.add).then_inc(weff_done, 1)

                def tile(m, tb):
                    scale = 0.25 if m < 2 else 1.0
                    dve.wait_ge(head_done, tb * 4 + (m + 1))
                    dve.wait_ge(sq_done, tb * 4 + (m + 1 + 4))
                    dve.wait_ge(tail_done, tb * 4 + (m + 1))
                    dve.scalar_tensor_tensor(out=resid[:, m % 2, :], in0=ps_p[:, m, :], scalar=scale,
                                             in1=part[:, m, 0, :], op0=ALU.mult,
                                             op1=ALU.subtract).then_inc(resid_done, 1)
                    dve.wait_ge(resid_done, tb * 4 + (m + 1 + 4))
                    dve.tensor_copy(part[:, m, 1, :], resid[:, m % 2, :]).then_inc(mid_done, 1)
                    dve.wait_ge(norm_mm, tb * 4 + (m + 1 + 2))
                    dve.tensor_reduce(nmax[:, m, bass.ds(tb, 1)], ps_n[0:8, m % 2, :], AX.X, ALU.max).then_inc(norm_max, 1)

                with dve.Fori(0, NB) as tb:
                    for m in range(4):
                        tile(m, tb)
                dve.wait_ge(norm_max, 4 * NB + 2)
                dve.tensor_reduce(nm[:], nmax[:], AX.X, ALU.max).then_inc(bnd_step, 1)
                dve.wait_ge(bnd_step, 1)
                dve.tensor_tensor(bnd[:], nm[:, 0:2], nm[:, 2:4], ALU.mult).then_inc(bnd_step, 1)
                dve.wait_ge(bnd_step, 2)
                dve.tensor_reduce(bnd1[:], bnd[:], AX.X, ALU.max).then_inc(bnd_step, 1)
                dve.wait_ge(bnd_T, 1)
                dve.tensor_reduce(one[:, 0:1], ps_n[0:1, 0, 0:8], AX.X, ALU.max).then_inc(bnd_step, 1)
                dve.wait_ge(bnd_step, 4)
                dve.tensor_scalar(one[:, 1:2], one[:, 0:1], 0.99 * BOUND * BOUND, None, ALU.is_le).then_inc(bnd_step, 1)
                dve.wait_ge(bnd_step, 5)
                dve.tensor_scalar(flag[:], one[:, 1:2], -1.0, 1.0, ALU.mult, ALU.add).then_inc(bnd_step, 1)

            @block.gpsimd
            def _(pool):
                pool.memset(zeros, 0.0).then_inc(zero_set, 1)
                pool.wait_ge(zero_set, 1)
                for rows in (slots_x, slots_y):
                    pool.dma_start(rows[SLOTS:SLOTS + 1, :], zeros[0:1, 0:D]).then_inc(zero_out, 16)
                flat = slots_x[0:SLOTS, :].rearrange("r d -> (r d)").rearrange("(p n) -> p n", p=P)
                with pool.Fori(0, NB) as tb:
                    pool.wait_ge(mid_done, tb * 4 + 1)
                    alone(pool)
                    pool.dma_start(flat[:, bass.ds(tb * ZERO_COLS, ZERO_COLS)], zeros).then_inc(zero_out, 16)
                    for m in range(4):
                        pool.wait_ge(mid_done, tb * 4 + (m + 1))
                        alone(pool)
                        pool.tensor_tensor(part[:, m, 2, :], resid[:, m % 2, :], part[:, m, 1, :],
                                           ALU.subtract).then_inc(tail_done, 1)
                pool.wait_ge(zero_out, 16 * (NB + 2))


def load_keys(eng, io, parts, kop, slot_ap, g, loaded):
    for s, (_, pk) in enumerate(PAIRS):
        src = parts["k"][pk].rearrange("(g h d) t -> g d h t", h=G, d=DH)
        eng.dma_start(slot_ap(16 * s, 16 * s + 16), src[g]).then_inc(loaded, 16)
    src = io["key_const"].rearrange("(g h) a t -> g a h t", h=G)
    eng.dma_start(slot_ap(ROW_BIAS, KROWS), src[g]).then_inc(loaded, 16)


def load_queries(eng, parts, shift, qop, slot, g, tok, loaded):
    for s, (pq, _) in enumerate(PAIRS):
        src = parts["q"][pq].rearrange("(g h d) t -> g d h t", h=G, d=DH)
        eng.dma_start(qop[16 * s:16 * s + 16, slot], src[g, :, :, tok]).then_inc(loaded, 16)
    src = shift.rearrange("(g h) a t -> g a h t", h=G)
    eng.dma_start(qop[ROW_SHIFT:KROWS, slot], src[g, :, :, tok]).then_inc(loaded, 16)


LOADS = len(PAIRS) + 1



def exact_maxima(nc, io, sb, psum, sem, parts, shift, flag, kop, qop, ident_b):
    WIDE = T + QB - P
    OFF = T - P
    with ExitStack() as st:
        wide = sb("wide", [P, WIDE], BF16, st)
        cmax = sb("cmax", [P, KT, G], F32, st)
        rmax = sb("rmax", [P, KT, G], F32, st)
        rest = sb("rest", [P, KT * G], F32, st)
        mparts = sb("mparts", [P, 3, KT * G], BF16, st)
        rows = sb("rows", [3 * KT * G, P], BF16, st)
        ps_m = psum("ps_m", [P, 2, 2, QB], F32, st)
        ps_t = psum("ps_t", [3 * KT * G, P], BF16, st)
        m_wide = sem("m_wide")
        m_kload = sem("m_kload")
        m_qload = sem("m_qload")
        m_mm = sem("m_mm")
        m_red = sem("m_red")
        m_run = sem("m_run")
        m_parts = sem("m_parts")
        m_T = sem("m_T")
        m_rows = sem("m_rows")
        m_out = sem("m_out")
        m_step = sem("m_step")
        UNITS = 2 * KT

        nc.sync.sem_inc(m_red, 2)
        nc.sync.sem_inc(m_parts, 1)
        nc.sync.sem_inc(m_T, 1)
        nc.sync.sem_inc(m_rows, 1)
        nc.sync.sem_inc(m_out, 192)

        def chunks(g, b):
            return g * (NB * (NB + 1) // 2) + (b * (b + 1)) // 2

        with nc.Block() as block:
            @block.sync
            def _(sp):
                with sp.If(sp.value_load(flag[0:1, 0:1], min_val=0, max_val=1)):
                    sp.dma_start(wide[:], io["wide"]).then_inc(m_wide, 16)
                    with sp.Fori(0, NG) as g:
                        sp.wait_ge(m_parts, g * NB + 1)
                        load_keys(sp, io, parts, kop, lambda a, z: kop[a:z, 0], g, m_kload)
                        with sp.Fori(0, NB) as b:
                            sp.wait_ge(m_parts, g * NB + b + 1)
                            load_queries(sp, parts, shift, qop, 0, g, bass.ds(b * QB, QB), m_qload)

            @block.tensor
            def _(pe):
                with pe.If(pe.value_load(flag[0:1, 0:1], min_val=0, max_val=1)):
                    pe.wait_ge(m_wide, 16)
                    with pe.Fori(0, NG) as g:
                        pe.wait_ge(m_kload, g * (16 * LOADS) + 16 * LOADS)
                        alone(pe)
                        with pe.Fori(0, NB) as b:
                            pe.wait_ge(m_qload, (g * NB + b) * (16 * LOADS) + 16 * LOADS)
                            alone(pe)
                            with pe.Fori(0, b + 1) as j:
                                here = nc.s_assert_within(OFF + j * QB - b * QB, P * (KT - 1), OFF, skip_runtime_bounds_check_because="j is at most b")
                                for n in range(UNITS):
                                    qt, half = n // 2, n % 2
                                    pe.wait_ge(m_red, (chunks(g, b) + j) * UNITS + (n + 1))
                                    for i in range(2):
                                        h = 2 * half + i
                                        out = ps_m[:, n % 2, i, :]
                                        pe.matmul(out, qop[0:ROW_SHIFT, 0, h, qt * P:(qt + 1) * P],
                                                  kop[0:ROW_SHIFT, 0, h, bass.ds(j * QB, QB)],
                                                  start=True, stop=False)
                                        mm = pe.matmul(out, ident_b[:],
                                                       wide[:, bass.ds(here - qt * P, QB)],
                                                       start=False, stop=True)
                                    mm.then_inc(m_mm, 1)
                            pe.wait_ge(m_parts, g * NB + b + 2)
                            pe.wait_ge(m_rows, g * NB + b + 1)
                            alone(pe)
                            pe.transpose(ps_t[:], mparts[:].rearrange("p a n -> p (a n)"), ident_b[:]).then_inc(m_T, 1)

            @block.vector
            def _(dve):
                with dve.If(dve.value_load(flag[0:1, 0:1], min_val=0, max_val=1)):
                    with dve.Fori(0, NG) as g:
                        with dve.Fori(0, NB) as b:
                            B = g * NB + b
                            c = Chain(dve, m_step, B * 4, 4)
                            dve.memset(rmax[:], -3e38).then_inc(m_run, 1)
                            with dve.Fori(0, b + 1) as j:
                                n0 = (chunks(g, b) + j) * UNITS
                                dve.wait_ge(m_run, (chunks(g, b) + j) + B + 1)
                                for n in range(UNITS):
                                    qt, half = n // 2, n % 2
                                    dve.wait_ge(m_mm, n0 + (n + 1))
                                    dve.tensor_reduce(cmax[:, qt, 2 * half:2 * half + 2], ps_m[:, n % 2],
                                                      AX.X, ALU.max).then_inc(m_red, 1)
                                dve.wait_ge(m_red, n0 + UNITS + 2)
                                dve.tensor_tensor(rmax[:], rmax[:], cmax[:], ALU.max).then_inc(m_run, 1)
                            dve.wait_ge(m_run, chunks(g, b) + b + B + 2)
                            dve.wait_ge(m_T, B + 1)
                            neg = rmax[:].rearrange("p a h -> p (a h)")
                            c.did(dve.tensor_scalar(mparts[:, 0, :], neg, -1.0, None, ALU.mult))
                            c.wait()
                            c.did(dve.scalar_tensor_tensor(out=rest[:], in0=neg, scalar=-1.0, in1=mparts[:, 0, :],
                                                           op0=ALU.mult, op1=ALU.subtract))
                            c.wait()
                            c.did(dve.tensor_copy(mparts[:, 1, :], rest[:]))
                            c.wait()
                            c.did(dve.tensor_tensor(mparts[:, 2, :], rest[:], mparts[:, 1, :], ALU.subtract))
                            c.wait()
                            c.end()
                            dve.tensor_copy(rest[:, 0:1], rest[:, 0:1]).then_inc(m_parts, 1)

            @block.scalar
            def _(act):
                with act.If(act.value_load(flag[0:1, 0:1], min_val=0, max_val=1)):
                    with act.Fori(0, NG) as g:
                        with act.Fori(0, NB) as b:
                            B = g * NB + b
                            act.wait_ge(m_T, B + 2)
                            act.wait_ge(m_out, B * 192 + 192)
                            act.activation(rows[:], ps_t[:], ACT.Identity).then_inc(m_rows, 1)
                            act.wait_ge(m_rows, B + 2)
                            dst = shift.rearrange("(g h) a t -> g a h t", h=G)
                            for a in range(3):
                                for qt in range(KT):
                                    r0 = a * KT * G + qt * G
                                    act.dma_start(dst[g, a, :, bass.ds(b * QB + qt * P, P)],
                                                  rows[r0:r0 + G, :]).then_inc(m_out, 16)
                    act.wait_ge(m_out, 192 * (NG * NB + 1))



THREE = ([0, 1, 2, 0, 1, 2, 0, 1],
         [2, 2, 5, 3, 3, 3, 3, 3])
TWO = ([0, 1] * 4, [2] * 8)
E0 = 5

BODIES = NB * (NB + 1) // 2
ROUTE_AT = {}
_free = 0
for _n in range(NB - 1):
    _t = max((_n + 1) * (_n + 2) // 2 + 1, _free)
    ROUTE_AT[_t] = ("project", _n)
    ROUTE_AT[_t + 1] = ("project_last", _n)
    ROUTE_AT[_t + 3] = ("count", _n)
    _free = _t + 4
SCATTER_AT = {t + 2 + k: (n, k) for t, (step, n) in ROUTE_AT.items() if step == "count" for k in range(2)}
assert max(SCATTER_AT) < BODIES


def attend(nc, io, sb, psum, sem, parts, shift, attnT, kop, qop, ident_b, cmask, v_stage, v_sb, r):
    with ExitStack() as st:
        prob = sb("prob", [P, KT, G, QB], F32, st)
        denom = sb("denom", [P, QB], F32, st)
        recip = sb("recip", [P, QB], F32, st)
        outT = sb("outT", [P, 2, QB], F32, st)
        ps_s = psum("ps_s", [P, 3, 2, QB], F32, st)
        ps_o = psum("ps_o", [P, 2, QB], F32, st)
        k_loaded = sem("k_loaded")
        q_loaded = [sem(f"q_loaded{s}") for s in range(2)]
        scores = sem("scores")
        exp_done = sem("exp_done")
        staged = sem("staged")
        pv_done = sem("pv_done")
        spread = sem("spread")
        inverted = sem("inverted")
        normed = sem("normed")
        out_stored = [sem(f"out_stored{s}") for s in range(2)]

        nc.sync.sem_inc(exp_done, E0)
        nc.sync.sem_inc(pv_done, KT)
        nc.sync.sem_inc(normed, 2)
        for s in out_stored:
            nc.sync.sem_inc(s, 64)

        with nc.Block() as block:
            @block.sync
            def _(sp):
                def store(g, b):
                    sp.wait_ge(normed, g * NB + (b + 1 + 2))
                    for h in range(G):
                        sp.dma_start(attnT[bass.ds(g * G * DH + h * DH, DH), b * QB:(b + 1) * QB],
                                     outT[32 * h:32 * h + DH, b % 2, :]).then_inc(out_stored[b % 2], 16)

                def group(g, last):
                    for b in range(NB):
                        sp.wait_ge(scores, tiles_before(g, b) * 2 + KT * (b + 1) * 2)
                        if b == 0 and not last:
                            load_keys(sp, io, parts, kop, lambda a, z: kop[a:z, (g + 1) % 2], g + 1, k_loaded)
                        if b + 2 < NB:
                            load_queries(sp, parts, shift, qop, b % 2, g, bass.ds((b + 2) * QB, QB), q_loaded[b % 2])
                        elif not last:
                            load_queries(sp, parts, shift, qop, b % 2, g + 1, bass.ds((b + 2 - NB) * QB, QB), q_loaded[b % 2])
                        if b >= 1:
                            store(g, b - 1)
                    store(g, NB - 1)

                load_keys(sp, io, parts, kop, lambda a, z: kop[a:z, 0], 0, k_loaded)
                for b in range(2):
                    load_queries(sp, parts, shift, qop, b, 0, bass.ds(b * QB, QB), q_loaded[b])
                r.load_constants(sp)
                with sp.Fori(0, NG - 1) as g:
                    group(g, False)
                for b in range(NB):
                    if b >= 1:
                        store(NG - 1, b - 1)
                        sp.wait_ge(out_stored[(b - 1) % 2], 64 * ((NG - 1) * NB // 2 + (b - 1) // 2 + 2))
                        r.load(sp, b - 1)
                    if b + 2 < NB:
                        sp.wait_ge(scores, tiles_before(NG - 1, b) * 2 + KT * (b + 1) * 2)
                        load_queries(sp, parts, shift, qop, b % 2, NG - 1, bass.ds((b + 2) * QB, QB), q_loaded[b % 2])
                store(NG - 1, NB - 1)
                sp.wait_ge(out_stored[(NB - 1) % 2], 64 * (NG * NB // 2 + 1))
                r.load(sp, NB - 1)
                for s in out_stored:
                    sp.wait_ge(s, 64 * (NG * NB // 2 + 1))

            @block.tensor
            def _(pe):
                def pv(t, r, b, q0, first, last):
                    pe.wait_ge(exp_done, t * 2 + (2 + E0))
                    pe.wait_ge(staged, t + 1)
                    for h in range(G):
                        mm = pe.matmul(ps_o[32 * h:32 * h + 32, b % 2, q0:], v_stage[:, r, h, :], prob[:, r, h, q0:],
                                       start=first, stop=last)
                    mm.then_inc(pv_done, 1)

                def body(g, b, t0, kt0, diag, before, opens, ring=THREE):
                    slot, back = ring
                    for r in range(KT):
                        q0 = r * P if diag else 0
                        for half in range(2):
                            n = 2 * r + half
                            pe.wait_ge(exp_done, t0 * 2 + (n - back[n] + 1 + E0))
                            for i in range(2):
                                h = 2 * half + i
                                out = ps_s[:, slot[n], i, :]
                                mm = pe.matmul(out[:, q0:], kop[:, g % 2, h, bass.ds(kt0 + r * P, P)],
                                               qop[:, b % 2, h, q0:], start=True, stop=not diag)
                                if diag:
                                    mm = pe.matmul(out[:, q0:q0 + P], ident_b[:], cmask[:], start=False, stop=True)
                            mm.then_inc(scores, 1)
                        if r == 0:
                            before()
                        else:
                            pv(t0 + (r - 1), r - 1, b, q0 - P if diag else 0, opens and r == 1, False)

                def opening(g, b):
                    if b >= 1:
                        pv(tiles_before(g, b - 1) + (KT * b - 1), KT - 1, b - 1, (KT - 1) * P, False, True)
                    pe.wait_ge(normed, g * NB + (b + 1))

                with pe.Fori(0, NG - 1) as g:
                    pe.wait_ge(k_loaded, g * (16 * LOADS) + 16 * LOADS)
                    alone(pe)
                    for b in range(NB):
                        pe.wait_ge(q_loaded[b % 2], g * (NB // 2 * 16 * LOADS) + (b // 2 + 1) * 16 * LOADS)
                        T0 = tiles_before(g, b)

                        def first():
                            opening(g, b)

                        def inner(t0):
                            return lambda: pv(t0, KT - 1, b, 0, False, False)

                        if b >= 1:
                            body(g, b, T0, 0, False, first, True)
                        if b >= 2:
                            with pe.Fori(0, b - 1) as j:
                                body(g, b, T0 + KT + j * KT, QB + j * QB, False, inner(T0 + (KT - 1) + j * KT), False)
                        body(g, b, T0 + KT * b, QB * b, True, inner(T0 + (KT * b - 1)) if b else first, b == 0)
                    pv(tiles_before(g, NB - 1) + (KT * NB - 1), KT - 1, NB - 1, (KT - 1) * P, False, True)

                g, t = NG - 1, 0
                pe.wait_ge(k_loaded, NG * 16 * LOADS)
                for b in range(NB):
                    pe.wait_ge(q_loaded[b % 2], (g * NB // 2 + b // 2 + 1) * 16 * LOADS)
                    T0 = tiles_before(g, b)
                    for j in range(b + 1):
                        def before():
                            if j == 0:
                                opening(g, b)
                            else:
                                pv(T0 + KT * j - 1, KT - 1, b, 0, False, False)

                        body(g, b, T0 + KT * j, QB * j, j == b, before, j == 0, TWO)
                        if t == 0:
                            r.pe_setup(pe, ps_s[:, 2, 0])
                        r.pe_step(pe, ROUTE_AT.get(t), ps_s[:, 2])
                        t += 1
                pv(tiles_before(g, NB - 1) + (KT * NB - 1), KT - 1, NB - 1, (KT - 1) * P, False, True)

            @block.scalar
            def _(act):
                def body(t0, diag, ring=THREE):
                    for r in range(KT):
                        q0 = r * P if diag else 0
                        act.wait_ge(pv_done, t0 + (r + 1))
                        for half in range(2):
                            act.wait_ge(scores, t0 * 2 + (2 * r + half + 1))
                            act.activation(prob[:, r, 2 * half:2 * half + 2, q0:],
                                           ps_s[:, ring[0][2 * r + half], :, q0:], ACT.Exp).then_inc(exp_done, 1)

                with act.Fori(0, NG - 1) as g:
                    for b in range(NB):
                        T0 = tiles_before(g, b)
                        if b >= 1:
                            with act.Fori(0, b) as j:
                                body(T0 + j * KT, False)
                        body(T0 + KT * b, True)
                for b in range(NB):
                    T0 = tiles_before(NG - 1, b)
                    if b >= 1:
                        with act.Fori(0, b) as j:
                            body(T0 + j * KT, False, TWO)
                    body(T0 + KT * b, True, TWO)

            @block.gpsimd
            def _(pool):
                def body(g, t0, kt0, scatter=None):
                    for q in range(KT):
                        pool.wait_ge(pv_done, t0 + (q + 1))
                        alone(pool)
                        src = v_sb[:, bass.ds(kt0 + q, 1), bass.ds(g * (G * DH), G * DH)]
                        pool.tensor_copy(v_stage[:, q, :, 0:DH], src.rearrange("p o (h d) -> p (o h) d", h=G)).then_inc(staged, 1)
                        if scatter:
                            n, half = scatter
                            r.scatter(pool, n, half * KT + q)

                with pool.Fori(0, NG - 1) as g:
                    for b in range(NB):
                        with pool.Fori(0, b + 1) as j:
                            body(g, tiles_before(g, b) + j * KT, j * KT)
                g, t = NG - 1, 0
                for b in range(NB):
                    for j in range(b + 1):
                        body(g, tiles_before(g, b) + j * KT, j * KT, SCATTER_AT.get(t))
                        t += 1
                r.pool_end(pool)

            @block.vector
            def _(dve):
                spread_mask = [DH + i % DH for i in range(32)]

                def normalise(g, b):
                    n = g * NB + (b + 1)
                    dve.wait_ge(pv_done, tiles_before(g, b) + (KT * (b + 1) + KT))
                    alone(dve)
                    dve.stream_shuffle(denom[:], ps_o[:, b % 2, :], spread_mask).then_inc(spread, 1)
                    dve.wait_ge(spread, n)
                    dve.reciprocal(recip[:], denom[:]).then_inc(inverted, 1)
                    dve.wait_ge(inverted, n)
                    dve.wait_ge(out_stored[b % 2], g * (64 * NB // 2) + 64 * (b // 2 + 1))
                    dve.tensor_tensor(outT[:, b % 2, :], ps_o[:, b % 2, :], recip[:], ALU.mult).then_inc(normed, 1)

                with dve.Fori(0, NG - 1) as g:
                    for b in range(NB):
                        normalise(g, b)
                r.dve_constants(dve)
                t = 0
                for b in range(NB):
                    for j in range(b + 1):
                        if j == 0 and b >= 1:
                            normalise(NG - 1, b - 1)
                        if t == 0:
                            r.dve_setup(dve, ps_s[:, 2, 0])
                        r.dve_step(dve, ROUTE_AT.get(t), ps_s[:, 2])
                        t += 1
                normalise(NG - 1, NB - 1)



RSQRT_MAGIC = 0x5F3759DF
NEWTON = 3
RSQRT_STEPS = 3 + 3 * NEWTON


def rsqrt(c, var, tmp, out):
    dve = c.eng
    v, sq, half, a, b = tmp
    c.did(dve.tensor_scalar(v, var, EPS, None, ALU.add))
    c.wait()
    c.did(dve.tensor_scalar(a.bitcast(I32), v.bitcast(I32), 1, None, ALU.arith_shift_right))
    c.wait()
    c.did(dve.tensor_scalar(b.bitcast(I32), a.bitcast(I32), -1, RSQRT_MAGIC, ALU.mult, ALU.add))
    c.wait()
    root = b
    for k in range(NEWTON):
        to = out if k == NEWTON - 1 else (a, b)[k % 2]
        c.did(dve.tensor_tensor(sq, root, root, ALU.mult))
        c.wait()
        c.did(dve.scalar_tensor_tensor(out=half, in0=sq, scalar=-0.5, in1=v, op0=ALU.mult, op1=ALU.mult))
        c.wait()
        c.did(dve.scalar_tensor_tensor(out=to, in0=half, scalar=1.5, in1=root, op0=ALU.add, op1=ALU.mult))
        c.wait()
        root = to


class Router:

    STEPS = 4 + 4 + RSQRT_STEPS + 3 + 4 + 4 + 1 + 1 + 2 + 3 + 1 + 1 + 1 + 1 + 1
    CONSTANTS = 6

    def __init__(r, io, sb, sem, attnT, slots_x, x1_all, dest_all, weight_all):
        r.io, r.attnT, r.slots_x, r.x1, r.dest_all, r.weight_all = io, attnT, slots_x, x1_all, dest_all, weight_all
        r.aT = sb("aT", [P, 2, 2, QB], F32)
        r.xT = sb("rxT", [P, 2, 2, QB], F32)
        r.wp = sb("wp", [P, 2, D], F32)
        r.wpn = sb("wpn", [P, 2, D], F32)
        r.wg = sb("wg", [P, 2, E], F32)
        r.wpg = sb("wpg", [P, 2, E], F32)
        r.wsum = sb("wsum", [P, E], F32)
        r.ones_f = sb("ones_f", [P, P], F32)
        r.before = sb("before", [P, P], BF16)
        r.ones = sb("ones", [P, P], BF16)
        r.iota = sb("iota", [P, KT, 2, E], F32)
        r.stats = sb("stats", [P, KT, 6], F32)
        r.mv = sb("mv", [P, KT, 2], F32)
        r.tmp = sb("tmp", [P, 5, KT], F32)
        r.rstd = sb("rstd", [P, KT], F32)
        r.slogit = sb("slogit", [P, KT, E], F32)
        r.shiftl = sb("shiftl", [P, KT, E], F32)
        r.clogit = sb("clogit", [P, KT, E], F32)
        r.logit = sb("logit", [P, KT, E], F32)
        r.top = sb("top", [P, KT, 8], F32)
        r.topi = sb("topi", [P, KT, 8], U32)
        r.chosen = sb("chosen", [P, KT, 2], F32)
        r.hot = sb("hot", [P, KT, 2, E], F32)
        r.counts = sb("counts", [P, KT, E], BF16)
        r.ahead = sb("ahead", [P, KT, E], BF16)
        r.run = sb("run", [P, E], BF16)
        r.place = sb("place", [P, KT, 2, E], F32)
        r.pos = sb("pos", [P, KT * 2], F32)
        r.row = sb("row", [P, KT * 2], F32)
        r.row2 = sb("row2", [P, KT * 2], F32)
        r.gap_all = sb("gap_all", [P, NB, KT], F32)
        r.gexp = sb("gexp", [P, NB, KT], F32)
        r.gsum = sb("gsum", [P, NB, KT], F32)
        r.gate = sb("gate", [P, NB, KT, 2], F32)
        r.keep_all = sb("keep_all", [P, NB, KT * 2], F32)

        r.const = sem("r_const")
        r.loaded = [sem(f"r_loaded{u}") for u in range(2)]
        r.ones_done = sem("ones_done")
        r.setup_mm = sem("setup_mm")
        r.setup_done = sem("setup_done")
        r.y_mm = sem("y_mm")
        r.summed = sem("summed")
        r.logits_out = sem("logits_out")
        r.step = sem("r_step")
        r.x1_done = sem("x1_done")
        r.count_done = sem("count_done")
        r.c_mm = sem("c_mm")
        r.placed = sem("placed")
        r.dest_done = sem("dest_done")
        r.scattered = sem("scattered")
        r.gexp_done = sem("gexp_done")
        r.g_step = sem("g_step")
        r.weights = sem("weights")


    def load_constants(r, sp):
        io = r.io
        for dst, src in ((r.wp[:], io["WpT"].rearrange("(c p) o -> p c o", p=P)),
                         (r.wpn[:], io["Wp"].rearrange("(c p) i -> p c i", p=P)),
                         (r.wg[:], io["Wg"].rearrange("(c p) e -> p c e", p=P)),
                         (r.before[:], io["before"]), (r.ones[:], io["ones"]), (r.iota[:], io["iota"])):
            sp.dma_start(dst, src).then_inc(r.const, 16)

    def load(r, sp, n):
        u = n % 2
        cols = slice(n * QB, (n + 1) * QB)
        if n >= 2:
            sp.wait_ge(r.y_mm, (n - 1) * KT)
        sp.dma_start(r.aT[:, u], r.attnT.rearrange("(c p) t -> p c t", p=P)[:, :, cols]).then_inc(r.loaded[u], 16)
        sp.dma_start(r.xT[:, u], r.io["xT"].rearrange("(c p) t -> p c t", p=P)[:, :, cols]).then_inc(r.loaded[u], 16)
        x = r.io["x"].rearrange("(n t p) d -> n p t d", t=KT, p=P)
        sp.dma_start(r.x1[:, n], x[n]).then_inc(r.loaded[u], 16)


    def pe_setup(r, pe, bank):
        pe.wait_ge(r.const, 16 * r.CONSTANTS)
        pe.wait_ge(r.ones_done, 1)
        for i in range(2):
            for c in range(2):
                pe.matmul(bank[:, i * E:(i + 1) * E], r.wpn[:, c, i * P:(i + 1) * P], r.wg[:, c, :],
                          start=(c == 0), stop=(c == 1))
        for c in range(2):
            mm = pe.matmul(bank[:, 2 * E:3 * E], r.ones_f[:], r.wg[:, c, :], start=(c == 0), stop=(c == 1))
        mm.then_inc(r.setup_mm, 1)

    def pe_step(r, pe, step, banks):
        if step is None:
            return
        what, n = step
        u = n % 2

        def tile(s, out):
            for c in range(2):
                mm = pe.matmul(out, r.aT[:, u, c, s * P:(s + 1) * P], r.wp[:, c, :], start=(c == 0), stop=(c == 1))
            mm.then_inc(r.y_mm, 1)

        if what == "project":
            pe.wait_ge(r.loaded[u], 48 * (n // 2 + 1))
            if n == 0:
                pe.wait_ge(r.setup_done, 2)
            else:
                pe.wait_ge(r.placed, n)
            for s in range(2):
                tile(s, banks[:, 0, s * D:(s + 1) * D])
            for s in range(KT):
                out = banks[:, 1, D + s * E:D + (s + 1) * E]
                for c in range(2):
                    pe.matmul(out, r.xT[:, u, c, s * P:(s + 1) * P], r.wg[:, c, :], start=(c == 0), stop=False)
                for c in range(2):
                    pe.matmul(out, r.aT[:, u, c, s * P:(s + 1) * P], r.wpg[:, c, :], start=False, stop=(c == 1))
            tile(2, banks[:, 1, 0:D])
        elif what == "project_last":
            pe.wait_ge(r.summed, n * KT + 2)
            tile(3, banks[:, 0, 0:D])
        else:
            pe.wait_ge(r.count_done, n + 1)
            out = banks[:, 0, 0:KT * E]
            pe.matmul(out, r.before[:], r.counts[:].rearrange("p s e -> p (s e)"), start=True, stop=False)
            pe.matmul(out, r.ones[:], r.ahead[:].rearrange("p s e -> p (s e)"), start=False, stop=True).then_inc(r.c_mm, 1)


    def dve_constants(r, dve):
        dve.memset(r.ones_f[:], 1.0).then_inc(r.ones_done, 1)
        dve.memset(r.run[:], 0.0).then_inc(r.ones_done, 1)

    def dve_setup(r, dve, bank):
        dve.wait_ge(r.setup_mm, 1)
        dve.tensor_copy(r.wpg[:].rearrange("p c e -> p (c e)"), bank[:, 0:2 * E]).then_inc(r.setup_done, 1)
        dve.tensor_copy(r.wsum[:], bank[:, 2 * E:3 * E]).then_inc(r.setup_done, 1)

    def dve_step(r, dve, step, banks):
        if step is None:
            return
        what, n = step
        if what == "project":
            for s in range(3):
                dve.wait_ge(r.y_mm, n * KT + max(s + 1, 2))
                dve.tensor_tensor(r.x1[:, n, s], banks[:, s // 2, s % 2 * D:(s % 2 + 1) * D], r.x1[:, n, s],
                                  ALU.add).then_inc(r.summed, 1)
            dve.tensor_copy(r.slogit[:].rearrange("p s e -> p (s e)"), banks[:, 1, D:D + KT * E]).then_inc(r.logits_out, 1)
        elif what == "project_last":
            dve.wait_ge(r.y_mm, n * KT + 4)
            dve.tensor_tensor(r.x1[:, n, 3], banks[:, 0, 0:D], r.x1[:, n, 3], ALU.add).then_inc(r.summed, 1)
            r.choose(dve, n)
        else:
            r.places(dve, n, banks)

    def choose(r, dve, n):
        c = Chain(dve, r.step, n * r.STEPS, r.STEPS)
        r.chain = c
        layernorm_stats(c, lambda s: dve.wait_ge(r.summed, n * KT + (s + 1)), lambda s: r.x1[:, n, s], r.stats, r.mv)
        rsqrt(c, r.mv[:, :, 1], [r.tmp[:, k] for k in range(5)], r.rstd[:])
        for s in range(KT):
            dve.tensor_scalar(r.x1[:, n, s], r.x1[:, n, s], r.mv[:, s, 0:1], r.rstd[:, s:s + 1],
                              ALU.subtract, ALU.mult).then_inc(r.x1_done, 1)
        mean = r.mv[:, :, 0:1].broadcast_to([P, KT, E])
        c.did(dve.tensor_tensor(r.shiftl[:], mean, r.wsum[:].unsqueeze(1).broadcast_to([P, KT, E]), ALU.mult))
        c.wait()
        dve.wait_ge(r.logits_out, n + 1)
        c.did(dve.tensor_tensor(r.clogit[:], r.slogit[:], r.shiftl[:], ALU.subtract))
        c.wait()
        c.did(dve.tensor_tensor(r.logit[:], r.clogit[:], r.rstd[:].unsqueeze(2).broadcast_to([P, KT, E]), ALU.mult))
        c.wait()
        for s in range(KT):
            c.did(dve.max(r.top[:, s], r.logit[:, s]))
        c.wait()
        for s in range(KT):
            c.did(dve.max_index(r.topi[:, s], r.top[:, s], r.logit[:, s]))
        c.wait()
        c.did(dve.tensor_copy(r.chosen[:], r.topi[:, :, 0:2]))
        c.wait()
        c.did(dve.tensor_tensor(r.hot[:], r.iota[:], r.chosen[:].unsqueeze(3).broadcast_to([P, KT, 2, E]), ALU.is_equal))
        c.wait()
        c.did(dve.tensor_tensor(r.counts[:], r.hot[:, :, 0], r.hot[:, :, 1], ALU.add))
        if n == 0:
            dve.wait_ge(r.ones_done, 2)
        c.did(dve.tensor_copy(r.ahead[:, 0], r.run[:]))
        c.wait()
        for s in range(1, KT):
            c.did(dve.tensor_tensor(r.ahead[:, s], r.ahead[:, s - 1], r.counts[:, s - 1], ALU.add))
            c.wait()
        dve.tensor_tensor(r.run[:], r.ahead[:, KT - 1], r.counts[:, KT - 1], ALU.add).then_inc(r.count_done, 1)
        c.did(dve.tensor_tensor(r.gap_all[:, n], r.top[:, :, 1], r.top[:, :, 0], ALU.subtract))

    def places(r, dve, n, banks):
        c = r.chain
        dve.wait_ge(r.c_mm, n + 1)
        ahead = banks[:, 0, 0:KT * E].rearrange("p (s e) -> p s e", s=KT)
        dve.tensor_tensor(r.place[:], r.hot[:], ahead.unsqueeze(2).broadcast_to([P, KT, 2, E]), ALU.mult).then_inc(r.placed, 1)
        dve.wait_ge(r.placed, n + 1)
        c.did(dve.tensor_reduce(r.pos[:], r.place[:].rearrange("p s k e -> p (s k) e"), AX.X, ALU.add))
        c.wait()
        c.did(dve.tensor_scalar(r.keep_all[:, n], r.pos[:], float(CAP), None, ALU.is_lt))
        c.did(dve.scalar_tensor_tensor(out=r.row[:], in0=r.chosen[:].rearrange("p s k -> p (s k)"),
                                       scalar=float(CAP), in1=r.pos[:], op0=ALU.mult, op1=ALU.add))
        c.wait()
        c.did(dve.scalar_tensor_tensor(out=r.row2[:], in0=r.row[:], scalar=-float(DROPPED), in1=r.keep_all[:, n],
                                       op0=ALU.add, op1=ALU.mult))
        c.wait()
        dve.tensor_scalar(r.dest_all[:, n], r.row2[:], float(DROPPED), None, ALU.add).then_inc(r.dest_done, 1)
        c.end()

    def scatter(r, pool, n, m):
        if m == 0:
            pool.wait_ge(r.dest_done, n + 1)
            pool.wait_ge(r.x1_done, (n + 1) * KT)
            alone(pool)
        pool.indirect_dma_start(
            out=r.slots_x, out_offset=bass.IndirectOffsetOnAxis(ap=r.dest_all[:, n, m:m + 1], axis=0),
            in_=r.x1[:, n, m // 2], in_offset=None, bounds_check=SLOTS - 1,
            oob_is_err=False).then_inc(r.scattered, 16)

    def pool_end(r, pool):
        pool.wait_ge(r.scattered, (NB - 1) * KT * 2 * 16)

    def act_gates(r, act):
        act.wait_ge(r.step, NB * r.STEPS)
        act.activation(r.gexp[:], r.gap_all[:], ACT.Exp).then_inc(r.gexp_done, 1)

    def dve_gates(r, dve):
        c = Chain(dve, r.g_step, 0, 3)
        dve.wait_ge(r.gexp_done, 1)
        c.did(dve.tensor_scalar(r.gsum[:], r.gexp[:], 1.0, None, ALU.add))
        c.wait()
        c.did(dve.reciprocal(r.gate[:, :, :, 0], r.gsum[:]))
        c.wait()
        c.did(dve.tensor_tensor(r.gate[:, :, :, 1], r.gexp[:], r.gate[:, :, :, 0], ALU.mult))
        c.wait()
        c.end()
        dve.tensor_tensor(r.weight_all[:], r.gate[:].rearrange("p n s k -> p n (s k)"), r.keep_all[:],
                          ALU.mult).then_inc(r.weights, 1)


def route_last(nc, io, psum, r, x):
    n = NB - 1
    with ExitStack() as st:
        banks = psum("ps_r", [P, 2, QB], F32, st)
        with nc.Block() as block:
            @block.sync
            def _(sp):
                x.load_weights(sp, io, 0, 0)
                x.load_constants(sp, io)
                x.load_weights(sp, io, 1, 1)

            @block.tensor
            def _(pe):
                for what in ("project", "project_last", "count"):
                    r.pe_step(pe, (what, n), banks)

            @block.vector
            def _(dve):
                for what in ("project", "project_last", "count"):
                    r.dve_step(dve, (what, n), banks)
                r.dve_gates(dve)

            @block.scalar
            def _(act):
                x.weights_high(act, 0, 0, 0)
                r.act_gates(act)

            @block.gpsimd
            def _(pool):
                x.weights_low(pool, 0, 0)
                for m in range(2 * KT):
                    r.scatter(pool, n, m)
                pool.wait_ge(r.scattered, NB * KT * 2 * 16)


def layernorm_stats(c, ready, src, stats, mv):
    dve = c.eng
    for s in range(KT):
        ready(s)
        c.did(dve.bn_stats(stats[:, s], src(s)))
    c.wait()
    alone(dve)
    for s in range(KT):
        c.did(dve.bn_aggr(mv[:, s], stats[:, s]))
    c.wait()



SB = [(0, 3), (3, 6), (6, ST)]


class Experts:

    def __init__(x, sb, sem):
        x.sb, x.sem = sb, sem
        x.w1 = sb("w1", [P, 2, 2, HID], F32)
        x.w2 = sb("w2", [P, 2, HC, D], F32)
        x.w1s = sb("w1s", [P, 2, 2, 2, HID], BF16)
        x.w2s = sb("w2s", [P, 2, 2, HC, D], BF16)
        x.b1 = sb("b1", [P, E, HC], F32)
        x.b2 = sb("b2", [P, E, D], F32)
        x.ident = sb("ident5", [P, P], F32)
        x.const = sem("e_const")
        x.w_loaded = [sem(f"we_loaded{u}") for u in range(2)]
        x.ye_mm = sem("ye_mm")
        x.wh = sem("w_high")
        x.ws = sem("w_split")

    def load_constants(x, sp, io):
        sp.dma_start(x.ident[:], io["ident"]).then_inc(x.const, 16)
        sp.dma_start(x.b1[:], io["b1T"]).then_inc(x.const, 16)
        for e in range(E):
            sp.dma_start(x.b2[:, e], io["b2"][e:e + 1].broadcast_to([P, D])).then_inc(x.const, 16)

    def load_weights(x, sp, io, u, e):
        sp.dma_start(x.w1[:, u], io["W1"][e].rearrange("(c p) h -> p c h", p=P)).then_inc(x.w_loaded[u], 16)
        sp.dma_start(x.w2[:, u], io["W2"][e].rearrange("(c p) d -> p c d", p=P)).then_inc(x.w_loaded[u], 16)

    def weights_high(x, act, e, i, u):
        act.wait_ge(x.w_loaded[u], i * 32 + 32)
        if not (isinstance(e, int) and e < 2):
            act.wait_ge(x.ye_mm, (e - 1) * ST)
        for src, dst in ((x.w1, x.w1s), (x.w2, x.w2s)):
            act.activation(dst[:, u, 0], src[:, u], ACT.Identity).then_inc(x.wh, 1)

    def weights_low(x, pool, e, u):
        for k, (src, dst) in enumerate(((x.w1, x.w1s), (x.w2, x.w2s))):
            pool.wait_ge(x.wh, e * 2 + (k + 1))
            alone(pool)
            pool.tensor_tensor(dst[:, u, 1], src[:, u], dst[:, u, 0], ALU.subtract).then_inc(x.ws, 1)


def experts(nc, io, psum, slots_x, slots_y, X, st):
    sb, sem = X.sb, X.sem
    w1s, w2s, b1, b2, ident, ws, ye_mm = X.w1s, X.w2s, X.b1, X.b2, X.ident, X.ws, X.ye_mm
    if True:
        warm = sb("warm5", [1, 1], F32)
        xe = sb("xe", [P, 2, ST, D], F32)
        xs = sb("xs", [P, 2, 2, 2, ST * P], BF16)
        hid = sb("hid", [P, 4, 3 * P], F32)
        hs = sb("hs", [P, 2, 2, HC, 3 * P], BF16)
        y = sb("y", [P, 3, D], F32)
        ps_h = psum("ps_h", [P, 4, QB], F32, st)
        ps_y = psum("ps_y5", [P, 2, QB], F32, st)
        ps_x = psum("ps_x", [P, 2, QB], F32, st)

        x_loaded = [sem(f"xe_loaded{u}") for u in range(2)]
        x_mm = sem("x_mm")
        x_high = sem("x_high")
        x_low = sem("x_low")
        h_mm = sem("h_mm")
        gelu = sem("gelu")
        h_high = sem("h_high")
        h_low = sem("h_low")
        y_out = sem("y_out")
        y_stored = [sem(f"y_stored{k}") for k in range(3)]

        nc.sync.sem_inc(x_low, 2)
        nc.sync.sem_inc(h_low, 4)
        nc.sync.sem_inc(ye_mm, 2 * ST)
        nc.sync.sem_inc(h_mm, 2 * 24)
        nc.sync.sem_inc(y_out, 2)
        nc.sync.sem_inc(gelu, 4)
        for k in range(3):
            nc.sync.sem_inc(y_stored[k], 16)

        def width(sbk):
            a, z = SB[sbk]
            return min(z * P, CAP) - a * P

        def rows_of(k):
            return LAST if k == ST - 1 else P

        def over_experts(eng, one):
            with eng.Fori(0, E // 2 - 1) as i:
                for u in range(2):
                    one(2 * i + u, i, u, True)
            for u in range(2):
                one(E - 2 + u, E // 2 - 1, u, u == 0)

        xs_d = slots_x[0:SLOTS].rearrange("(e r) d -> e r d", e=E)
        ys_d = slots_y[0:SLOTS].rearrange("(e r) d -> e r d", e=E)
        with nc.Block() as block:
            @block.sync
            def _(sp):
                def load(u, e):
                    sp.dma_start(xe[:, u, 0:ST - 1], xs_d[e, 0:(ST - 1) * P].rearrange("(k p) d -> p k d", p=P)).then_inc(x_loaded[u], 16)
                    sp.dma_start(xe[0:LAST, u, ST - 1], xs_d[e, (ST - 1) * P:CAP]).then_inc(x_loaded[u], 16)

                def store(e):
                    for k in range(ST):
                        n = rows_of(k)
                        sp.wait_ge(y_out, e * ST + (k + 1 + 2))
                        sp.dma_start(ys_d[e, k * P:k * P + n], y[0:n, k % 3]).then_inc(y_stored[k % 3], 16)

                load(0, 0)
                load(1, 1)
                with sp.Fori(0, E // 2 - 1) as i:
                    for u in range(2):
                        e = 2 * i + u
                        sp.wait_ge(ws, e * 2 + 2)
                        sp.wait_ge(x_mm, e * ST + ST)
                        X.load_weights(sp, io, u, e + 2)
                        load(u, e + 2)
                        store(e)
                for e in range(E - 2, E):
                    store(e)
                for k in range(3):
                    sp.wait_ge(y_stored[k], 16 * (E * ST // 3 + 1))

            @block.gpsimd
            def _(pool):
                X.weights_low(pool, 1, 1)
                with pool.Fori(1, E // 2) as i:
                    for u in range(2):
                        X.weights_low(pool, 2 * i + u, u)

            @block.tensor
            def _(pe):
                pe.wait_ge(X.const, 16 * (E + 2))

                def transpose(e, i, u, k):
                    if k == 0:
                        pe.wait_ge(x_loaded[u], i * 32 + 32)
                    pe.wait_ge(x_low, e * ST + (k + 1))
                    alone(pe)
                    n = rows_of(k)
                    for c in range(2):
                        mm = pe.transpose(ps_x[:, (ST * u + k) % 2, c * P:c * P + n], xe[0:n, u, k, c * P:(c + 1) * P],
                                          ident[0:n, 0:n])
                    mm.then_inc(x_mm, 1)

                def up(e, u, sbk, m):
                    w = width(sbk)
                    q = sbk * HC + m
                    pe.wait_ge(gelu, e * 24 + (q + 1))
                    a = SB[sbk][0] * P
                    terms = [(0, 0), (0, 1), (1, 0)]
                    for t, (i1, i2) in enumerate(terms):
                        for c in range(2):
                            mm = pe.matmul(ps_h[:, q % 4, 0:w], w1s[:, u, i1, c, m * P:(m + 1) * P], xs[:, u, i2, c, a:a + w],
                                           start=(t == 0 and c == 0), stop=(t == 2 and c == 1))
                    mm.then_inc(h_mm, 1)

                def down(e, i, u, sbk, ahead):
                    for k in range(*SB[sbk]):
                        if ahead:
                            transpose(e + 1, i + u, 1 - u, k)
                        n = rows_of(k)
                        o = (k - SB[sbk][0]) * P
                        pe.wait_ge(y_out, e * ST + (k + 1))
                        pe.wait_ge(h_low, e * 24 + (sbk + 1) * HC + 4)
                        for t, (i1, i2) in enumerate([(0, 0), (0, 1), (1, 0)]):
                            for m in range(HC):
                                mm = pe.matmul(ps_y[0:n, (ST * u + k) % 2, 0:D], hs[:, (3 * u + sbk) % 2, i1, m, o:o + n],
                                               w2s[:, u, i2, m, :], start=(t == 0 and m == 0), stop=(t == 2 and m == HC - 1))
                        mm.then_inc(ye_mm, 1)

                def one(e, i, u, ahead):
                    pe.wait_ge(ws, e * 2 + 2)
                    pe.wait_ge(x_low, e * ST + ST + 2)
                    for m in range(HC):
                        up(e, u, 0, m)
                    for m in range(HC):
                        up(e, u, 1, m)
                    down(e, i, u, 0, ahead)
                    for m in range(HC):
                        up(e, u, 2, m)
                    down(e, i, u, 1, ahead)
                    down(e, i, u, 2, ahead)

                for k in range(ST):
                    transpose(0, 0, 0, k)
                over_experts(pe, one)

            @block.scalar
            def _(act):
                act.wait_ge(X.const, 16 * (E + 2))
                act.activation(warm[:], b1[0:1, 0, 0:1], ACT.Gelu_apprx_tanh)

                def tokens_high(e, u, k):
                    act.wait_ge(x_mm, e * ST + (k + 1))
                    act.wait_ge(h_mm, e * 24 + 24)
                    n = rows_of(k)
                    src = ps_x[:, (ST * u + k) % 2, 0:2 * P].rearrange("p (c n) -> p c n", c=2)
                    act.activation(xs[:, u, 0, :, k * P:k * P + n], src[:, :, 0:n], ACT.Identity).then_inc(x_high, 1)

                def one(e, i, u, ahead):
                    def hidden(q):
                        w = width(q // HC)
                        act.wait_ge(h_mm, e * 24 + (q + 1 + 48))
                        act.wait_ge(h_low, e * 24 + (q + 1))
                        alone(act)
                        act.activation(hid[:, q % 4, 0:w], ps_h[:, q % 4, 0:w], ACT.Gelu_apprx_tanh,
                                       bias=b1[:, e, q % HC:q % HC + 1]).then_inc(gelu, 1)

                    for q in range(2 * HC):
                        hidden(q)
                        if q == HC - 1 and ahead:
                            X.weights_high(act, e + 1, i + u, 1 - u)
                    if ahead:
                        for k in range(*SB[0]):
                            tokens_high(e + 1, 1 - u, k)
                    for q in range(2 * HC, 3 * HC):
                        hidden(q)
                    if ahead:
                        for k in range(SB[1][0], ST):
                            tokens_high(e + 1, 1 - u, k)

                for k in range(ST):
                    tokens_high(0, 0, k)
                over_experts(act, one)

            @block.vector
            def _(dve):
                def tokens_low(e, u, k):
                    n = rows_of(k)
                    dve.wait_ge(x_high, e * ST + (k + 1))
                    src = ps_x[:, (ST * u + k) % 2, 0:2 * P].rearrange("p (c n) -> p c n", c=2)
                    dve.tensor_tensor(xs[:, u, 1, :, k * P:k * P + n], src[:, :, 0:n],
                                      xs[:, u, 0, :, k * P:k * P + n], ALU.subtract).then_inc(x_low, 1)

                def out(e, u, k):
                    n = rows_of(k)
                    dve.wait_ge(ye_mm, e * ST + (k + 1 + 2 * ST))
                    dve.wait_ge(y_stored[k % 3], e * (16 * ST // 3) + (k // 3) * 16 + 16)
                    bias = b2[0:n, bass.ds(e, 1)].rearrange("p o d -> p (o d)")
                    dve.tensor_tensor(y[0:n, k % 3], ps_y[0:n, (ST * u + k) % 2, 0:D], bias, ALU.add).then_inc(y_out, 1)

                def split(e, u, q):
                    w = width(q // HC)
                    sl = (3 * u + q // HC) % 2
                    dve.wait_ge(gelu, e * 24 + (q + 1 + 4))
                    if q % HC == 0:
                        dve.wait_ge(ye_mm, e * ST + (ends(q // HC - 2)) + 2 * ST)
                    dve.tensor_copy(hs[:, sl, 0, q % HC, 0:w], hid[:, q % 4, 0:w]).then_inc(h_high, 1)
                    dve.wait_ge(h_high, e * 24 + (q + 1))
                    dve.tensor_tensor(hs[:, sl, 1, q % HC, 0:w], hid[:, q % 4, 0:w], hs[:, sl, 0, q % HC, 0:w],
                                      ALU.subtract).then_inc(h_low, 1)

                def ends(sbk):
                    return SB[sbk][1] if sbk >= 0 else SB[sbk % 3][1] - ST

                def one(e, i, u, ahead):
                    for q in range(2 * HC):
                        split(e, u, q)
                    for k in range(ST):
                        if ahead:
                            tokens_low(e + 1, 1 - u, k)
                        if k >= 1:
                            out(e, u, k - 1)
                        if k == SB[0][1] - 1:
                            for q in range(2 * HC, 3 * HC):
                                split(e, u, q)
                    out(e, u, ST - 1)

                for k in range(ST):
                    tokens_low(0, 0, k)
                over_experts(dve, one)



def combine(nc, io, sb, psum, sem, x1_all, slots_y, dest_all, weight_all):
    with ExitStack() as st:
        yg = sb("yg", [P, 2, KT * 2, D], F32, st)
        z = sb("z", [P, 2, KT, D], F32, st)
        half = sb("half", [P, KT, D], F32, st)
        dest = sb("destc", [P, 2, KT * 2], U32, st)
        weight = sb("weightc", [P, 2, KT * 2], F32, st)
        stats = sb("statsc", [P, KT, 6], F32, st)
        mv = sb("mvc", [P, KT, 2], F32, st)
        tmp = sb("tmpc", [P, 5, KT], F32, st)
        rstd = sb("rstdc", [P, KT], F32, st)
        gathered = [sem(f"gathered{u}") for u in range(2)]
        dest_set = sem("dest_set")
        weight_set = sem("weight_set")
        z_done = sem("z_done")
        c_step = sem("c_step")
        applied = sem("applied")
        out_done = [sem(f"out_done{u}") for u in range(2)]
        STEPS = 4 + 4 + 4 + RSQRT_STEPS
        nc.sync.sem_inc(z_done, 2 * KT)
        for u in range(2):
            nc.sync.sem_inc(out_done[u], 16)

        out_v = io["out"].rearrange("o (n t p) d -> (o n) p t d", t=KT, p=P)
        with nc.Block() as block:
            @block.sync
            def _(sp):
                def store(u, n):
                    sp.wait_ge(applied, n * KT + KT)
                    sp.dma_start(out_v[n], z[:, u]).then_inc(out_done[u], 16)

                with sp.Fori(0, NB // 2) as i:
                    for u in range(2):
                        store(u, 2 * i + u)
                for u in range(2):
                    sp.wait_ge(out_done[u], 16 * (NB // 2 + 1))

            @block.gpsimd
            def _(pool):
                with pool.Fori(0, NB // 2) as i:
                    for u in range(2):
                        n = 2 * i + u
                        pool.wait_ge(z_done, n * KT + KT)
                        alone(pool)
                        pool.tensor_copy(dest[:, u], dest_all[:, bass.ds(n, 1)].rearrange("p o k -> p (o k)")).then_inc(dest_set, 1)
                        pool.wait_ge(dest_set, n + 1)
                        alone(pool)
                        for m in range(2 * KT):
                            pool.indirect_dma_start(
                                out=yg[:, u, m], out_offset=None, in_=slots_y,
                                in_offset=bass.IndirectOffsetOnAxis(ap=dest[:, u, m:m + 1], axis=0)).then_inc(gathered[u], 16)

            @block.vector
            def _(dve):
                with dve.Fori(0, NB // 2) as i:
                    for u in range(2):
                        n = 2 * i + u
                        c = Chain(dve, c_step, n * STEPS, STEPS)
                        dve.tensor_copy(weight[:, u], weight_all[:, bass.ds(n, 1)].rearrange("p o k -> p (o k)")).then_inc(weight_set, 1)
                        dve.wait_ge(weight_set, n + 1)
                        dve.wait_ge(gathered[u], i * (32 * KT) + 32 * KT)
                        dve.wait_ge(out_done[u], i * 16 + 16)
                        for s in range(KT):
                            c.did(dve.scalar_tensor_tensor(out=half[:, s], in0=yg[:, u, 2 * s], scalar=weight[:, u, 2 * s:2 * s + 1],
                                                           in1=x1_all[:, bass.ds(n, 1), s].rearrange("p o d -> p (o d)"), op0=ALU.mult, op1=ALU.add))
                        c.wait()
                        for s in range(KT):
                            dve.scalar_tensor_tensor(out=z[:, u, s], in0=yg[:, u, 2 * s + 1], scalar=weight[:, u, 2 * s + 1:2 * s + 2],
                                                     in1=half[:, s], op0=ALU.mult, op1=ALU.add).then_inc(z_done, 1)
                        layernorm_stats(c, lambda s: dve.wait_ge(z_done, n * KT + (s + 1 + 2 * KT)),
                                        lambda s: z[:, u, s], stats, mv)
                        rsqrt(c, mv[:, :, 1], [tmp[:, k] for k in range(5)], rstd[:])
                        for s in range(KT):
                            dve.tensor_scalar(z[:, u, s], z[:, u, s], mv[:, s, 0:1], rstd[:, s:s + 1],
                                              ALU.subtract, ALU.mult).then_inc(applied, 1)
                        c.end()



def constants():
    bf = mybir.dt.np(BF16)
    start = 2.0 ** (-2.0 ** (-(math.log2(H) - 3)))
    slopes = np.array([start * start ** i for i in range(H)], np.float32)
    rest = -slopes[:, None] * np.arange(T, dtype=np.float32)[None, :]
    key_const = np.ones((H, 6, T), bf)
    for a in range(3):
        key_const[:, a] = rest.astype(bf)
        rest = rest - key_const[:, a].astype(np.float32)
    p = np.arange(P)
    wide = np.where(np.arange(T + QB - P)[None, :] - (T - P) > p[:, None], MASKED, 0.0)
    return {
        "key_const": key_const,
        "q_const": np.ones((3, G, QB), bf),
        "no_shift": np.zeros((H, 3 * T), bf),
        "cmask": np.where(p[:, None] > p[None, :], MASKED, 0.0).astype(bf),
        "wide": wide.astype(bf),
        "ident_b": np.eye(P, dtype=bf),
        "ident": np.eye(P, dtype=np.float32),
        "headsel": (p[:, None] // DH == np.arange(8)[None, :]).astype(bf),
        "before": (p[:, None] < p[None, :]).astype(bf),
        "ones": np.ones((P, P), bf),
        "iota": np.ascontiguousarray(np.broadcast_to(np.arange(E, dtype=np.float32), (P, KT, 2, E))),
    }


def kernel(**inputs):
    import concourse.bacc as bacc
    from concourse.bass_utils import run_bass_kernel_spmd as run

    a = {k[3:]: np.asarray(v) for k, v in inputs.items()}
    arrays = {
        "x": a["attn_x"][0], "xT": a["attn_x"][0].T, "WpT": a["attn_Wp"].T, "Wp": a["attn_Wp"], "Wg": a["ffn_Wg"],
        "W1": a["ffn_W1"], "W2": a["ffn_W2"], "b2": a["ffn_b2"],
        "b1T": a["ffn_b1"].reshape(E, HC, P).transpose(2, 0, 1),
    }
    for w in "qkv":
        arrays["W" + w] = a["attn_W" + w].T
        arrays["A" + w] = a["attn_A" + w].T
        arrays["B" + w] = a["attn_B" + w]
    arrays.update(constants())
    arrays = {k: np.ascontiguousarray(v) for k, v in arrays.items()}
    nc = bacc.Bacc("TRN2", target_bir_lowering=False, num_devices=1)
    io = {k: nc.dram_tensor("in_" + k, v.shape, mybir.dt.from_np(v.dtype), kind="ExternalInput").ap()
          for k, v in arrays.items()}
    io["out"] = nc.dram_tensor("out_0", (1, T, D), F32, kind="ExternalOutput").ap()
    build(nc, io)
    r = run(nc, [{"in_" + k: v for k, v in arrays.items()}], core_ids=[0])
    return r.results[0]["out_0"]
```

```python
import math
from contextlib import ExitStack

import numpy as np

import concourse.bass as bass
from concourse import mybir

F32 = mybir.dt.float32
BF16 = mybir.dt.bfloat16
I32 = mybir.dt.int32
U32 = mybir.dt.uint32
ACT = mybir.ActivationFunctionType
ALU = mybir.AluOpType
AX = mybir.AxisListType

P = 128
T = 4096
D = 256
H = 16
DH = D // H
G = 4
NG = H // G
QB = 512
NB = T // QB
KT = QB // P
R = 8
LORA_SCALE = 2.0
EPS = 1e-5

PAIRS = [(0, 0), (0, 1), (1, 0), (1, 1), (0, 2), (2, 0)]
NP_ROWS = 16 * len(PAIRS)
ROW_BIAS = NP_ROWS
ROW_SHIFT = NP_ROWS + 3
KROWS = NP_ROWS + 6
BOUND = 60.0
MASKED = -1e30

E = 8
HID = 1024
CAP = int(math.ceil(T * 2 / E * 1.05))
SLOTS = E * CAP
DROPPED = SLOTS
HC = HID // P
ST = -(-CAP // P)
LAST = CAP - (ST - 1) * P
LATE = (H - G) * DH - P
ZERO_COLS = SLOTS * D // P // NB
assert ZERO_COLS * NB * P == SLOTS * D


def alone(eng):
    eng.sem_inc(PASSED["sem"], 1)


PASSED = {}


class Chain:

    def __init__(self, eng, sem, base, steps):
        self.eng, self.sem, self.base, self.steps, self.n = eng, sem, base, steps, 0

    def did(self, ins):
        self.n += 1
        ins.then_inc(self.sem, 1)

    def wait(self):
        self.eng.wait_ge(self.sem, self.base + self.n)

    def end(self):
        assert self.n == self.steps, (self.n, self.steps)


def tiles_before(g, b):
    return g * (2 * NB * (NB + 1)) + 2 * b * (b + 1)


def build(nc, io):
    with ExitStack() as ctx:
        def sb(name, shape, dt, c=ctx):
            return c.enter_context(nc.sbuf_tensor(name, shape, dt))

        def psum(name, shape, dt, c):
            return c.enter_context(nc.psum_tensor(name, shape, dt))

        def sem(name):
            return ctx.enter_context(nc.semaphore(name))

        def dram(name, shape, dt):
            return nc.dram_tensor(name, shape, dt, kind="Internal").ap()

        parts = {m: dram(f"parts_{m}", (3, D, T), BF16) for m in "qk"}
        shift = dram("shift", (H, 3, T), BF16)
        attnT = dram("attnT", (D, T), F32)
        slots_x = dram("slots_x", (SLOTS + 1, D), F32)
        slots_y = dram("slots_y", (SLOTS + 1, D), F32)

        flag = sb("flag", [1, 1], I32)
        x1_all = sb("x1_all", [P, NB, KT, D], F32)
        dest_all = sb("dest_all", [P, NB, KT * 2], U32)
        weight_all = sb("weight_all", [P, NB, KT * 2], F32)
        PASSED["sem"] = sem("passed")
        with ExitStack() as mid:
            r = Router(io, lambda n, sh, dt: sb(n, sh, dt, mid), sem, attnT, slots_x, x1_all, dest_all, weight_all)
            attention(nc, io, sb, psum, sem, parts, shift, attnT, flag, slots_x, slots_y, r)
            with ExitStack() as st:
                x = Experts(lambda n, sh, dt: sb(n, sh, dt, st), sem)
                route_last(nc, io, psum, r, x)
                experts(nc, io, psum, slots_x, slots_y, x, st)
        combine(nc, io, sb, psum, sem, x1_all, slots_y, dest_all, weight_all)


def attention(nc, io, sb, psum, sem, parts, shift, attnT, flag, slots_x, slots_y, r):
    with ExitStack() as big:
        v_sb = sb("v_sb", [P, T // P, D], F32, big)
        kop = sb("kop", [KROWS, 2, G, T], BF16, big)
        qop = sb("qop", [KROWS, 2, G, QB], BF16, big)
        ident_b = sb("ident_b", [P, P], BF16, big)
        cmask = sb("cmask", [P, P], BF16, big)
        v_stage = sb("v_stage", [P, KT, G, 32], F32, big)

        project(nc, io, sb, psum, sem, parts, shift, flag, v_sb, qop, ident_b, cmask, v_stage,
                slots_x, slots_y, r.x1[:].rearrange("p n t d -> p (n t d)"))
        exact_maxima(nc, io, sb, psum, sem, parts, shift, flag, kop, qop, ident_b)
        attend(nc, io, sb, psum, sem, parts, shift, attnT, kop, qop, ident_b, cmask, v_stage, v_sb, r)



def project(nc, io, sb, psum, sem, parts, shift, flag, v_sb, qop, ident_b, cmask, v_stage,
            slots_x, slots_y, spare):
    with ExitStack() as st:
        wT = sb("wT", [P, 3, 2, D], F32, st)
        loA = sb("loA", [R, 3, D], F32, st)
        loB = sb("loB", [R, 3, D], F32, st)
        weff = sb("weff", [P, 3, 2, D], F32, st)
        xT = sb("xT", [P, 2, 2, QB], F32, st)
        part = sb("part", [P, 4, 3, QB], BF16, st)
        resid = sb("resid", [P, 2, QB], F32, st)
        sq = sb("sq", [P, 2, QB], BF16, st)
        hsel = sb("hsel", [P, 8], BF16, st)
        ident8 = sb("ident8", [8, 8], F32, st)
        nmax = sb("nmax", [8, 4, NB], F32, st)
        nm = sb("nm", [8, 4], F32, st)
        bnd = sb("bnd", [8, 2], F32, st)
        bnd1 = sb("bnd1", [8, 1], F32, st)
        one = sb("one", [1, 2], F32, st)
        zeros = spare[:, 0:ZERO_COLS]
        warm = sb("warm", [1, 1], F32, st)
        zero_set = sem("zero_set")
        zero_out = sem("zero_out")
        ps_p = psum("ps_p", [P, 4, QB], F32, st)
        ps_v = psum("ps_v", [P, 2, 2, D], F32, st)
        ps_n = psum("ps_n", [P, 2, QB], F32, st)

        w_loaded = sem("w_loaded")
        small_loaded = sem("small_loaded")
        x_loaded = [sem(f"x_loaded{u}") for u in range(2)]
        lora_mm = sem("lora_mm")
        weff_done = sem("weff_done")
        proj_mm = sem("proj_mm")
        v_mm = sem("v_mm")
        v_out = sem("v_out")
        head_done = sem("head_done")
        sq_done = sem("sq_done")
        resid_done = sem("resid_done")
        mid_done = sem("mid_done")
        tail_done = sem("tail_done")
        norm_mm = sem("norm_mm")
        norm_max = sem("norm_max")
        stored = [sem(f"stored{m}") for m in range(4)]
        shift_out = sem("shift_out")
        bnd_step = sem("bnd_step")
        bnd_T = sem("bnd_T")
        ones_set = sem("ones_set")

        nc.sync.sem_inc(resid_done, 4)
        nc.sync.sem_inc(sq_done, 4)
        nc.sync.sem_inc(norm_mm, 2)
        nc.sync.sem_inc(norm_max, 2)
        nc.sync.sem_inc(tail_done, 2)
        nc.sync.sem_inc(v_out, 2)
        for s in stored:
            nc.sync.sem_inc(s, 16)

        xT_d = io["xT"].rearrange("(c p) t -> p c t", p=P)
        with nc.Block() as block:
            @block.sync
            def _(sp):
                for m, w in enumerate("qkv"):
                    sp.dma_start(loA[:, m, :], io["A" + w]).then_inc(w_loaded, 16)
                    sp.dma_start(loB[:, m, :], io["B" + w]).then_inc(w_loaded, 16)
                    sp.dma_start(wT[:, m], io["W" + w].rearrange("(c p) o -> p c o", p=P)).then_inc(w_loaded, 16)
                for u in range(2):
                    sp.dma_start(xT[:, u], xT_d[:, :, u * QB:(u + 1) * QB]).then_inc(x_loaded[u], 16)
                sp.dma_start(hsel[:], io["headsel"]).then_inc(small_loaded, 16)
                sp.dma_start(ident8[:], io["ident"][0:8, 0:8]).then_inc(small_loaded, 16)
                sp.dma_start(ident_b[:], io["ident_b"]).then_inc(small_loaded, 16)
                sp.dma_start(cmask[:], io["cmask"]).then_inc(small_loaded, 16)
                for s in range(2):
                    sp.dma_start(qop[ROW_BIAS:ROW_SHIFT, s], io["q_const"][0:3]).then_inc(small_loaded, 16)
                sp.dma_start(shift.rearrange("h a t -> h (a t)"), io["no_shift"]).then_inc(shift_out, 16)

                def store(m, tb):
                    sp.wait_ge(tail_done, tb * 4 + (m + 1 + 2))
                    dst = parts["qk"[m // 2]][:, (m % 2) * P:(m % 2 + 1) * P, bass.ds(tb * QB, QB)]
                    sp.dma_start(dst.rearrange("a p t -> p a t"), part[:, m]).then_inc(stored[m], 16)

                with sp.Fori(0, NB // 2 - 1) as i:
                    for u in range(2):
                        tb = 2 * i + u
                        for m in range(4):
                            store(m, tb)
                        sp.wait_ge(v_mm, tb * 2 + 2)
                        sp.dma_start(xT[:, u], xT_d[:, :, bass.ds((tb + 2) * QB, QB)]).then_inc(x_loaded[u], 16)
                for tb in range(NB - 2, NB):
                    for m in range(4):
                        store(m, tb)
                sp.wait_ge(small_loaded, 16 * 6)
                for m in range(4):
                    sp.wait_ge(stored[m], 16 * (NB + 1))
                sp.wait_ge(shift_out, 16)

            @block.tensor
            def _(pe):
                pe.wait_ge(w_loaded, 16 * 9)
                for m in range(3):
                    for c in range(2):
                        mm = pe.matmul(ps_p[:, m, c * D:(c + 1) * D], loB[:, m, c * P:(c + 1) * P], loA[:, m, :],
                                       start=True, stop=True)
                mm.then_inc(lora_mm, 1)
                pe.wait_ge(weff_done, 6)
                pe.wait_ge(small_loaded, 16 * 6)

                def norm(m, tb):
                    pe.wait_ge(sq_done, tb * 4 + (m + 1 + 4))
                    pe.wait_ge(norm_max, tb * 4 + (m + 1))
                    pe.matmul(ps_n[0:8, m % 2, :], hsel[:], sq[:, m % 2, :], start=True, stop=True).then_inc(norm_mm, 1)

                def block_of(tb, u, i):
                    pe.wait_ge(x_loaded[u], i * 16 + 16)
                    for m in range(4):
                        pe.wait_ge(resid_done, tb * 4 + (m + 1))
                        pe.wait_ge(sq_done, tb * 4 + (m + 1))
                        for c in range(2):
                            mm = pe.matmul(ps_p[:, m, :], weff[:, m // 2, c, (m % 2) * P:(m % 2 + 1) * P],
                                           xT[:, u, c, :], start=(c == 0), stop=(c == 1))
                        mm.then_inc(proj_mm, 1)
                        if m >= 1:
                            norm(m - 1, tb)
                    for j in range(2):
                        pe.wait_ge(v_out, tb * 2 + (j + 1))
                        for s in range(2):
                            for c in range(2):
                                mm = pe.matmul(ps_v[:, j, s, :], xT[:, u, c, (2 * j + s) * P:(2 * j + s + 1) * P],
                                               weff[:, 2, c, :], start=(c == 0), stop=(c == 1))
                        mm.then_inc(v_mm, 1)
                        if j == 0:
                            norm(3, tb)

                with pe.Fori(0, NB // 2) as i:
                    for u in range(2):
                        block_of(2 * i + u, u, i)
                pe.wait_ge(bnd_step, 3)
                pe.transpose(ps_n[0:1, 0, 0:8], bnd1[:], ident8[:]).then_inc(bnd_T, 1)

            @block.scalar
            def _(act):
                def tile(m, tb):
                    scale = 0.25 if m < 2 else 1.0
                    act.wait_ge(proj_mm, tb * 4 + (m + 1))
                    act.wait_ge(stored[m], tb * 16 + 16)
                    act.activation(part[:, m, 0, :], ps_p[:, m, :], ACT.Identity, scale=scale).then_inc(head_done, 1)
                    act.wait_ge(norm_mm, tb * 4 + (m + 1))
                    act.activation(sq[:, m % 2, :], ps_p[:, m, :], ACT.Square, scale=scale).then_inc(sq_done, 1)

                act.wait_ge(ones_set, 1)
                act.activation(warm[:], v_stage[0:1, 0, 0, 0:1], ACT.Exp)
                with act.Fori(0, NB) as tb:
                    for m in range(4):
                        tile(m, tb)
                    for j in range(2):
                        act.wait_ge(v_mm, tb * 2 + (j + 1))
                        alone(act)
                        act.activation(v_sb[:, bass.ds(tb * 4 + 2 * j, 2), :], ps_v[:, j], ACT.Identity).then_inc(v_out, 1)

            @block.vector
            def _(dve):
                dve.memset(v_stage[:], 1.0).then_inc(ones_set, 1)
                dve.wait_ge(lora_mm, 1)
                for m in range(3):
                    for c in range(2):
                        dve.scalar_tensor_tensor(out=weff[:, m, c, :], in0=ps_p[:, m, c * D:(c + 1) * D],
                                                 scalar=LORA_SCALE, in1=wT[:, m, c, :], op0=ALU.mult,
                                                 op1=ALU.add).then_inc(weff_done, 1)

                def tile(m, tb):
                    scale = 0.25 if m < 2 else 1.0
                    dve.wait_ge(head_done, tb * 4 + (m + 1))
                    dve.wait_ge(sq_done, tb * 4 + (m + 1 + 4))
                    dve.wait_ge(tail_done, tb * 4 + (m + 1))
                    dve.scalar_tensor_tensor(out=resid[:, m % 2, :], in0=ps_p[:, m, :], scalar=scale,
                                             in1=part[:, m, 0, :], op0=ALU.mult,
                                             op1=ALU.subtract).then_inc(resid_done, 1)
                    dve.wait_ge(resid_done, tb * 4 + (m + 1 + 4))
                    dve.tensor_copy(part[:, m, 1, :], resid[:, m % 2, :]).then_inc(mid_done, 1)
                    dve.wait_ge(norm_mm, tb * 4 + (m + 1 + 2))
                    dve.tensor_reduce(nmax[:, m, bass.ds(tb, 1)], ps_n[0:8, m % 2, :], AX.X, ALU.max).then_inc(norm_max, 1)

                with dve.Fori(0, NB) as tb:
                    for m in range(4):
                        tile(m, tb)
                dve.wait_ge(norm_max, 4 * NB + 2)
                dve.tensor_reduce(nm[:], nmax[:], AX.X, ALU.max).then_inc(bnd_step, 1)
                dve.wait_ge(bnd_step, 1)
                dve.tensor_tensor(bnd[:], nm[:, 0:2], nm[:, 2:4], ALU.mult).then_inc(bnd_step, 1)
                dve.wait_ge(bnd_step, 2)
                dve.tensor_reduce(bnd1[:], bnd[:], AX.X, ALU.max).then_inc(bnd_step, 1)
                dve.wait_ge(bnd_T, 1)
                dve.tensor_reduce(one[:, 0:1], ps_n[0:1, 0, 0:8], AX.X, ALU.max).then_inc(bnd_step, 1)
                dve.wait_ge(bnd_step, 4)
                dve.tensor_scalar(one[:, 1:2], one[:, 0:1], 0.99 * BOUND * BOUND, None, ALU.is_le).then_inc(bnd_step, 1)
                dve.wait_ge(bnd_step, 5)
                dve.tensor_scalar(flag[:], one[:, 1:2], -1.0, 1.0, ALU.mult, ALU.add).then_inc(bnd_step, 1)

            @block.gpsimd
            def _(pool):
                pool.memset(zeros, 0.0).then_inc(zero_set, 1)
                pool.wait_ge(zero_set, 1)
                for rows in (slots_x, slots_y):
                    pool.dma_start(rows[SLOTS:SLOTS + 1, :], zeros[0:1, 0:D]).then_inc(zero_out, 16)
                flat = slots_x[0:SLOTS, :].rearrange("r d -> (r d)").rearrange("(p n) -> p n", p=P)
                with pool.Fori(0, NB) as tb:
                    pool.wait_ge(mid_done, tb * 4 + 1)
                    alone(pool)
                    pool.dma_start(flat[:, bass.ds(tb * ZERO_COLS, ZERO_COLS)], zeros).then_inc(zero_out, 16)
                    for m in range(4):
                        pool.wait_ge(mid_done, tb * 4 + (m + 1))
                        alone(pool)
                        pool.tensor_tensor(part[:, m, 2, :], resid[:, m % 2, :], part[:, m, 1, :],
                                           ALU.subtract).then_inc(tail_done, 1)
                pool.wait_ge(zero_out, 16 * (NB + 2))


def load_keys(eng, io, parts, kop, slot_ap, g, loaded):
    for s, (_, pk) in enumerate(PAIRS):
        src = parts["k"][pk].rearrange("(g h d) t -> g d h t", h=G, d=DH)
        eng.dma_start(slot_ap(16 * s, 16 * s + 16), src[g]).then_inc(loaded, 16)
    src = io["key_const"].rearrange("(g h) a t -> g a h t", h=G)
    eng.dma_start(slot_ap(ROW_BIAS, KROWS), src[g]).then_inc(loaded, 16)


def load_queries(eng, parts, shift, qop, slot, g, tok, loaded):
    for s, (pq, _) in enumerate(PAIRS):
        src = parts["q"][pq].rearrange("(g h d) t -> g d h t", h=G, d=DH)
        eng.dma_start(qop[16 * s:16 * s + 16, slot], src[g, :, :, tok]).then_inc(loaded, 16)
    src = shift.rearrange("(g h) a t -> g a h t", h=G)
    eng.dma_start(qop[ROW_SHIFT:KROWS, slot], src[g, :, :, tok]).then_inc(loaded, 16)


LOADS = len(PAIRS) + 1



def exact_maxima(nc, io, sb, psum, sem, parts, shift, flag, kop, qop, ident_b):
    WIDE = T + QB - P
    OFF = T - P
    with ExitStack() as st:
        wide = sb("wide", [P, WIDE], BF16, st)
        cmax = sb("cmax", [P, KT, G], F32, st)
        rmax = sb("rmax", [P, KT, G], F32, st)
        rest = sb("rest", [P, KT * G], F32, st)
        mparts = sb("mparts", [P, 3, KT * G], BF16, st)
        rows = sb("rows", [3 * KT * G, P], BF16, st)
        ps_m = psum("ps_m", [P, 2, 2, QB], F32, st)
        ps_t = psum("ps_t", [3 * KT * G, P], BF16, st)
        m_wide = sem("m_wide")
        m_kload = sem("m_kload")
        m_qload = sem("m_qload")
        m_mm = sem("m_mm")
        m_red = sem("m_red")
        m_run = sem("m_run")
        m_parts = sem("m_parts")
        m_T = sem("m_T")
        m_rows = sem("m_rows")
        m_out = sem("m_out")
        m_step = sem("m_step")
        UNITS = 2 * KT

        nc.sync.sem_inc(m_red, 2)
        nc.sync.sem_inc(m_parts, 1)
        nc.sync.sem_inc(m_T, 1)
        nc.sync.sem_inc(m_rows, 1)
        nc.sync.sem_inc(m_out, 192)

        def chunks(g, b):
            return g * (NB * (NB + 1) // 2) + (b * (b + 1)) // 2

        with nc.Block() as block:
            @block.sync
            def _(sp):
                with sp.If(sp.value_load(flag[0:1, 0:1], min_val=0, max_val=1)):
                    sp.dma_start(wide[:], io["wide"]).then_inc(m_wide, 16)
                    with sp.Fori(0, NG) as g:
                        sp.wait_ge(m_parts, g * NB + 1)
                        load_keys(sp, io, parts, kop, lambda a, z: kop[a:z, 0], g, m_kload)
                        with sp.Fori(0, NB) as b:
                            sp.wait_ge(m_parts, g * NB + b + 1)
                            load_queries(sp, parts, shift, qop, 0, g, bass.ds(b * QB, QB), m_qload)

            @block.tensor
            def _(pe):
                with pe.If(pe.value_load(flag[0:1, 0:1], min_val=0, max_val=1)):
                    pe.wait_ge(m_wide, 16)
                    with pe.Fori(0, NG) as g:
                        pe.wait_ge(m_kload, g * (16 * LOADS) + 16 * LOADS)
                        alone(pe)
                        with pe.Fori(0, NB) as b:
                            pe.wait_ge(m_qload, (g * NB + b) * (16 * LOADS) + 16 * LOADS)
                            alone(pe)
                            with pe.Fori(0, b + 1) as j:
                                here = nc.s_assert_within(OFF + j * QB - b * QB, P * (KT - 1), OFF, skip_runtime_bounds_check_because="j is at most b")
                                for n in range(UNITS):
                                    qt, half = n // 2, n % 2
                                    pe.wait_ge(m_red, (chunks(g, b) + j) * UNITS + (n + 1))
                                    for i in range(2):
                                        h = 2 * half + i
                                        out = ps_m[:, n % 2, i, :]
                                        pe.matmul(out, qop[0:ROW_SHIFT, 0, h, qt * P:(qt + 1) * P],
                                                  kop[0:ROW_SHIFT, 0, h, bass.ds(j * QB, QB)],
                                                  start=True, stop=False)
                                        mm = pe.matmul(out, ident_b[:],
                                                       wide[:, bass.ds(here - qt * P, QB)],
                                                       start=False, stop=True)
                                    mm.then_inc(m_mm, 1)
                            pe.wait_ge(m_parts, g * NB + b + 2)
                            pe.wait_ge(m_rows, g * NB + b + 1)
                            alone(pe)
                            pe.transpose(ps_t[:], mparts[:].rearrange("p a n -> p (a n)"), ident_b[:]).then_inc(m_T, 1)

            @block.vector
            def _(dve):
                with dve.If(dve.value_load(flag[0:1, 0:1], min_val=0, max_val=1)):
                    with dve.Fori(0, NG) as g:
                        with dve.Fori(0, NB) as b:
                            B = g * NB + b
                            c = Chain(dve, m_step, B * 4, 4)
                            dve.memset(rmax[:], -3e38).then_inc(m_run, 1)
                            with dve.Fori(0, b + 1) as j:
                                n0 = (chunks(g, b) + j) * UNITS
                                dve.wait_ge(m_run, (chunks(g, b) + j) + B + 1)
                                for n in range(UNITS):
                                    qt, half = n // 2, n % 2
                                    dve.wait_ge(m_mm, n0 + (n + 1))
                                    dve.tensor_reduce(cmax[:, qt, 2 * half:2 * half + 2], ps_m[:, n % 2],
                                                      AX.X, ALU.max).then_inc(m_red, 1)
                                dve.wait_ge(m_red, n0 + UNITS + 2)
                                dve.tensor_tensor(rmax[:], rmax[:], cmax[:], ALU.max).then_inc(m_run, 1)
                            dve.wait_ge(m_run, chunks(g, b) + b + B + 2)
                            dve.wait_ge(m_T, B + 1)
                            neg = rmax[:].rearrange("p a h -> p (a h)")
                            c.did(dve.tensor_scalar(mparts[:, 0, :], neg, -1.0, None, ALU.mult))
                            c.wait()
                            c.did(dve.scalar_tensor_tensor(out=rest[:], in0=neg, scalar=-1.0, in1=mparts[:, 0, :],
                                                           op0=ALU.mult, op1=ALU.subtract))
                            c.wait()
                            c.did(dve.tensor_copy(mparts[:, 1, :], rest[:]))
                            c.wait()
                            c.did(dve.tensor_tensor(mparts[:, 2, :], rest[:], mparts[:, 1, :], ALU.subtract))
                            c.wait()
                            c.end()
                            dve.tensor_copy(rest[:, 0:1], rest[:, 0:1]).then_inc(m_parts, 1)

            @block.scalar
            def _(act):
                with act.If(act.value_load(flag[0:1, 0:1], min_val=0, max_val=1)):
                    with act.Fori(0, NG) as g:
                        with act.Fori(0, NB) as b:
                            B = g * NB + b
                            act.wait_ge(m_T, B + 2)
                            act.wait_ge(m_out, B * 192 + 192)
                            act.activation(rows[:], ps_t[:], ACT.Identity).then_inc(m_rows, 1)
                            act.wait_ge(m_rows, B + 2)
                            dst = shift.rearrange("(g h) a t -> g a h t", h=G)
                            for a in range(3):
                                for qt in range(KT):
                                    r0 = a * KT * G + qt * G
                                    act.dma_start(dst[g, a, :, bass.ds(b * QB + qt * P, P)],
                                                  rows[r0:r0 + G, :]).then_inc(m_out, 16)
                    act.wait_ge(m_out, 192 * (NG * NB + 1))



THREE = ([0, 2, 1, 0, 1, 2, 0, 1],
         [2, 4, 3, 3, 2, 4, 3, 3])
TWO = ([0, 1] * 4, [2] * 8)
E0 = 5

BODIES = NB * (NB + 1) // 2
ROUTE_AT = {}
_free = 0
for _n in range(NB - 1):
    _t = max((_n + 1) * (_n + 2) // 2 + 1, _free)
    ROUTE_AT[_t] = ("project", _n)
    ROUTE_AT[_t + 1] = ("project_last", _n)
    ROUTE_AT[_t + 3] = ("count", _n)
    _free = _t + 4
SCATTER_AT = {t + 2 + k: (n, k) for t, (step, n) in ROUTE_AT.items() if step == "count" for k in range(2)}
SPLIT_AT = {t + 1: n for t, (step, n) in ROUTE_AT.items() if step == "count"}
assert max(SCATTER_AT) < BODIES


def attend(nc, io, sb, psum, sem, parts, shift, attnT, kop, qop, ident_b, cmask, v_stage, v_sb, r):
    with ExitStack() as st:
        prob = sb("prob", [P, KT, G, QB], F32, st)
        denom = sb("denom", [P, QB], F32, st)
        recip = sb("recip", [P, QB], F32, st)
        outT = sb("outT", [P, 2, QB], F32, st)
        ps_s = psum("ps_s", [P, 3, 2, QB], F32, st)
        ps_o = psum("ps_o", [P, 2, QB], F32, st)
        k_loaded = sem("k_loaded")
        q_loaded = [sem(f"q_loaded{s}") for s in range(2)]
        scores = sem("scores")
        exp_done = sem("exp_done")
        staged = sem("staged")
        pv_done = sem("pv_done")
        spread = sem("spread")
        inverted = sem("inverted")
        normed = sem("normed")
        out_stored = [sem(f"out_stored{s}") for s in range(2)]

        nc.sync.sem_inc(exp_done, E0)
        nc.sync.sem_inc(pv_done, KT)
        nc.sync.sem_inc(normed, 2)
        for s in out_stored:
            nc.sync.sem_inc(s, 64)

        with nc.Block() as block:
            @block.sync
            def _(sp):
                def store(g, b):
                    sp.wait_ge(normed, g * NB + (b + 1 + 2))
                    for h in range(G):
                        sp.dma_start(attnT[bass.ds(g * G * DH + h * DH, DH), b * QB:(b + 1) * QB],
                                     outT[32 * h:32 * h + DH, b % 2, :]).then_inc(out_stored[b % 2], 16)

                def group(g, last):
                    for b in range(NB):
                        sp.wait_ge(scores, tiles_before(g, b) * 2 + KT * (b + 1) * 2)
                        if b == 0 and not last:
                            load_keys(sp, io, parts, kop, lambda a, z: kop[a:z, (g + 1) % 2], g + 1, k_loaded)
                        if b + 2 < NB:
                            load_queries(sp, parts, shift, qop, b % 2, g, bass.ds((b + 2) * QB, QB), q_loaded[b % 2])
                        elif not last:
                            load_queries(sp, parts, shift, qop, b % 2, g + 1, bass.ds((b + 2 - NB) * QB, QB), q_loaded[b % 2])
                        if b >= 1:
                            store(g, b - 1)
                    store(g, NB - 1)

                load_keys(sp, io, parts, kop, lambda a, z: kop[a:z, 0], 0, k_loaded)
                for b in range(2):
                    load_queries(sp, parts, shift, qop, b, 0, bass.ds(b * QB, QB), q_loaded[b])
                r.load_constants(sp)
                with sp.Fori(0, NG - 1) as g:
                    group(g, False)
                for s in out_stored:
                    sp.wait_ge(s, 64 * ((NG - 1) * NB // 2 + 1))
                for b in range(NB):
                    if b >= 1:
                        sp.wait_ge(normed, (NG - 1) * NB + b + 2)
                        r.store(sp, b - 1, outT[:, (b - 1) % 2])
                    if b + 2 < NB:
                        sp.wait_ge(scores, tiles_before(NG - 1, b) * 2 + KT * (b + 1) * 2)
                        load_queries(sp, parts, shift, qop, b % 2, NG - 1, bass.ds((b + 2) * QB, QB), q_loaded[b % 2])
                    r.load(sp, b)
                sp.wait_ge(normed, NG * NB + 2)
                r.store(sp, NB - 1, outT[:, (NB - 1) % 2])
                sp.wait_ge(r.late, 64 * NB)

            @block.tensor
            def _(pe):
                def pv(t, r, b, q0, first, last):
                    pe.wait_ge(exp_done, t * 2 + (2 + E0))
                    pe.wait_ge(staged, t + 1)
                    for h in range(G):
                        mm = pe.matmul(ps_o[32 * h:32 * h + 32, b % 2, q0:], v_stage[:, r, h, :], prob[:, r, h, q0:],
                                       start=first, stop=last)
                    mm.then_inc(pv_done, 1)

                def body(g, b, t0, kt0, diag, before, opens, ring=THREE):
                    slot, back = ring
                    for r in range(KT):
                        q0 = r * P if diag else 0
                        for half in range(2):
                            n = 2 * r + half
                            pe.wait_ge(exp_done, t0 * 2 + (n - back[n] + 1 + E0))
                            for i in range(2):
                                h = 2 * half + i
                                out = ps_s[:, slot[n], i, :]
                                mm = pe.matmul(out[:, q0:], kop[:, g % 2, h, bass.ds(kt0 + r * P, P)],
                                               qop[:, b % 2, h, q0:], start=True, stop=not diag)
                                if diag:
                                    mm = pe.matmul(out[:, q0:q0 + P], ident_b[:], cmask[:], start=False, stop=True)
                            mm.then_inc(scores, 1)
                        if r == 0:
                            before()
                        else:
                            pv(t0 + (r - 1), r - 1, b, q0 - P if diag else 0, opens and r == 1, False)

                def opening(g, b):
                    if b >= 1:
                        pv(tiles_before(g, b - 1) + (KT * b - 1), KT - 1, b - 1, (KT - 1) * P, False, True)
                    pe.wait_ge(normed, g * NB + (b + 1))

                with pe.Fori(0, NG - 1) as g:
                    pe.wait_ge(k_loaded, g * (16 * LOADS) + 16 * LOADS)
                    alone(pe)
                    for b in range(NB):
                        pe.wait_ge(q_loaded[b % 2], g * (NB // 2 * 16 * LOADS) + (b // 2 + 1) * 16 * LOADS)
                        T0 = tiles_before(g, b)

                        def first():
                            opening(g, b)

                        def inner(t0):
                            return lambda: pv(t0, KT - 1, b, 0, False, False)

                        if b >= 1:
                            body(g, b, T0, 0, False, first, True)
                        if b >= 2:
                            with pe.Fori(0, b - 1) as j:
                                body(g, b, T0 + KT + j * KT, QB + j * QB, False, inner(T0 + (KT - 1) + j * KT), False)
                        body(g, b, T0 + KT * b, QB * b, True, inner(T0 + (KT * b - 1)) if b else first, b == 0)
                    pv(tiles_before(g, NB - 1) + (KT * NB - 1), KT - 1, NB - 1, (KT - 1) * P, False, True)

                g, t = NG - 1, 0
                pe.wait_ge(k_loaded, NG * 16 * LOADS)
                for b in range(NB):
                    pe.wait_ge(q_loaded[b % 2], (g * NB // 2 + b // 2 + 1) * 16 * LOADS)
                    T0 = tiles_before(g, b)
                    for j in range(b + 1):
                        def before():
                            if j == 0:
                                opening(g, b)
                            else:
                                pv(T0 + KT * j - 1, KT - 1, b, 0, False, False)

                        body(g, b, T0 + KT * j, QB * j, j == b, before, j == 0, TWO)
                        if t == 0:
                            r.pe_setup(pe, ps_s[:, 2, 0])
                        r.pe_step(pe, ROUTE_AT.get(t), ps_s[:, 2])
                        t += 1
                pv(tiles_before(g, NB - 1) + (KT * NB - 1), KT - 1, NB - 1, (KT - 1) * P, False, True)

            @block.scalar
            def _(act):
                def body(t0, diag, ring=THREE):
                    for r in range(KT):
                        q0 = r * P if diag else 0
                        act.wait_ge(pv_done, t0 + (r + 1))
                        for half in range(2):
                            act.wait_ge(scores, t0 * 2 + (2 * r + half + 1))
                            act.activation(prob[:, r, 2 * half:2 * half + 2, q0:],
                                           ps_s[:, ring[0][2 * r + half], :, q0:], ACT.Exp).then_inc(exp_done, 1)

                with act.Fori(0, NG - 1) as g:
                    for b in range(NB):
                        T0 = tiles_before(g, b)
                        if b >= 1:
                            with act.Fori(0, b) as j:
                                body(T0 + j * KT, False)
                        body(T0 + KT * b, True)
                for b in range(NB):
                    T0 = tiles_before(NG - 1, b)
                    if b >= 1:
                        with act.Fori(0, b) as j:
                            body(T0 + j * KT, False, TWO)
                    body(T0 + KT * b, True, TWO)

            @block.gpsimd
            def _(pool):
                def body(g, t0, kt0, scatter=None):
                    for q in range(KT):
                        pool.wait_ge(pv_done, t0 + (q + 1))
                        alone(pool)
                        src = v_sb[:, bass.ds(kt0 + q, 1), bass.ds(g * (G * DH), G * DH)]
                        pool.tensor_copy(v_stage[:, q, :, 0:DH], src.rearrange("p o (h d) -> p (o h) d", h=G)).then_inc(staged, 1)
                        if scatter:
                            n, half = scatter
                            r.scatter(pool, n, half * KT + q)

                with pool.Fori(0, NG - 1) as g:
                    for b in range(NB):
                        with pool.Fori(0, b + 1) as j:
                            body(g, tiles_before(g, b) + j * KT, j * KT)
                g, t = NG - 1, 0
                for b in range(NB):
                    for j in range(b + 1):
                        if t in SPLIT_AT:
                            r.split(pool, SPLIT_AT[t])
                        body(g, tiles_before(g, b) + j * KT, j * KT, SCATTER_AT.get(t))
                        t += 1
                r.pool_end(pool)

            @block.vector
            def _(dve):
                spread_mask = [DH + i % DH for i in range(32)]

                def normalise(g, b, late=False):
                    n = g * NB + (b + 1)
                    dve.wait_ge(pv_done, tiles_before(g, b) + (KT * (b + 1) + KT))
                    alone(dve)
                    dve.stream_shuffle(denom[:], ps_o[:, b % 2, :], spread_mask).then_inc(spread, 1)
                    dve.wait_ge(spread, n)
                    dve.reciprocal(recip[:], denom[:]).then_inc(inverted, 1)
                    dve.wait_ge(inverted, n)
                    if late and b >= 2:
                        dve.wait_ge(r.late, 64 * (b - 1))
                    else:
                        dve.wait_ge(out_stored[b % 2], g * (64 * NB // 2) + 64 * (b // 2 + 1 if not late else 1))
                    dve.tensor_tensor(outT[:, b % 2, :], ps_o[:, b % 2, :], recip[:], ALU.mult).then_inc(normed, 1)

                with dve.Fori(0, NG - 1) as g:
                    for b in range(NB):
                        normalise(g, b)
                r.dve_constants(dve)
                t = 0
                for b in range(NB):
                    for j in range(b + 1):
                        if j == 0 and b >= 1:
                            normalise(NG - 1, b - 1, True)
                        if t == 0:
                            r.dve_setup(dve, ps_s[:, 2, 0])
                        r.dve_step(dve, ROUTE_AT.get(t), ps_s[:, 2])
                        t += 1
                normalise(NG - 1, NB - 1, True)



RSQRT_MAGIC = 0x5F3759DF
NEWTON = 3
RSQRT_STEPS = 3 + 3 * NEWTON


def rsqrt(c, var, tmp, out):
    dve = c.eng
    v, sq, half, a, b = tmp
    c.did(dve.tensor_scalar(v, var, EPS, None, ALU.add))
    c.wait()
    c.did(dve.tensor_scalar(a.bitcast(I32), v.bitcast(I32), 1, None, ALU.arith_shift_right))
    c.wait()
    c.did(dve.tensor_scalar(b.bitcast(I32), a.bitcast(I32), -1, RSQRT_MAGIC, ALU.mult, ALU.add))
    c.wait()
    root = b
    for k in range(NEWTON):
        to = out if k == NEWTON - 1 else (a, b)[k % 2]
        c.did(dve.tensor_tensor(sq, root, root, ALU.mult))
        c.wait()
        c.did(dve.scalar_tensor_tensor(out=half, in0=sq, scalar=-0.5, in1=v, op0=ALU.mult, op1=ALU.mult))
        c.wait()
        c.did(dve.scalar_tensor_tensor(out=to, in0=half, scalar=1.5, in1=root, op0=ALU.add, op1=ALU.mult))
        c.wait()
        root = to


class Router:

    STEPS = 4 + 4 + RSQRT_STEPS + 3 + 4 + 4 + 1 + 1 + 2 + 3 + 1 + 1 + 1 + 1 + 1
    CONSTANTS = 6

    def __init__(r, io, sb, sem, attnT, slots_x, x1_all, dest_all, weight_all):
        r.io, r.attnT, r.slots_x, r.x1, r.dest_all, r.weight_all = io, attnT, slots_x, x1_all, dest_all, weight_all
        r.aT = sb("aT", [P, 2, 2, QB], F32)
        r.xT = sb("rxT", [P, 2, QB], F32)
        r.xsplit = sb("xsplit", [P, KT, 2, D], BF16)
        r.wp = sb("wp", [P, 2, D + E], F32)
        r.wpn = sb("wpn", [P, 2, D], F32)
        r.wg = sb("wg", [P, 2, E], F32)
        r.wsum = sb("wsum", [P, E], F32)
        r.ones_f = sb("ones_f", [P, P], F32)
        r.before = sb("before", [P, P], BF16)
        r.ones = sb("ones", [P, P], BF16)
        r.iota = sb("iota", [P, KT, 2, E], F32)
        r.stats = sb("stats", [P, KT, 6], F32)
        r.mv = sb("mv", [P, KT, 2], F32)
        r.tmp = sb("tmp", [P, 5, KT], F32)
        r.rstd = sb("rstd", [P, KT], F32)
        r.slogit = sb("slogit", [P, KT, E], F32)
        r.shiftl = sb("shiftl", [P, KT, E], F32)
        r.clogit = sb("clogit", [P, KT, E], F32)
        r.logit = sb("logit", [P, KT, E], F32)
        r.top = sb("top", [P, KT, 8], F32)
        r.topi = sb("topi", [P, KT, 8], U32)
        r.chosen = sb("chosen", [P, KT, 2], F32)
        r.hot = sb("hot", [P, KT, 2, E], F32)
        r.counts = sb("counts", [P, KT, E], BF16)
        r.ahead = sb("ahead", [P, KT, E], BF16)
        r.run = sb("run", [P, E], BF16)
        r.place = sb("place", [P, KT, 2, E], F32)
        r.pos = sb("pos", [P, KT * 2], F32)
        r.row = sb("row", [P, KT * 2], F32)
        r.row2 = sb("row2", [P, KT * 2], F32)
        r.gap_all = sb("gap_all", [P, NB, KT], F32)
        r.gexp = sb("gexp", [P, NB, KT], F32)
        r.gsum = sb("gsum", [P, NB, KT], F32)
        r.gate = sb("gate", [P, NB, KT, 2], F32)
        r.keep_all = sb("keep_all", [P, NB, KT * 2], F32)

        r.const = sem("r_const")
        r.loaded = sem("r_loaded")
        r.late = sem("last_group_out")
        r.split_high = sem("split_high")
        r.split_low = sem("split_low")
        r.ones_done = sem("ones_done")
        r.setup_mm = sem("setup_mm")
        r.setup_done = sem("setup_done")
        r.y_mm = sem("y_mm")
        r.summed = sem("summed")
        r.logits_out = sem("logits_out")
        r.step = sem("r_step")
        r.x1_done = sem("x1_done")
        r.count_done = sem("count_done")
        r.c_mm = sem("c_mm")
        r.placed = sem("placed")
        r.dest_done = sem("dest_done")
        r.scattered = sem("scattered")
        r.gexp_done = sem("gexp_done")
        r.g_step = sem("g_step")
        r.weights = sem("weights")


    def load_constants(r, sp):
        io = r.io
        for dst, src in ((r.wp[:, :, 0:D], io["WpT"].rearrange("(c p) o -> p c o", p=P)),
                         (r.wpn[:], io["Wp"].rearrange("(c p) i -> p c i", p=P)),
                         (r.wg[:], io["Wg"].rearrange("(c p) e -> p c e", p=P)),
                         (r.before[:], io["before"]), (r.ones[:], io["ones"]), (r.iota[:], io["iota"])):
            sp.dma_start(dst, src).then_inc(r.const, 16)

    def load(r, sp, n):
        cols = slice(n * QB, (n + 1) * QB)
        if n >= 2:
            sp.wait_ge(r.y_mm, (n - 1) * KT)
        old = r.attnT[:, cols]
        sp.dma_start(r.aT[:, n % 2, 0], old[0:P]).then_inc(r.loaded, 16)
        sp.dma_start(r.aT[0:LATE, n % 2, 1], old[P:P + LATE]).then_inc(r.loaded, 16)
        x = r.io["x"].rearrange("(n t p) d -> n p t d", t=KT, p=P)
        sp.dma_start(r.x1[:, n], x[n]).then_inc(r.loaded, 16)
        if n >= 1:
            sp.wait_ge(r.y_mm, n * KT)
        sp.dma_start(r.xT[:], r.io["xT"].rearrange("(c p) t -> p c t", p=P)[:, :, cols]).then_inc(r.loaded, 16)

    def store(r, sp, n, out):
        if n >= 2:
            sp.wait_ge(r.y_mm, (n - 1) * KT)
        for h in range(G):
            sp.dma_start(r.aT[LATE + h * DH:LATE + (h + 1) * DH, n % 2, 1], out[32 * h:32 * h + DH]).then_inc(r.late, 16)


    def pe_setup(r, pe, bank):
        pe.wait_ge(r.const, 16 * r.CONSTANTS)
        pe.wait_ge(r.ones_done, 1)
        for i in range(2):
            for c in range(2):
                pe.matmul(bank[:, i * E:(i + 1) * E], r.wpn[:, c, i * P:(i + 1) * P], r.wg[:, c, :],
                          start=(c == 0), stop=(c == 1))
        for c in range(2):
            mm = pe.matmul(bank[:, 2 * E:3 * E], r.ones_f[:], r.wg[:, c, :], start=(c == 0), stop=(c == 1))
        mm.then_inc(r.setup_mm, 1)

    def pe_step(r, pe, step, banks):
        if step is None:
            return
        what, n = step
        u = n % 2

        def tile(s, out):
            for c in range(2):
                mm = pe.matmul(out, r.aT[:, u, c, s * P:(s + 1) * P], r.wp[:, c, :], start=(c == 0), stop=False)
            for c in range(2):
                mm = pe.matmul(out[:, D:], r.xT[:, c, s * P:(s + 1) * P], r.wg[:, c, :], start=False, stop=(c == 1))
            mm.then_inc(r.y_mm, 1)

        if what == "project":
            pe.wait_ge(r.loaded, 64 * (n + 1))
            pe.wait_ge(r.late, 64 * (n + 1))
            if n == 0:
                pe.wait_ge(r.setup_done, 2)
            else:
                pe.wait_ge(r.placed, n)
            for s in range(2):
                tile(s, banks[:, s, 0:D + E])
        elif what == "project_last":
            for s in range(2, KT):
                pe.wait_ge(r.summed, n * KT + s - 1)
                pe.wait_ge(r.logits_out, n * KT + s - 1)
                tile(s, banks[:, s % 2, 0:D + E])
        else:
            pe.wait_ge(r.count_done, n + 1)
            out = banks[:, 0, 0:KT * E]
            pe.matmul(out, r.before[:], r.counts[:].rearrange("p s e -> p (s e)"), start=True, stop=False)
            pe.matmul(out, r.ones[:], r.ahead[:].rearrange("p s e -> p (s e)"), start=False, stop=True).then_inc(r.c_mm, 1)


    def dve_constants(r, dve):
        dve.memset(r.ones_f[:], 1.0).then_inc(r.ones_done, 1)
        dve.memset(r.run[:], 0.0).then_inc(r.ones_done, 1)

    def dve_setup(r, dve, bank):
        dve.wait_ge(r.setup_mm, 1)
        dve.tensor_copy(r.wp[:, :, D:], bank[:, 0:2 * E].rearrange("p (c e) -> p c e", c=2)).then_inc(r.setup_done, 1)
        dve.tensor_copy(r.wsum[:], bank[:, 2 * E:3 * E]).then_inc(r.setup_done, 1)

    def dve_step(r, dve, step, banks):
        if step is None:
            return
        what, n = step
        if what != "count":
            for s in (range(2) if what == "project" else range(2, KT)):
                dve.wait_ge(r.y_mm, n * KT + s + 1)
                dve.tensor_copy(r.slogit[:, s], banks[:, s % 2, D:D + E]).then_inc(r.logits_out, 1)
                dve.tensor_tensor(r.x1[:, n, s], banks[:, s % 2, 0:D], r.x1[:, n, s], ALU.add).then_inc(r.summed, 1)
        if what == "project_last":
            r.choose(dve, n)
        if what == "count":
            r.places(dve, n, banks)

    def choose(r, dve, n):
        c = Chain(dve, r.step, n * r.STEPS, r.STEPS)
        r.chain = c
        layernorm_stats(c, lambda s: dve.wait_ge(r.summed, n * KT + (s + 1)), lambda s: r.x1[:, n, s], r.stats, r.mv)
        rsqrt(c, r.mv[:, :, 1], [r.tmp[:, k] for k in range(5)], r.rstd[:])
        for s in range(KT):
            dve.tensor_scalar(r.x1[:, n, s], r.x1[:, n, s], r.mv[:, s, 0:1], r.rstd[:, s:s + 1],
                              ALU.subtract, ALU.mult).then_inc(r.x1_done, 1)
        mean = r.mv[:, :, 0:1].broadcast_to([P, KT, E])
        c.did(dve.tensor_tensor(r.shiftl[:], mean, r.wsum[:].unsqueeze(1).broadcast_to([P, KT, E]), ALU.mult))
        c.wait()
        dve.wait_ge(r.logits_out, (n + 1) * KT)
        c.did(dve.tensor_tensor(r.clogit[:], r.slogit[:], r.shiftl[:], ALU.subtract))
        c.wait()
        c.did(dve.tensor_tensor(r.logit[:], r.clogit[:], r.rstd[:].unsqueeze(2).broadcast_to([P, KT, E]), ALU.mult))
        c.wait()
        for s in range(KT):
            c.did(dve.max(r.top[:, s], r.logit[:, s]))
        c.wait()
        for s in range(KT):
            c.did(dve.max_index(r.topi[:, s], r.top[:, s], r.logit[:, s]))
        c.wait()
        c.did(dve.tensor_copy(r.chosen[:], r.topi[:, :, 0:2]))
        c.wait()
        c.did(dve.tensor_tensor(r.hot[:], r.iota[:], r.chosen[:].unsqueeze(3).broadcast_to([P, KT, 2, E]), ALU.is_equal))
        c.wait()
        c.did(dve.tensor_tensor(r.counts[:], r.hot[:, :, 0], r.hot[:, :, 1], ALU.add))
        if n == 0:
            dve.wait_ge(r.ones_done, 2)
        c.did(dve.tensor_copy(r.ahead[:, 0], r.run[:]))
        c.wait()
        for s in range(1, KT):
            c.did(dve.tensor_tensor(r.ahead[:, s], r.ahead[:, s - 1], r.counts[:, s - 1], ALU.add))
            c.wait()
        dve.tensor_tensor(r.run[:], r.ahead[:, KT - 1], r.counts[:, KT - 1], ALU.add).then_inc(r.count_done, 1)
        c.did(dve.tensor_tensor(r.gap_all[:, n], r.top[:, :, 1], r.top[:, :, 0], ALU.subtract))

    def places(r, dve, n, banks):
        c = r.chain
        dve.wait_ge(r.c_mm, n + 1)
        ahead = banks[:, 0, 0:KT * E].rearrange("p (s e) -> p s e", s=KT)
        dve.tensor_tensor(r.place[:], r.hot[:], ahead.unsqueeze(2).broadcast_to([P, KT, 2, E]), ALU.mult).then_inc(r.placed, 1)
        dve.wait_ge(r.placed, n + 1)
        c.did(dve.tensor_reduce(r.pos[:], r.place[:].rearrange("p s k e -> p (s k) e"), AX.X, ALU.add))
        c.wait()
        c.did(dve.tensor_scalar(r.keep_all[:, n], r.pos[:], float(CAP), None, ALU.is_lt))
        c.did(dve.scalar_tensor_tensor(out=r.row[:], in0=r.chosen[:].rearrange("p s k -> p (s k)"),
                                       scalar=float(CAP), in1=r.pos[:], op0=ALU.mult, op1=ALU.add))
        c.wait()
        c.did(dve.scalar_tensor_tensor(out=r.row2[:], in0=r.row[:], scalar=-float(DROPPED), in1=r.keep_all[:, n],
                                       op0=ALU.add, op1=ALU.mult))
        c.wait()
        dve.tensor_scalar(r.dest_all[:, n], r.row2[:], float(DROPPED), None, ALU.add).then_inc(r.dest_done, 1)
        c.end()

    def split(r, pool, n):
        pool.wait_ge(r.x1_done, (n + 1) * KT)
        if n >= 1:
            pool.wait_ge(r.scattered, n * KT * 2 * 16)
        pool.tensor_copy(r.xsplit[:, :, 0], r.x1[:, n]).then_inc(r.split_high, 1)
        r.split_rest(pool, n)

    def split_rest(r, pool, n):
        pool.wait_ge(r.split_high, n + 1)
        pool.tensor_tensor(r.xsplit[:, :, 1], r.x1[:, n], r.xsplit[:, :, 0], ALU.subtract).then_inc(r.split_low, 1)

    def scatter(r, pool, n, m):
        if m == 0:
            pool.wait_ge(r.dest_done, n + 1)
            pool.wait_ge(r.split_low, n + 1)
            alone(pool)
        pool.indirect_dma_start(
            out=r.slots_x, out_offset=bass.IndirectOffsetOnAxis(ap=r.dest_all[:, n, m:m + 1], axis=0),
            in_=r.xsplit[:, m // 2].rearrange("p a d -> p (a d)").bitcast(F32), in_offset=None, bounds_check=SLOTS - 1,
            oob_is_err=False).then_inc(r.scattered, 16)

    def pool_end(r, pool):
        pool.wait_ge(r.scattered, (NB - 1) * KT * 2 * 16)

    def act_gates(r, act):
        act.wait_ge(r.step, NB * r.STEPS)
        act.activation(r.gexp[:], r.gap_all[:], ACT.Exp).then_inc(r.gexp_done, 1)

    def dve_gates(r, dve):
        c = Chain(dve, r.g_step, 0, 3)
        dve.wait_ge(r.gexp_done, 1)
        c.did(dve.tensor_scalar(r.gsum[:], r.gexp[:], 1.0, None, ALU.add))
        c.wait()
        c.did(dve.reciprocal(r.gate[:, :, :, 0], r.gsum[:]))
        c.wait()
        c.did(dve.tensor_tensor(r.gate[:, :, :, 1], r.gexp[:], r.gate[:, :, :, 0], ALU.mult))
        c.wait()
        c.end()
        dve.tensor_tensor(r.weight_all[:], r.gate[:].rearrange("p n s k -> p n (s k)"), r.keep_all[:],
                          ALU.mult).then_inc(r.weights, 1)


def route_last(nc, io, psum, r, x):
    n = NB - 1
    with ExitStack() as st:
        banks = psum("ps_r", [P, 2, QB], F32, st)
        with nc.Block() as block:
            @block.sync
            def _(sp):
                x.load_weights(sp, io, 0, 0)
                x.load_constants(sp, io)
                x.load_weights(sp, io, 1, 1)

            @block.tensor
            def _(pe):
                for what in ("project", "project_last", "count"):
                    r.pe_step(pe, (what, n), banks)

            @block.vector
            def _(dve):
                for what in ("project", "project_last", "count"):
                    r.dve_step(dve, (what, n), banks)
                r.dve_gates(dve)

            @block.scalar
            def _(act):
                for k in range(2):
                    x.weights_high(act, 0, 0, 0, k)
                act.wait_ge(r.x1_done, NB * KT)
                act.wait_ge(r.scattered, n * KT * 2 * 16)
                act.activation(r.xsplit[:, :, 0], r.x1[:, n], ACT.Identity).then_inc(r.split_high, 1)
                r.act_gates(act)

            @block.gpsimd
            def _(pool):
                x.weights_low(pool, 0, 0, 0)
                r.split_rest(pool, n)
                for m in range(2 * KT):
                    r.scatter(pool, n, m)
                x.weights_low(pool, 0, 0, 1)
                pool.wait_ge(r.scattered, NB * KT * 2 * 16)


def layernorm_stats(c, ready, src, stats, mv):
    dve = c.eng
    for s in range(KT):
        ready(s)
        c.did(dve.bn_stats(stats[:, s], src(s)))
    c.wait()
    alone(dve)
    for s in range(KT):
        c.did(dve.bn_aggr(mv[:, s], stats[:, s]))
    c.wait()



SB = [(0, 3), (3, 6), (6, ST)]


class Experts:

    def __init__(x, sb, sem):
        x.sb, x.sem = sb, sem
        x.w1 = sb("w1", [P, 2, 2, HID], F32)
        x.w2 = sb("w2", [P, 2, HC, D], F32)
        x.w1s = sb("w1s", [P, 2, 2, 2, HID], BF16)
        x.w2s = sb("w2s", [P, 2, 2, HC, D], BF16)
        x.b1 = sb("b1", [P, E, HC], F32)
        x.b2 = sb("b2", [P, E, D], F32)
        x.ident = sb("ident5", [P, P], BF16)
        x.const = sem("e_const")
        x.w_loaded = [sem(f"we_loaded{u}") for u in range(2)]
        x.ye_mm = sem("ye_mm")
        x.wh = sem("w_high")
        x.ws = sem("w_split")

    def load_constants(x, sp, io):
        sp.dma_start(x.ident[:], io["ident_b"]).then_inc(x.const, 16)
        sp.dma_start(x.b1[:], io["b1T"]).then_inc(x.const, 16)
        for e in range(E):
            sp.dma_start(x.b2[:, e], io["b2"][e:e + 1].broadcast_to([P, D])).then_inc(x.const, 16)

    def load_weights(x, sp, io, u, e):
        sp.dma_start(x.w1[:, u], io["W1"][e].rearrange("(c p) h -> p c h", p=P)).then_inc(x.w_loaded[u], 16)
        sp.dma_start(x.w2[:, u], io["W2"][e].rearrange("(c p) d -> p c d", p=P)).then_inc(x.w_loaded[u], 16)

    def weights_high(x, act, e, i, u, k):
        act.wait_ge(x.w_loaded[u], i * 32 + 32)
        if not (isinstance(e, int) and e < 2):
            act.wait_ge(x.ye_mm, (e - 1) * ST)
        src, dst = ((x.w1, x.w1s), (x.w2, x.w2s))[k]
        act.activation(dst[:, u, 0], src[:, u], ACT.Identity).then_inc(x.wh, 1)

    def weights_low(x, pool, e, u, k):
        src, dst = ((x.w1, x.w1s), (x.w2, x.w2s))[k]
        pool.wait_ge(x.wh, e * 2 + (k + 1))
        alone(pool)
        pool.tensor_tensor(dst[:, u, 1], src[:, u], dst[:, u, 0], ALU.subtract).then_inc(x.ws, 1)


def experts(nc, io, psum, slots_x, slots_y, X, st):
    sb, sem = X.sb, X.sem
    w1s, w2s, b1, b2, ident, ws, ye_mm = X.w1s, X.w2s, X.b1, X.b2, X.ident, X.ws, X.ye_mm
    if True:
        warm = sb("warm5", [1, 1], F32)
        xe = sb("xe", [P, 2, ST, D], F32)
        xs = sb("xs", [P, 2, 2, 2, ST * P], BF16)
        hid = sb("hid", [P, 4, 3 * P], F32)
        hs = sb("hs", [P, 2, 2, HC, 3 * P], BF16)
        y = sb("y", [P, 3, D], F32)
        ps_h = psum("ps_h", [P, 4, QB], F32, st)
        ps_y = psum("ps_y5", [P, 2, QB], F32, st)
        ps_x = psum("ps_x", [P, 2, 2 * QB], BF16, st)

        x_first = [sem(f"xe_first{u}") for u in range(2)]
        x_loaded = [sem(f"xe_loaded{u}") for u in range(2)]
        x_mm = sem("x_mm")
        x_out = sem("x_out")
        h_mm = sem("h_mm")
        gelu = sem("gelu")
        h_high = sem("h_high")
        h_low = sem("h_low")
        y_out = sem("y_out")
        y_stored = [sem(f"y_stored{k}") for k in range(3)]

        nc.sync.sem_inc(x_out, 2)
        nc.sync.sem_inc(h_low, 4)
        nc.sync.sem_inc(ye_mm, 2 * ST)
        nc.sync.sem_inc(h_mm, 2 * 24)
        nc.sync.sem_inc(y_out, 2)
        nc.sync.sem_inc(gelu, 4)
        for k in range(3):
            nc.sync.sem_inc(y_stored[k], 16)

        def width(sbk):
            a, z = SB[sbk]
            return min(z * P, CAP) - a * P

        def rows_of(k):
            return LAST if k == ST - 1 else P

        def over_experts(eng, one):
            for u in range(2):
                one(u, 0, u, True)
            with eng.Fori(1, E // 2 - 1) as i:
                for u in range(2):
                    one(2 * i + u, i, u, True)
            for u in range(2):
                one(E - 2 + u, E // 2 - 1, u, u == 0)

        xs_d = slots_x[0:SLOTS].rearrange("(e r) d -> e r d", e=E)
        ys_d = slots_y[0:SLOTS].rearrange("(e r) d -> e r d", e=E)
        with nc.Block() as block:
            @block.sync
            def _(sp):
                def load(u, e):
                    z = SB[0][1]
                    sp.dma_start(xe[:, u, 0:z], xs_d[e, 0:z * P].rearrange("(k p) d -> p k d", p=P)).then_inc(x_first[u], 16)
                    sp.dma_start(xe[:, u, z:ST - 1], xs_d[e, z * P:(ST - 1) * P].rearrange("(k p) d -> p k d", p=P)).then_inc(x_loaded[u], 16)
                    sp.dma_start(xe[0:LAST, u, ST - 1], xs_d[e, (ST - 1) * P:CAP]).then_inc(x_loaded[u], 16)

                def store(e):
                    for k in range(ST):
                        n = rows_of(k)
                        sp.wait_ge(y_out, e * ST + (k + 1 + 2))
                        sp.dma_start(ys_d[e, k * P:k * P + n], y[0:n, k % 3]).then_inc(y_stored[k % 3], 16)

                load(0, 0)
                load(1, 1)
                with sp.Fori(0, E // 2 - 1) as i:
                    for u in range(2):
                        e = 2 * i + u
                        sp.wait_ge(ws, e * 2 + 2)
                        sp.wait_ge(x_mm, e * ST + ST)
                        X.load_weights(sp, io, u, e + 2)
                        load(u, e + 2)
                        store(e)
                for e in range(E - 2, E):
                    store(e)
                for k in range(3):
                    sp.wait_ge(y_stored[k], 16 * (E * ST // 3 + 1))

            @block.gpsimd
            def _(pool):
                for k in range(2):
                    X.weights_low(pool, 1, 1, k)
                with pool.Fori(1, E // 2) as i:
                    for u in range(2):
                        for k in range(2):
                            X.weights_low(pool, 2 * i + u, u, k)

            @block.tensor
            def _(pe):
                pe.wait_ge(X.const, 16 * (E + 2))

                def transpose(e, i, u, k):
                    if k == 0:
                        pe.wait_ge(x_first[u], i * 16 + 16)
                    if k == SB[0][1]:
                        pe.wait_ge(x_loaded[u], i * 32 + 32)
                    pe.wait_ge(x_out, e * ST + (k + 1))
                    alone(pe)
                    n = rows_of(k)
                    rows = xe[0:n, u, k].bitcast(BF16)
                    for c in range(4):
                        mm = pe.transpose(ps_x[:, (ST * u + k) % 2, c * P:c * P + n], rows[:, c * P:(c + 1) * P],
                                          ident[0:n, 0:n])
                    mm.then_inc(x_mm, 1)

                def up(e, u, sbk, m):
                    w = width(sbk)
                    q = sbk * HC + m
                    pe.wait_ge(gelu, e * 24 + (q + 1))
                    a = SB[sbk][0] * P
                    terms = [(0, 0), (0, 1), (1, 0)]
                    for t, (i1, i2) in enumerate(terms):
                        for c in range(2):
                            mm = pe.matmul(ps_h[:, q % 4, 0:w], w1s[:, u, i1, c, m * P:(m + 1) * P], xs[:, u, i2, c, a:a + w],
                                           start=(t == 0 and c == 0), stop=(t == 2 and c == 1))
                    mm.then_inc(h_mm, 1)

                def down(e, i, u, sbk, ahead):
                    for k in range(*SB[sbk]):
                        if ahead:
                            transpose(e + 1, i + u, 1 - u, k)
                        n = rows_of(k)
                        o = (k - SB[sbk][0]) * P
                        pe.wait_ge(y_out, e * ST + (k + 1))
                        pe.wait_ge(h_low, e * 24 + (sbk + 1) * HC + 4)
                        for t, (i1, i2) in enumerate([(0, 0), (0, 1), (1, 0)]):
                            for m in range(HC):
                                mm = pe.matmul(ps_y[0:n, (ST * u + k) % 2, 0:D], hs[:, (3 * u + sbk) % 2, i1, m, o:o + n],
                                               w2s[:, u, i2, m, :], start=(t == 0 and m == 0), stop=(t == 2 and m == HC - 1))
                        mm.then_inc(ye_mm, 1)

                def one(e, i, u, ahead):
                    pe.wait_ge(ws, e * 2 + 2)
                    first = isinstance(e, int) and e == 0
                    pe.wait_ge(x_out, e * ST + (SB[0][1] if first else ST) + 2)
                    for m in range(HC):
                        up(e, u, 0, m)
                        if first and SB[0][1] + m < ST:
                            transpose(0, 0, 0, SB[0][1] + m)
                    if first:
                        pe.wait_ge(x_out, ST + 2)
                    for m in range(HC):
                        up(e, u, 1, m)
                    down(e, i, u, 0, ahead)
                    for m in range(HC):
                        up(e, u, 2, m)
                    down(e, i, u, 1, ahead)
                    down(e, i, u, 2, ahead)

                for k in range(*SB[0]):
                    transpose(0, 0, 0, k)
                over_experts(pe, one)

            @block.scalar
            def _(act):
                act.wait_ge(X.const, 16 * (E + 2))
                act.activation(warm[:], b1[0:1, 0, 0:1], ACT.Gelu_apprx_tanh)

                def tokens(e, u, k):
                    act.wait_ge(x_mm, e * ST + (k + 1))
                    act.wait_ge(h_mm, e * 24 + 24)
                    n = rows_of(k)
                    src = ps_x[:, (ST * u + k) % 2, 0:4 * P].rearrange("p (c n) -> p c n", c=4)
                    act.activation(xs[:, u, :, :, k * P:k * P + n].rearrange("p a c n -> p (a c) n"), src[:, :, 0:n],
                                   ACT.Identity).then_inc(x_out, 1)

                def one(e, i, u, ahead):
                    def hidden(q):
                        w = width(q // HC)
                        act.wait_ge(h_mm, e * 24 + (q + 1 + 48))
                        act.wait_ge(h_low, e * 24 + (q + 1))
                        alone(act)
                        act.activation(hid[:, q % 4, 0:w], ps_h[:, q % 4, 0:w], ACT.Gelu_apprx_tanh,
                                       bias=b1[:, e, q % HC:q % HC + 1]).then_inc(gelu, 1)

                    first = isinstance(e, int) and e == 0
                    for q in range(2 * HC):
                        hidden(q)
                        if first and SB[0][1] + q < ST:
                            tokens(0, 0, SB[0][1] + q)
                        if ahead and q in (5, 13):
                            X.weights_high(act, e + 1, i + u, 1 - u, q // HC)
                    if ahead:
                        for k in range(*SB[0]):
                            tokens(e + 1, 1 - u, k)
                    for q in range(2 * HC, 3 * HC):
                        hidden(q)
                    if ahead:
                        for k in range(SB[1][0], ST):
                            tokens(e + 1, 1 - u, k)

                for k in range(*SB[0]):
                    tokens(0, 0, k)
                over_experts(act, one)

            @block.vector
            def _(dve):
                def out(e, u, k):
                    n = rows_of(k)
                    dve.wait_ge(ye_mm, e * ST + (k + 1 + 2 * ST))
                    dve.wait_ge(y_stored[k % 3], e * (16 * ST // 3) + (k // 3) * 16 + 16)
                    bias = b2[0:n, bass.ds(e, 1)].rearrange("p o d -> p (o d)")
                    dve.tensor_tensor(y[0:n, k % 3], ps_y[0:n, (ST * u + k) % 2, 0:D], bias, ALU.add).then_inc(y_out, 1)

                def split(e, u, q):
                    w = width(q // HC)
                    sl = (3 * u + q // HC) % 2
                    dve.wait_ge(gelu, e * 24 + (q + 1 + 4))
                    if q % HC == 0:
                        dve.wait_ge(ye_mm, e * ST + (ends(q // HC - 2)) + 2 * ST)
                    dve.tensor_copy(hs[:, sl, 0, q % HC, 0:w], hid[:, q % 4, 0:w]).then_inc(h_high, 1)
                    dve.wait_ge(h_high, e * 24 + (q + 1))
                    dve.tensor_tensor(hs[:, sl, 1, q % HC, 0:w], hid[:, q % 4, 0:w], hs[:, sl, 0, q % HC, 0:w],
                                      ALU.subtract).then_inc(h_low, 1)

                def ends(sbk):
                    return SB[sbk][1] if sbk >= 0 else SB[sbk % 3][1] - ST

                def one(e, i, u, ahead):
                    for q in range(2 * HC):
                        split(e, u, q)
                    for k in range(ST):
                        if k >= 1:
                            out(e, u, k - 1)
                        if k == SB[0][1] - 1:
                            for q in range(2 * HC, 3 * HC):
                                split(e, u, q)
                    out(e, u, ST - 1)

                over_experts(dve, one)



def combine(nc, io, sb, psum, sem, x1_all, slots_y, dest_all, weight_all):
    with ExitStack() as st:
        yg = sb("yg", [P, 2, KT * 2, D], F32, st)
        z = sb("z", [P, 2, KT, D], F32, st)
        half = sb("half", [P, KT, D], F32, st)
        dest = sb("destc", [P, 2, KT * 2], U32, st)
        weight = sb("weightc", [P, 2, KT * 2], F32, st)
        stats = sb("statsc", [P, KT, 6], F32, st)
        mv = sb("mvc", [P, KT, 2], F32, st)
        tmp = sb("tmpc", [P, 5, KT], F32, st)
        nmr = sb("nmr", [P, 2, KT], F32, st)
        rstd = sb("rstdc", [P, 2, KT], F32, st)
        gathered = [[sem(f"gathered{u}{s}") for s in range(KT)] for u in range(2)]
        dest_set = sem("dest_set")
        weight_set = sem("weight_set")
        z_done = sem("z_done")
        c_step = sem("c_step")
        applied = sem("applied")
        out_done = [sem(f"out_done{u}") for u in range(2)]
        STEPS = 4 + 4 + RSQRT_STEPS
        half_done = sem("half_done")
        scales = sem("scales")
        nc.sync.sem_inc(z_done, 2 * KT)
        nc.sync.sem_inc(applied, 2 * KT)
        for u in range(2):
            nc.sync.sem_inc(out_done[u], 16)

        out_v = io["out"].rearrange("o (n t p) d -> (o n) p t d", t=KT, p=P)
        with nc.Block() as block:
            @block.sync
            def _(sp):
                def store(u, n):
                    sp.wait_ge(applied, n * KT + 3 * KT)
                    sp.dma_start(out_v[n], z[:, u]).then_inc(out_done[u], 16)

                with sp.Fori(0, NB // 2) as i:
                    for u in range(2):
                        store(u, 2 * i + u)
                for u in range(2):
                    sp.wait_ge(out_done[u], 16 * (NB // 2 + 1))

            @block.gpsimd
            def _(pool):
                with pool.Fori(0, NB // 2) as i:
                    for u in range(2):
                        n = 2 * i + u
                        pool.wait_ge(z_done, n * KT + KT)
                        alone(pool)
                        pool.tensor_copy(dest[:, u], dest_all[:, bass.ds(n, 1)].rearrange("p o k -> p (o k)")).then_inc(dest_set, 1)
                        pool.wait_ge(dest_set, n + 1)
                        alone(pool)
                        for m in range(2 * KT):
                            pool.indirect_dma_start(
                                out=yg[:, u, m], out_offset=None, in_=slots_y,
                                in_offset=bass.IndirectOffsetOnAxis(ap=dest[:, u, m:m + 1], axis=0)).then_inc(gathered[u][m // 2], 16)

            @block.scalar
            def _(act):
                with act.Fori(0, NB // 2) as i:
                    for u in range(2):
                        n = 2 * i + u
                        act.wait_ge(scales, n + 1)
                        alone(act)
                        for s in range(KT):
                            act.activation(z[:, u, s], z[:, u, s], ACT.Identity, scale=rstd[:, u, s:s + 1],
                                           bias=nmr[:, u, s:s + 1]).then_inc(applied, 1)

            @block.vector
            def _(dve):
                with dve.Fori(0, NB // 2) as i:
                    for u in range(2):
                        n = 2 * i + u
                        c = Chain(dve, c_step, n * STEPS, STEPS)
                        dve.tensor_copy(weight[:, u], weight_all[:, bass.ds(n, 1)].rearrange("p o k -> p (o k)")).then_inc(weight_set, 1)
                        dve.wait_ge(weight_set, n + 1)
                        dve.wait_ge(out_done[u], i * 16 + 16)

                        def first(s):
                            dve.wait_ge(gathered[u][s], i * 32 + 32)
                            alone(dve)
                            dve.scalar_tensor_tensor(out=half[:, s], in0=yg[:, u, 2 * s], scalar=weight[:, u, 2 * s:2 * s + 1],
                                                     in1=x1_all[:, bass.ds(n, 1), s].rearrange("p o d -> p (o d)"), op0=ALU.mult, op1=ALU.add).then_inc(half_done, 1)

                        def second(s):
                            dve.wait_ge(half_done, n * KT + s + 1)
                            dve.scalar_tensor_tensor(out=z[:, u, s], in0=yg[:, u, 2 * s + 1], scalar=weight[:, u, 2 * s + 1:2 * s + 2],
                                                     in1=half[:, s], op0=ALU.mult, op1=ALU.add).then_inc(z_done, 1)

                        def spread(s):
                            dve.wait_ge(z_done, n * KT + (s + 1 + 2 * KT))
                            c.did(dve.bn_stats(stats[:, s], z[:, u, s]))

                        for s in range(KT + 2):
                            if s < KT:
                                first(s)
                            if 1 <= s <= KT:
                                second(s - 1)
                            if s >= 2:
                                spread(s - 2)
                        c.wait()
                        alone(dve)
                        for s in range(KT):
                            c.did(dve.bn_aggr(mv[:, s], stats[:, s]))
                        c.wait()
                        dve.wait_ge(applied, n * KT + KT)
                        rsqrt(c, mv[:, :, 1], [tmp[:, k] for k in range(5)], rstd[:, u])
                        dve.scalar_tensor_tensor(out=nmr[:, u], in0=mv[:, :, 0], scalar=-1.0, in1=rstd[:, u],
                                                 op0=ALU.mult, op1=ALU.mult).then_inc(scales, 1)
                        c.end()



def constants():
    bf = mybir.dt.np(BF16)
    start = 2.0 ** (-2.0 ** (-(math.log2(H) - 3)))
    slopes = np.array([start * start ** i for i in range(H)], np.float32)
    rest = -slopes[:, None] * np.arange(T, dtype=np.float32)[None, :]
    key_const = np.ones((H, 6, T), bf)
    for a in range(3):
        key_const[:, a] = rest.astype(bf)
        rest = rest - key_const[:, a].astype(np.float32)
    p = np.arange(P)
    wide = np.where(np.arange(T + QB - P)[None, :] - (T - P) > p[:, None], MASKED, 0.0)
    return {
        "key_const": key_const,
        "q_const": np.ones((3, G, QB), bf),
        "no_shift": np.zeros((H, 3 * T), bf),
        "cmask": np.where(p[:, None] > p[None, :], MASKED, 0.0).astype(bf),
        "wide": wide.astype(bf),
        "ident_b": np.eye(P, dtype=bf),
        "ident": np.eye(P, dtype=np.float32),
        "headsel": (p[:, None] // DH == np.arange(8)[None, :]).astype(bf),
        "before": (p[:, None] < p[None, :]).astype(bf),
        "ones": np.ones((P, P), bf),
        "iota": np.ascontiguousarray(np.broadcast_to(np.arange(E, dtype=np.float32), (P, KT, 2, E))),
    }


def kernel(**inputs):
    import concourse.bacc as bacc
    from concourse.bass_utils import run_bass_kernel_spmd as run

    a = {k[3:]: np.asarray(v) for k, v in inputs.items()}
    arrays = {
        "x": a["attn_x"][0], "xT": a["attn_x"][0].T, "WpT": a["attn_Wp"].T, "Wp": a["attn_Wp"], "Wg": a["ffn_Wg"],
        "W1": a["ffn_W1"], "W2": a["ffn_W2"], "b2": a["ffn_b2"],
        "b1T": a["ffn_b1"].reshape(E, HC, P).transpose(2, 0, 1),
    }
    for w in "qkv":
        arrays["W" + w] = a["attn_W" + w].T
        arrays["A" + w] = a["attn_A" + w].T
        arrays["B" + w] = a["attn_B" + w]
    arrays.update(constants())
    arrays = {k: np.ascontiguousarray(v) for k, v in arrays.items()}
    nc = bacc.Bacc("TRN2", target_bir_lowering=False, num_devices=1)
    io = {k: nc.dram_tensor("in_" + k, v.shape, mybir.dt.from_np(v.dtype), kind="ExternalInput").ap()
          for k, v in arrays.items()}
    io["out"] = nc.dram_tensor("out_0", (1, T, D), F32, kind="ExternalOutput").ap()
    build(nc, io)
    r = run(nc, [{"in_" + k: v for k, v in arrays.items()}], core_ids=[0])
    return r.results[0]["out_0"]
```

```python
import math
from contextlib import ExitStack

import numpy as np

import concourse.bass as bass
from concourse import mybir

F32 = mybir.dt.float32
BF16 = mybir.dt.bfloat16
I32 = mybir.dt.int32
U32 = mybir.dt.uint32
ACT = mybir.ActivationFunctionType
ALU = mybir.AluOpType
AX = mybir.AxisListType

P = 128
T = 4096
D = 256
H = 16
DH = D // H
G = 4
NG = H // G
QB = 512
NB = T // QB
KT = QB // P
R = 8
LORA_SCALE = 2.0
EPS = 1e-5

PAIRS = [(0, 0), (0, 1), (1, 0), (1, 1), (0, 2), (2, 0)]
NP_ROWS = 16 * len(PAIRS)
ROW_BIAS = NP_ROWS
ROW_SHIFT = NP_ROWS + 3
KROWS = NP_ROWS + 6
BOUND = 60.0
MASKED = -1e30

E = 8
HID = 1024
CAP = int(math.ceil(T * 2 / E * 1.05))
SLOTS = E * CAP
DROPPED = SLOTS
HC = HID // P
ST = -(-CAP // P)
LAST = CAP - (ST - 1) * P
LATE = (H - G) * DH - P
ROW = D + 2
ROWS_X = 17
SLOT_ROWS = 4 * ROWS_X * P
assert SLOT_ROWS >= SLOTS
NOBODY = 4.0 * T
ROWS_Y = 11
ENTRY_ROWS = 6 * ROWS_Y * P
assert ENTRY_ROWS >= 2 * T and ROWS_X * ROW + ROWS_Y * D <= NB * KT * D


def alone(eng):
    eng.sem_inc(PASSED["sem"], 1)


PASSED = {}


class Chain:

    def __init__(self, eng, sem, base, steps):
        self.eng, self.sem, self.base, self.steps, self.n = eng, sem, base, steps, 0

    def did(self, ins):
        self.n += 1
        ins.then_inc(self.sem, 1)

    def wait(self):
        self.eng.wait_ge(self.sem, self.base + self.n)

    def end(self):
        assert self.n == self.steps, (self.n, self.steps)


def tiles_before(g, b):
    return g * (2 * NB * (NB + 1)) + 2 * b * (b + 1)


def build(nc, io):
    with ExitStack() as ctx:
        def sb(name, shape, dt, c=ctx):
            return c.enter_context(nc.sbuf_tensor(name, shape, dt))

        def psum(name, shape, dt, c):
            return c.enter_context(nc.psum_tensor(name, shape, dt))

        def sem(name):
            return ctx.enter_context(nc.semaphore(name))

        def dram(name, shape, dt):
            return nc.dram_tensor(name, shape, dt, kind="Internal").ap()

        parts = {m: dram(f"parts_{m}", (3, D, T), BF16) for m in "qk"}
        shift = dram("shift", (H, 3, T), BF16)
        attnT = dram("attnT", (D, T), F32)
        slots_x = dram("slots_x", (SLOT_ROWS, ROW), F32)
        entries_y = dram("entries_y", (ENTRY_ROWS, D), F32)

        flag = sb("flag", [1, 1], I32)
        x1_all = sb("x1_all", [P, NB, KT, D], F32)
        dest_all = sb("dest_all", [P, NB, KT * 2], U32)
        weight_all = sb("weight_all", [P, NB, KT * 2], F32)
        PASSED["sem"] = sem("passed")
        with ExitStack() as mid:
            r = Router(io, lambda n, sh, dt: sb(n, sh, dt, mid), sem, attnT, slots_x, x1_all, dest_all, weight_all)
            attention(nc, io, sb, psum, sem, parts, shift, attnT, flag, slots_x, entries_y, r)
            with ExitStack() as st:
                ex = Experts(lambda n, sh, dt: sb(n, sh, dt, st), sem)
                route_last(nc, io, psum, r, ex)
                experts(nc, io, psum, slots_x, entries_y, ex)
        combine(nc, io, sb, psum, sem, x1_all, entries_y, weight_all)


def attention(nc, io, sb, psum, sem, parts, shift, attnT, flag, slots_x, entries_y, r):
    with ExitStack() as big:
        v_sb = sb("v_sb", [P, T // P, D + E], F32, big)
        kop = sb("kop", [KROWS, 2, G, T], BF16, big)
        qop = sb("qop", [KROWS, 2, G, QB], BF16, big)
        ident_b = sb("ident_b", [P, P], BF16, big)
        cmask = sb("cmask", [P, P], BF16, big)
        v_stage = sb("v_stage", [P, KT, G, 32], F32, big)

        project(nc, io, sb, psum, sem, parts, shift, flag, v_sb, qop, ident_b, cmask, v_stage,
                slots_x, r.x1[:].rearrange("p n t d -> p (n t d)"))
        exact_maxima(nc, io, sb, psum, sem, parts, shift, flag, kop, qop, ident_b)
        attend(nc, io, sb, psum, sem, parts, shift, attnT, kop, qop, ident_b, cmask, v_stage, v_sb, r, entries_y)



def project(nc, io, sb, psum, sem, parts, shift, flag, v_sb, qop, ident_b, cmask, v_stage,
            slots_x, spare):
    with ExitStack() as st:
        wT = sb("wT", [P, 3, 2, D], F32, st)
        loA = sb("loA", [R, 3, D], F32, st)
        loB = sb("loB", [R, 3, D], F32, st)
        weff = sb("weff", [P, 3, 2, D + E], F32, st)
        xT = sb("xT", [P, 2, 2, QB], F32, st)
        part = sb("part", [P, 4, 3, QB], BF16, st)
        resid = sb("resid", [P, 2, QB], F32, st)
        sq = sb("sq", [P, 2, QB], BF16, st)
        hsel = sb("hsel", [P, 8], BF16, st)
        ident8 = sb("ident8", [8, 8], F32, st)
        nmax = sb("nmax", [8, 4, NB], F32, st)
        nm = sb("nm", [8, 4], F32, st)
        bnd = sb("bnd", [8, 2], F32, st)
        bnd1 = sb("bnd1", [8, 1], F32, st)
        one = sb("one", [1, 2], F32, st)
        warm = sb("warm", [1, 1], F32, st)
        zero_set = sem("zero_set")
        zero_out = sem("zero_out")
        ps_p = psum("ps_p", [P, 4, QB], F32, st)
        ps_v = psum("ps_v", [P, 2, QB], F32, st)
        ps_n = psum("ps_n", [P, 2, QB], F32, st)

        lora_loaded = sem("lora_loaded")
        w_loaded = sem("w_loaded")
        small_loaded = sem("small_loaded")
        x_loaded = [sem(f"x_loaded{u}") for u in range(2)]
        lora_mm = sem("lora_mm")
        weff_done = sem("weff_done")
        proj_mm = sem("proj_mm")
        v_mm = sem("v_mm")
        v_out = sem("v_out")
        head_done = sem("head_done")
        sq_done = sem("sq_done")
        resid_done = sem("resid_done")
        mid_done = sem("mid_done")
        tail_done = sem("tail_done")
        norm_mm = sem("norm_mm")
        norm_max = sem("norm_max")
        stored = [sem(f"stored{m}") for m in range(4)]
        shift_out = sem("shift_out")
        bnd_step = sem("bnd_step")
        bnd_T = sem("bnd_T")
        ones_set = sem("ones_set")

        nc.sync.sem_inc(resid_done, 4)
        nc.sync.sem_inc(sq_done, 4)
        nc.sync.sem_inc(norm_mm, 2)
        nc.sync.sem_inc(norm_max, 2)
        nc.sync.sem_inc(tail_done, 2)
        nc.sync.sem_inc(v_out, 2)
        for s in stored:
            nc.sync.sem_inc(s, 16)

        xT_d = io["xT"].rearrange("(c p) t -> p c t", p=P)
        with nc.Block() as block:
            @block.sync
            def _(sp):
                for m, w in enumerate("qkv"):
                    sp.dma_start(loA[:, m, :], io["A" + w]).then_inc(lora_loaded, 16)
                    sp.dma_start(loB[:, m, :], io["B" + w]).then_inc(lora_loaded, 16)
                for m, w in enumerate("qkv"):
                    sp.dma_start(wT[:, m], io["W" + w].rearrange("(c p) o -> p c o", p=P)).then_inc(w_loaded, 16)
                sp.dma_start(weff[:, 2, :, D:], io["Wg"].rearrange("(c p) e -> p c e", p=P)).then_inc(w_loaded, 16)
                for u in range(2):
                    sp.dma_start(xT[:, u], xT_d[:, :, u * QB:(u + 1) * QB]).then_inc(x_loaded[u], 16)
                sp.dma_start(hsel[:], io["headsel"]).then_inc(small_loaded, 16)
                sp.dma_start(ident8[:], io["ident"][0:8, 0:8]).then_inc(small_loaded, 16)
                sp.dma_start(ident_b[:], io["ident_b"]).then_inc(small_loaded, 16)
                sp.dma_start(cmask[:], io["cmask"]).then_inc(small_loaded, 16)
                for s in range(2):
                    sp.dma_start(qop[ROW_BIAS:ROW_SHIFT, s], io["q_const"][0:3]).then_inc(small_loaded, 16)
                sp.dma_start(shift.rearrange("h a t -> h (a t)"), io["no_shift"]).then_inc(shift_out, 16)

                def store(m, tb):
                    sp.wait_ge(tail_done, tb * 4 + (m + 1 + 2))
                    dst = parts["qk"[m // 2]][:, (m % 2) * P:(m % 2 + 1) * P, bass.ds(tb * QB, QB)]
                    sp.dma_start(dst.rearrange("a p t -> p a t"), part[:, m]).then_inc(stored[m], 16)

                with sp.Fori(0, NB // 2 - 1) as i:
                    for u in range(2):
                        tb = 2 * i + u
                        for m in range(4):
                            store(m, tb)
                        sp.wait_ge(v_mm, tb * KT + KT)
                        sp.dma_start(xT[:, u], xT_d[:, :, bass.ds((tb + 2) * QB, QB)]).then_inc(x_loaded[u], 16)
                for tb in range(NB - 2, NB):
                    for m in range(4):
                        store(m, tb)
                sp.wait_ge(small_loaded, 16 * 6)
                for m in range(4):
                    sp.wait_ge(stored[m], 16 * (NB + 1))
                sp.wait_ge(shift_out, 16)

            @block.tensor
            def _(pe):
                pe.wait_ge(lora_loaded, 16 * 6)
                for m in range(3):
                    for c in range(2):
                        mm = pe.matmul(ps_p[:, m, c * D:(c + 1) * D], loB[:, m, c * P:(c + 1) * P], loA[:, m, :],
                                       start=True, stop=True)
                mm.then_inc(lora_mm, 1)
                pe.wait_ge(weff_done, 6)
                pe.wait_ge(w_loaded, 16 * 4)
                pe.wait_ge(small_loaded, 16 * 6)

                def norm(m, tb):
                    pe.wait_ge(sq_done, tb * 4 + (m + 1 + 4))
                    pe.wait_ge(norm_max, tb * 4 + (m + 1))
                    pe.matmul(ps_n[0:8, m % 2, :], hsel[:], sq[:, m % 2, :], start=True, stop=True).then_inc(norm_mm, 1)

                def block_of(tb, u, i):
                    pe.wait_ge(x_loaded[u], i * 16 + 16)
                    for m in range(4):
                        pe.wait_ge(resid_done, tb * 4 + (m + 1))
                        pe.wait_ge(sq_done, tb * 4 + (m + 1))
                        for c in range(2):
                            mm = pe.matmul(ps_p[:, m, :], weff[:, m // 2, c, (m % 2) * P:(m % 2 + 1) * P],
                                           xT[:, u, c, :], start=(c == 0), stop=(c == 1))
                        mm.then_inc(proj_mm, 1)
                        if m >= 1:
                            norm(m - 1, tb)
                    for s in range(KT):
                        pe.wait_ge(v_out, tb * KT + (s + 1))
                        for c in range(2):
                            mm = pe.matmul(ps_v[:, s % 2, 0:D + E], xT[:, u, c, s * P:(s + 1) * P],
                                           weff[:, 2, c, :], start=(c == 0), stop=(c == 1))
                        mm.then_inc(v_mm, 1)
                        if s == 1:
                            norm(3, tb)

                with pe.Fori(0, NB // 2) as i:
                    for u in range(2):
                        block_of(2 * i + u, u, i)
                pe.wait_ge(bnd_step, 3)
                pe.transpose(ps_n[0:1, 0, 0:8], bnd1[:], ident8[:]).then_inc(bnd_T, 1)

            @block.scalar
            def _(act):
                def tile(m, tb):
                    scale = 0.25 if m < 2 else 1.0
                    act.wait_ge(proj_mm, tb * 4 + (m + 1))
                    act.wait_ge(stored[m], tb * 16 + 16)
                    act.activation(part[:, m, 0, :], ps_p[:, m, :], ACT.Identity, scale=scale).then_inc(head_done, 1)
                    act.wait_ge(norm_mm, tb * 4 + (m + 1))
                    act.activation(sq[:, m % 2, :], ps_p[:, m, :], ACT.Square, scale=scale).then_inc(sq_done, 1)

                act.wait_ge(ones_set, 1)
                act.activation(warm[:], v_stage[0:1, 0, 0, 0:1], ACT.Exp)
                with act.Fori(0, NB) as tb:
                    for m in range(4):
                        tile(m, tb)
                    for s in range(KT):
                        act.wait_ge(v_mm, tb * KT + (s + 1))
                        alone(act)
                        act.activation(v_sb[:, bass.ds(tb * KT + s, 1), :].rearrange("p o d -> p (o d)"), ps_v[:, s % 2, 0:D + E],
                                       ACT.Identity).then_inc(v_out, 1)

            @block.vector
            def _(dve):
                dve.memset(v_stage[:], 1.0).then_inc(ones_set, 1)
                dve.wait_ge(lora_mm, 1)
                dve.wait_ge(w_loaded, 16 * 4)
                for m in range(3):
                    for c in range(2):
                        dve.scalar_tensor_tensor(out=weff[:, m, c, 0:D], in0=ps_p[:, m, c * D:(c + 1) * D],
                                                 scalar=LORA_SCALE, in1=wT[:, m, c, :], op0=ALU.mult,
                                                 op1=ALU.add).then_inc(weff_done, 1)

                def tile(m, tb):
                    scale = 0.25 if m < 2 else 1.0
                    dve.wait_ge(head_done, tb * 4 + (m + 1))
                    dve.wait_ge(sq_done, tb * 4 + (m + 1 + 4))
                    dve.wait_ge(tail_done, tb * 4 + (m + 1))
                    dve.scalar_tensor_tensor(out=resid[:, m % 2, :], in0=ps_p[:, m, :], scalar=scale,
                                             in1=part[:, m, 0, :], op0=ALU.mult,
                                             op1=ALU.subtract).then_inc(resid_done, 1)
                    dve.wait_ge(resid_done, tb * 4 + (m + 1 + 4))
                    dve.tensor_copy(part[:, m, 1, :], resid[:, m % 2, :]).then_inc(mid_done, 1)
                    dve.wait_ge(norm_mm, tb * 4 + (m + 1 + 2))
                    dve.tensor_reduce(nmax[:, m, bass.ds(tb, 1)], ps_n[0:8, m % 2, :], AX.X, ALU.max).then_inc(norm_max, 1)

                with dve.Fori(0, NB) as tb:
                    for m in range(4):
                        tile(m, tb)
                dve.wait_ge(norm_max, 4 * NB + 2)
                dve.tensor_reduce(nm[:], nmax[:], AX.X, ALU.max).then_inc(bnd_step, 1)
                dve.wait_ge(bnd_step, 1)
                dve.tensor_tensor(bnd[:], nm[:, 0:2], nm[:, 2:4], ALU.mult).then_inc(bnd_step, 1)
                dve.wait_ge(bnd_step, 2)
                dve.tensor_reduce(bnd1[:], bnd[:], AX.X, ALU.max).then_inc(bnd_step, 1)
                dve.wait_ge(bnd_T, 1)
                dve.tensor_reduce(one[:, 0:1], ps_n[0:1, 0, 0:8], AX.X, ALU.max).then_inc(bnd_step, 1)
                dve.wait_ge(bnd_step, 4)
                dve.tensor_scalar(one[:, 1:2], one[:, 0:1], 0.99 * BOUND * BOUND, None, ALU.is_le).then_inc(bnd_step, 1)
                dve.wait_ge(bnd_step, 5)
                dve.tensor_scalar(flag[:], one[:, 1:2], -1.0, 1.0, ALU.mult, ALU.add).then_inc(bnd_step, 1)

            @block.gpsimd
            def _(pool):
                pool.memset(spare, 0.0).then_inc(zero_set, 1)
                pool.wait_ge(zero_set, 1)
                empty = spare[:, 0:ROWS_X * ROW]
                pool.memset(empty.rearrange("p (r w) -> p r w", w=ROW)[:, :, D:D + 1], NOBODY).then_inc(zero_set, 1)
                flat = slots_x.rearrange("(k p r) w -> k p (r w)", k=4, p=P)
                def rest(tb):
                    for m in range(4):
                        pool.wait_ge(mid_done, tb * 4 + (m + 1))
                        alone(pool)
                        pool.tensor_tensor(part[:, m, 2, :], resid[:, m % 2, :], part[:, m, 1, :],
                                           ALU.subtract).then_inc(tail_done, 1)

                pool.wait_ge(zero_set, 2)
                with pool.Fori(0, NB // 2) as i:
                    pool.wait_ge(mid_done, i * 8 + 1)
                    alone(pool)
                    pool.dma_start(flat[i], empty).then_inc(zero_out, 16)
                    for u in range(2):
                        rest(2 * i + u)
                pool.wait_ge(zero_out, 16 * 4)


def load_keys(eng, io, parts, kop, slot_ap, g, loaded, cols=slice(0, T)):
    for s, (_, pk) in enumerate(PAIRS):
        src = parts["k"][pk].rearrange("(g h d) t -> g d h t", h=G, d=DH)
        eng.dma_start(slot_ap(16 * s, 16 * s + 16)[:, :, cols], src[g][:, :, cols]).then_inc(loaded, 16)
    src = io["key_const"].rearrange("(g h) a t -> g a h t", h=G)
    eng.dma_start(slot_ap(ROW_BIAS, KROWS)[:, :, cols], src[g][:, :, cols]).then_inc(loaded, 16)


EARLY = 2 * QB


def load_queries(eng, parts, shift, qop, slot, g, tok, loaded):
    for s, (pq, _) in enumerate(PAIRS):
        src = parts["q"][pq].rearrange("(g h d) t -> g d h t", h=G, d=DH)
        eng.dma_start(qop[16 * s:16 * s + 16, slot], src[g, :, :, tok]).then_inc(loaded, 16)
    src = shift.rearrange("(g h) a t -> g a h t", h=G)
    eng.dma_start(qop[ROW_SHIFT:KROWS, slot], src[g, :, :, tok]).then_inc(loaded, 16)


LOADS = len(PAIRS) + 1



def exact_maxima(nc, io, sb, psum, sem, parts, shift, flag, kop, qop, ident_b):
    WIDE = T + QB - P
    OFF = T - P
    with ExitStack() as st:
        wide = sb("wide", [P, WIDE], BF16, st)
        cmax = sb("cmax", [P, KT, G], F32, st)
        rmax = sb("rmax", [P, KT, G], F32, st)
        rest = sb("rest", [P, KT * G], F32, st)
        mparts = sb("mparts", [P, 3, KT * G], BF16, st)
        rows = sb("rows", [3 * KT * G, P], BF16, st)
        ps_m = psum("ps_m", [P, 2, 2, QB], F32, st)
        ps_t = psum("ps_t", [3 * KT * G, P], BF16, st)
        m_wide = sem("m_wide")
        m_kload = sem("m_kload")
        m_qload = sem("m_qload")
        m_mm = sem("m_mm")
        m_red = sem("m_red")
        m_run = sem("m_run")
        m_parts = sem("m_parts")
        m_T = sem("m_T")
        m_rows = sem("m_rows")
        m_out = sem("m_out")
        m_step = sem("m_step")
        UNITS = 2 * KT

        nc.sync.sem_inc(m_red, 2)
        nc.sync.sem_inc(m_parts, 1)
        nc.sync.sem_inc(m_T, 1)
        nc.sync.sem_inc(m_rows, 1)
        nc.sync.sem_inc(m_out, 192)

        def chunks(g, b):
            return g * (NB * (NB + 1) // 2) + (b * (b + 1)) // 2

        with nc.Block() as block:
            @block.sync
            def _(sp):
                with sp.If(sp.value_load(flag[0:1, 0:1], min_val=0, max_val=1)):
                    sp.dma_start(wide[:], io["wide"]).then_inc(m_wide, 16)
                    with sp.Fori(0, NG) as g:
                        sp.wait_ge(m_parts, g * NB + 1)
                        load_keys(sp, io, parts, kop, lambda a, z: kop[a:z, 0], g, m_kload)
                        with sp.Fori(0, NB) as b:
                            sp.wait_ge(m_parts, g * NB + b + 1)
                            load_queries(sp, parts, shift, qop, 0, g, bass.ds(b * QB, QB), m_qload)

            @block.tensor
            def _(pe):
                with pe.If(pe.value_load(flag[0:1, 0:1], min_val=0, max_val=1)):
                    pe.wait_ge(m_wide, 16)
                    with pe.Fori(0, NG) as g:
                        pe.wait_ge(m_kload, g * (16 * LOADS) + 16 * LOADS)
                        alone(pe)
                        with pe.Fori(0, NB) as b:
                            pe.wait_ge(m_qload, (g * NB + b) * (16 * LOADS) + 16 * LOADS)
                            alone(pe)
                            with pe.Fori(0, b + 1) as j:
                                here = nc.s_assert_within(OFF + j * QB - b * QB, P * (KT - 1), OFF, skip_runtime_bounds_check_because="j is at most b")
                                for n in range(UNITS):
                                    qt, half = n // 2, n % 2
                                    pe.wait_ge(m_red, (chunks(g, b) + j) * UNITS + (n + 1))
                                    for i in range(2):
                                        h = 2 * half + i
                                        out = ps_m[:, n % 2, i, :]
                                        pe.matmul(out, qop[0:ROW_SHIFT, 0, h, qt * P:(qt + 1) * P],
                                                  kop[0:ROW_SHIFT, 0, h, bass.ds(j * QB, QB)],
                                                  start=True, stop=False)
                                        mm = pe.matmul(out, ident_b[:],
                                                       wide[:, bass.ds(here - qt * P, QB)],
                                                       start=False, stop=True)
                                    mm.then_inc(m_mm, 1)
                            pe.wait_ge(m_parts, g * NB + b + 2)
                            pe.wait_ge(m_rows, g * NB + b + 1)
                            alone(pe)
                            pe.transpose(ps_t[:], mparts[:].rearrange("p a n -> p (a n)"), ident_b[:]).then_inc(m_T, 1)

            @block.vector
            def _(dve):
                with dve.If(dve.value_load(flag[0:1, 0:1], min_val=0, max_val=1)):
                    with dve.Fori(0, NG) as g:
                        with dve.Fori(0, NB) as b:
                            B = g * NB + b
                            c = Chain(dve, m_step, B * 4, 4)
                            dve.memset(rmax[:], -3e38).then_inc(m_run, 1)
                            with dve.Fori(0, b + 1) as j:
                                n0 = (chunks(g, b) + j) * UNITS
                                dve.wait_ge(m_run, (chunks(g, b) + j) + B + 1)
                                for n in range(UNITS):
                                    qt, half = n // 2, n % 2
                                    dve.wait_ge(m_mm, n0 + (n + 1))
                                    dve.tensor_reduce(cmax[:, qt, 2 * half:2 * half + 2], ps_m[:, n % 2],
                                                      AX.X, ALU.max).then_inc(m_red, 1)
                                dve.wait_ge(m_red, n0 + UNITS + 2)
                                dve.tensor_tensor(rmax[:], rmax[:], cmax[:], ALU.max).then_inc(m_run, 1)
                            dve.wait_ge(m_run, chunks(g, b) + b + B + 2)
                            dve.wait_ge(m_T, B + 1)
                            neg = rmax[:].rearrange("p a h -> p (a h)")
                            c.did(dve.tensor_scalar(mparts[:, 0, :], neg, -1.0, None, ALU.mult))
                            c.wait()
                            c.did(dve.scalar_tensor_tensor(out=rest[:], in0=neg, scalar=-1.0, in1=mparts[:, 0, :],
                                                           op0=ALU.mult, op1=ALU.subtract))
                            c.wait()
                            c.did(dve.tensor_copy(mparts[:, 1, :], rest[:]))
                            c.wait()
                            c.did(dve.tensor_tensor(mparts[:, 2, :], rest[:], mparts[:, 1, :], ALU.subtract))
                            c.wait()
                            c.end()
                            dve.tensor_copy(rest[:, 0:1], rest[:, 0:1]).then_inc(m_parts, 1)

            @block.scalar
            def _(act):
                with act.If(act.value_load(flag[0:1, 0:1], min_val=0, max_val=1)):
                    with act.Fori(0, NG) as g:
                        with act.Fori(0, NB) as b:
                            B = g * NB + b
                            act.wait_ge(m_T, B + 2)
                            act.wait_ge(m_out, B * 192 + 192)
                            act.activation(rows[:], ps_t[:], ACT.Identity).then_inc(m_rows, 1)
                            act.wait_ge(m_rows, B + 2)
                            dst = shift.rearrange("(g h) a t -> g a h t", h=G)
                            for a in range(3):
                                for qt in range(KT):
                                    r0 = a * KT * G + qt * G
                                    act.dma_start(dst[g, a, :, bass.ds(b * QB + qt * P, P)],
                                                  rows[r0:r0 + G, :]).then_inc(m_out, 16)
                    act.wait_ge(m_out, 192 * (NG * NB + 1))



THREE = ([0, 2, 1, 0, 1, 2, 0, 1],
         [2, 4, 3, 3, 2, 4, 3, 3])
TWO = ([0, 1] * 4, [2] * 8)
E0 = 5

BODIES = NB * (NB + 1) // 2
ROUTE_AT = {}
_free = 0
for _n in range(NB - 1):
    _t = max((_n + 1) * (_n + 2) // 2 + 1, _free)
    ROUTE_AT[_t] = ("project", _n)
    ROUTE_AT[_t + 1] = ("project_last", _n)
    ROUTE_AT[_t + 3] = ("count", _n)
    _free = _t + 4
SCATTER_AT = {t + 2 + k: (n, k) for t, (step, n) in ROUTE_AT.items() if step == "count" for k in range(2)}
SPLIT_AT = {t + 1: n for t, (step, n) in ROUTE_AT.items() if step == "count"}
assert max(SCATTER_AT) < BODIES


def attend(nc, io, sb, psum, sem, parts, shift, attnT, kop, qop, ident_b, cmask, v_stage, v_sb, r, entries_y):
    with ExitStack() as st:
        prob = sb("prob", [P, KT, G, QB], F32, st)
        denom = sb("denom", [P, QB], F32, st)
        recip = sb("recip", [P, QB], F32, st)
        outT = sb("outT", [P, 2, QB], F32, st)
        ps_s = psum("ps_s", [P, 3, 2, QB], F32, st)
        ps_o = psum("ps_o", [P, 2, QB], F32, st)
        k_first = sem("k_first")
        k_loaded = sem("k_loaded")
        q_loaded = [sem(f"q_loaded{s}") for s in range(2)]
        scores = sem("scores")
        exp_done = sem("exp_done")
        staged = sem("staged")
        pv_done = sem("pv_done")
        spread = sem("spread")
        inverted = sem("inverted")
        normed = sem("normed")
        out_stored = [sem(f"out_stored{s}") for s in range(2)]
        y_cleared = sem("y_cleared")

        nc.sync.sem_inc(exp_done, E0)
        nc.sync.sem_inc(pv_done, KT)
        nc.sync.sem_inc(normed, 2)
        for s in out_stored:
            nc.sync.sem_inc(s, 64)

        with nc.Block() as block:
            @block.sync
            def _(sp):
                def store(g, b):
                    sp.wait_ge(normed, g * NB + (b + 1 + 2))
                    for h in range(G):
                        sp.dma_start(attnT[bass.ds(g * G * DH + h * DH, DH), b * QB:(b + 1) * QB],
                                     outT[32 * h:32 * h + DH, b % 2, :]).then_inc(out_stored[b % 2], 16)

                def group(g, last):
                    for b in range(NB):
                        sp.wait_ge(scores, tiles_before(g, b) * 2 + KT * (b + 1) * 2)
                        if b == 0 and not last:
                            load_keys(sp, io, parts, kop, lambda a, z: kop[a:z, (g + 1) % 2], g + 1, k_first, slice(0, EARLY))
                        if b == EARLY // QB and not last:
                            load_keys(sp, io, parts, kop, lambda a, z: kop[a:z, (g + 1) % 2], g + 1, k_loaded, slice(EARLY, T))
                        if b + 2 < NB:
                            load_queries(sp, parts, shift, qop, b % 2, g, bass.ds((b + 2) * QB, QB), q_loaded[b % 2])
                        elif not last:
                            load_queries(sp, parts, shift, qop, b % 2, g + 1, bass.ds((b + 2 - NB) * QB, QB), q_loaded[b % 2])
                        if b >= 1:
                            store(g, b - 1)
                    store(g, NB - 1)

                load_keys(sp, io, parts, kop, lambda a, z: kop[a:z, 0], 0, k_first, slice(0, EARLY))
                for b in range(2):
                    load_queries(sp, parts, shift, qop, b, 0, bass.ds(b * QB, QB), q_loaded[b])
                load_keys(sp, io, parts, kop, lambda a, z: kop[a:z, 0], 0, k_loaded, slice(EARLY, T))
                r.load_constants(sp)
                with sp.Fori(0, NG - 1) as g:
                    group(g, False)
                for s in out_stored:
                    sp.wait_ge(s, 64 * ((NG - 1) * NB // 2 + 1))
                for b in range(NB):
                    if b >= 1:
                        sp.wait_ge(normed, (NG - 1) * NB + b + 2)
                        r.store(sp, b - 1, outT[:, (b - 1) % 2])
                    if b + 2 < NB:
                        sp.wait_ge(scores, tiles_before(NG - 1, b) * 2 + KT * (b + 1) * 2)
                        load_queries(sp, parts, shift, qop, b % 2, NG - 1, bass.ds((b + 2) * QB, QB), q_loaded[b % 2])
                    r.load(sp, b)
                sp.wait_ge(normed, NG * NB + 2)
                r.store(sp, NB - 1, outT[:, (NB - 1) % 2])
                for u in range(2):
                    sp.wait_ge(r.late[u], 64 * NB // 2)

            @block.tensor
            def _(pe):
                def pv(t, r, b, q0, first, last):
                    pe.wait_ge(exp_done, t * 2 + (2 + E0))
                    pe.wait_ge(staged, t + 1)
                    for h in range(G):
                        mm = pe.matmul(ps_o[32 * h:32 * h + 32, b % 2, q0:], v_stage[:, r, h, :], prob[:, r, h, q0:],
                                       start=first, stop=last)
                    mm.then_inc(pv_done, 1)

                def body(g, b, t0, kt0, diag, before, opens, ring=THREE, lag=1):
                    slot, back = ring
                    for r in range(KT):
                        q0 = r * P if diag else 0
                        for half in range(2):
                            n = 2 * r + half
                            pe.wait_ge(exp_done, t0 * 2 + (n - back[n] + 1 + E0))
                            for i in range(2):
                                h = 2 * half + i
                                out = ps_s[:, slot[n], i, :]
                                mm = pe.matmul(out[:, q0:], kop[:, g % 2, h, bass.ds(kt0 + r * P, P)],
                                               qop[:, b % 2, h, q0:], start=True, stop=not diag)
                                if diag:
                                    mm = pe.matmul(out[:, q0:q0 + P], ident_b[:], cmask[:], start=False, stop=True)
                            mm.then_inc(scores, 1)
                            if half == (1 if lag == 1 else 0):
                                if r < lag:
                                    before(r)
                                else:
                                    pv(t0 + (r - lag), r - lag, b, q0 - lag * P if diag else 0, opens and r == lag, False)

                def opening(g, b):
                    if b >= 1:
                        pv(tiles_before(g, b - 1) + (KT * b - 1), KT - 1, b - 1, (KT - 1) * P, False, True)
                    pe.wait_ge(normed, g * NB + (b + 1))

                with pe.Fori(0, NG - 1) as g:
                    pe.wait_ge(k_first, g * (16 * LOADS) + 16 * LOADS)
                    alone(pe)
                    for b in range(NB):
                        if b == EARLY // QB:
                            pe.wait_ge(k_loaded, g * (16 * LOADS) + 16 * LOADS)
                            alone(pe)
                        pe.wait_ge(q_loaded[b % 2], g * (NB // 2 * 16 * LOADS) + (b // 2 + 1) * 16 * LOADS)
                        T0 = tiles_before(g, b)

                        def first(k):
                            opening(g, b)

                        def inner(t0):
                            return lambda k: pv(t0, KT - 1, b, 0, False, False)

                        if b >= 1:
                            body(g, b, T0, 0, False, first, True)
                        if b >= 2:
                            with pe.Fori(0, b - 1) as j:
                                body(g, b, T0 + KT + j * KT, QB + j * QB, False, inner(T0 + (KT - 1) + j * KT), False)
                        body(g, b, T0 + KT * b, QB * b, True, inner(T0 + (KT * b - 1)) if b else first, b == 0)
                    pv(tiles_before(g, NB - 1) + (KT * NB - 1), KT - 1, NB - 1, (KT - 1) * P, False, True)

                g, t = NG - 1, 0

                def closing(b, k):
                    q = KT - 2 + k
                    pv(tiles_before(g, b) + (KT * b + q), q, b, q * P, False, k == 1)

                pe.wait_ge(k_first, NG * 16 * LOADS)
                pe.wait_ge(k_loaded, NG * 16 * LOADS)
                for b in range(NB):
                    pe.wait_ge(q_loaded[b % 2], (g * NB // 2 + b // 2 + 1) * 16 * LOADS)
                    T0 = tiles_before(g, b)
                    for j in range(b + 1):
                        def before(k):
                            if j:
                                pv(T0 + KT * j - 2 + k, KT - 2 + k, b, 0, False, False)
                            elif b:
                                closing(b - 1, k)
                            if j == 0 and k == 1:
                                pe.wait_ge(normed, g * NB + b + 1)

                        body(g, b, T0 + KT * j, QB * j, j == b, before, j == 0, TWO, lag=2)
                        if t == 0:
                            r.pe_setup(pe, ps_s[:, 2, 0])
                        r.pe_step(pe, ROUTE_AT.get(t), ps_s[:, 2])
                        t += 1
                for k in range(2):
                    closing(NB - 1, k)

            @block.scalar
            def _(act):
                def body(t0, diag, ring=THREE):
                    for r in range(KT):
                        q0 = r * P if diag else 0
                        act.wait_ge(pv_done, t0 + (r + 1))
                        for half in range(2):
                            act.wait_ge(scores, t0 * 2 + (2 * r + half + 1))
                            act.activation(prob[:, r, 2 * half:2 * half + 2, q0:],
                                           ps_s[:, ring[0][2 * r + half], :, q0:], ACT.Exp).then_inc(exp_done, 1)

                with act.Fori(0, NG - 1) as g:
                    for b in range(NB):
                        T0 = tiles_before(g, b)
                        if b >= 1:
                            with act.Fori(0, b) as j:
                                body(T0 + j * KT, False)
                        body(T0 + KT * b, True)
                for b in range(NB):
                    T0 = tiles_before(NG - 1, b)
                    if b >= 1:
                        with act.Fori(0, b) as j:
                            body(T0 + j * KT, False, TWO)
                    body(T0 + KT * b, True, TWO)

            @block.gpsimd
            def _(pool):
                def body(g, t0, kt0, scatter=None):
                    for q in range(KT):
                        pool.wait_ge(pv_done, t0 + (q + 1))
                        alone(pool)
                        src = v_sb[:, bass.ds(kt0 + q, 1), bass.ds(g * (G * DH), G * DH)]
                        pool.tensor_copy(v_stage[:, q, :, 0:DH], src.rearrange("p o (h d) -> p (o h) d", h=G)).then_inc(staged, 1)
                        if scatter:
                            n, half = scatter
                            r.scatter(pool, n, half * KT + q)

                spare = r.x1[:].rearrange("p n t d -> p (n t d)")[:, ROWS_X * ROW:ROWS_X * ROW + ROWS_Y * D]
                flat = entries_y.rearrange("(k p r) d -> k p (r d)", k=6, p=P)
                with pool.Fori(0, NG - 1) as g:
                    for b in range(NB):
                        with pool.Fori(0, b + 1) as j:
                            body(g, tiles_before(g, b) + j * KT, j * KT)
                        if b in (3, 5):
                            pool.dma_start(flat[2 * g + b // 5], spare).then_inc(y_cleared, 16)
                pool.wait_ge(y_cleared, 16 * 6)
                r.cleared(pool)
                g, t = NG - 1, 0
                for b in range(NB):
                    for j in range(b + 1):
                        if t in SPLIT_AT:
                            r.split(pool, SPLIT_AT[t])
                        body(g, tiles_before(g, b) + j * KT, j * KT, SCATTER_AT.get(t))
                        t += 1
                r.pool_end(pool)

            @block.vector
            def _(dve):
                spread_mask = [DH + i % DH for i in range(32)]

                def normalise(g, b, late=False):
                    n = g * NB + (b + 1)
                    dve.wait_ge(pv_done, tiles_before(g, b) + (KT * (b + 1) + KT))
                    alone(dve)
                    dve.stream_shuffle(denom[:], ps_o[:, b % 2, :], spread_mask).then_inc(spread, 1)
                    dve.wait_ge(spread, n)
                    dve.reciprocal(recip[:], denom[:]).then_inc(inverted, 1)
                    dve.wait_ge(inverted, n)
                    if late and b >= 2:
                        dve.wait_ge(r.late[b % 2], 64 * (b // 2))
                    else:
                        dve.wait_ge(out_stored[b % 2], g * (64 * NB // 2) + 64 * (b // 2 + 1 if not late else 1))
                    dve.tensor_tensor(outT[:, b % 2, :], ps_o[:, b % 2, :], recip[:], ALU.mult).then_inc(normed, 1)

                with dve.Fori(0, NG - 1) as g:
                    for b in range(NB):
                        normalise(g, b)
                r.dve_constants(dve, v_sb)
                t = 0
                for b in range(NB):
                    for j in range(b + 1):
                        if j == 0 and b >= 1:
                            normalise(NG - 1, b - 1, True)
                        if t == 0:
                            r.dve_setup(dve, ps_s[:, 2, 0])
                        r.dve_step(dve, ROUTE_AT.get(t), ps_s[:, 2])
                        t += 1
                normalise(NG - 1, NB - 1, True)



RSQRT_MAGIC = 0x5F3759DF
NEWTON = 3
RSQRT_STEPS = 3 + 3 * NEWTON


def rsqrt(c, var, tmp, out):
    dve = c.eng
    v, sq, half, a, b = tmp
    c.did(dve.tensor_scalar(v, var, EPS, None, ALU.add))
    c.wait()
    c.did(dve.tensor_scalar(a.bitcast(I32), v.bitcast(I32), 1, None, ALU.arith_shift_right))
    c.wait()
    c.did(dve.tensor_scalar(b.bitcast(I32), a.bitcast(I32), -1, RSQRT_MAGIC, ALU.mult, ALU.add))
    c.wait()
    root = b
    for k in range(NEWTON):
        to = out if k == NEWTON - 1 else (a, b)[k % 2]
        c.did(dve.tensor_tensor(sq, root, root, ALU.mult))
        c.wait()
        c.did(dve.scalar_tensor_tensor(out=half, in0=sq, scalar=-0.5, in1=v, op0=ALU.mult, op1=ALU.mult))
        c.wait()
        c.did(dve.scalar_tensor_tensor(out=to, in0=half, scalar=1.5, in1=root, op0=ALU.add, op1=ALU.mult))
        c.wait()
        root = to


class Router:

    STEPS = 4 + 4 + RSQRT_STEPS + 3 + 4 + 4 + 1 + 1 + 2 + 3 + 1 + 1 + 1 + 1 + 1
    CONSTANTS = 7

    def __init__(r, io, sb, sem, attnT, slots_x, x1_all, dest_all, weight_all):
        r.io, r.attnT, r.slots_x, r.x1, r.dest_all, r.weight_all = io, attnT, slots_x, x1_all, dest_all, weight_all
        r.aT = sb("aT", [P, 2, 2, QB], F32)
        r.xg = sb("xg", [P, NB * KT, E], F32)
        r.xsplit = sb("xsplit", [P, KT, ROW], F32)
        r.high = r.xsplit[:, :, 0:D // 2].bitcast(BF16)
        r.low = r.xsplit[:, :, D // 2:D].bitcast(BF16)
        r.number2 = sb("number2", [P, NB, KT], F32)
        r.wp = sb("wp", [P, 2, D + E], F32)
        r.wpn = sb("wpn", [P, 2, D], F32)
        r.wg = sb("wg", [P, 2, E], F32)
        r.wsum = sb("wsum", [P, E], F32)
        r.ones_f = sb("ones_f", [P, P], F32)
        r.before = sb("before", [P, P], BF16)
        r.ones = sb("ones", [P, P], BF16)
        r.iota = sb("iota", [P, KT, 2, E], F32)
        r.stats = sb("stats", [P, KT, 6], F32)
        r.mv = sb("mv", [P, KT, 2], F32)
        r.tmp = sb("tmp", [P, 5, KT], F32)
        r.rstd = sb("rstd", [P, KT], F32)
        r.slogit = sb("slogit", [P, KT, E], F32)
        r.shiftl = sb("shiftl", [P, KT, E], F32)
        r.clogit = sb("clogit", [P, KT, E], F32)
        r.logit = sb("logit", [P, KT, E], F32)
        r.top = sb("top", [P, KT, 8], F32)
        r.topi = sb("topi", [P, KT, 8], U32)
        r.chosen = sb("chosen", [P, KT, 2], F32)
        r.hot = sb("hot", [P, KT, 2, E], F32)
        r.counts = sb("counts", [P, KT, E], BF16)
        r.ahead = sb("ahead", [P, KT, E], BF16)
        r.run = sb("run", [P, E], BF16)
        r.place = sb("place", [P, KT, 2, E], F32)
        r.pos = sb("pos", [P, KT * 2], F32)
        r.row = sb("row", [P, KT * 2], F32)
        r.row2 = sb("row2", [P, KT * 2], F32)
        r.gap_all = sb("gap_all", [P, NB, KT], F32)
        r.gexp = sb("gexp", [P, NB, KT], F32)
        r.gsum = sb("gsum", [P, NB, KT], F32)
        r.gate = sb("gate", [P, NB, KT, 2], F32)
        r.keep_all = sb("keep_all", [P, NB, KT * 2], F32)

        r.const = sem("r_const")
        r.loaded = [sem(f"r_loaded{u}") for u in range(2)]
        r.late = [sem(f"last_group_out{u}") for u in range(2)]
        r.split_high = sem("split_high")
        r.split_low = sem("split_low")
        r.spare_free = sem("spare_free")
        r.tags = sem("tags")
        r.ones_done = sem("ones_done")
        r.xg_done = sem("xg_done")
        r.setup_mm = sem("setup_mm")
        r.setup_done = sem("setup_done")
        r.y_mm = sem("y_mm")
        r.summed = sem("summed")
        r.logits_out = sem("logits_out")
        r.step = sem("r_step")
        r.x1_done = sem("x1_done")
        r.count_done = sem("count_done")
        r.c_mm = sem("c_mm")
        r.placed = sem("placed")
        r.dest_done = sem("dest_done")
        r.scattered = sem("scattered")
        r.gexp_done = sem("gexp_done")
        r.g_step = sem("g_step")
        r.weights = sem("weights")


    def load_constants(r, sp):
        io = r.io
        for dst, src in ((r.wp[:, :, 0:D], io["WpT"].rearrange("(c p) o -> p c o", p=P)),
                         (r.wpn[:], io["Wp"].rearrange("(c p) i -> p c i", p=P)),
                         (r.wg[:], io["Wg"].rearrange("(c p) e -> p c e", p=P)),
                         (r.before[:], io["before"]), (r.ones[:], io["ones"]), (r.iota[:], io["iota"]),
                         (r.number2[:], io["number2"])):
            sp.dma_start(dst, src).then_inc(r.const, 16)

    def load(r, sp, n):
        cols = slice(n * QB, (n + 1) * QB)
        if n >= 2:
            sp.wait_ge(r.y_mm, (n - 1) * KT)
        old = r.attnT[:, cols]
        sp.dma_start(r.aT[:, n % 2, 0], old[0:P]).then_inc(r.loaded[n % 2], 16)
        sp.dma_start(r.aT[0:LATE, n % 2, 1], old[P:P + LATE]).then_inc(r.loaded[n % 2], 16)
        x = r.io["x"].rearrange("(n t p) d -> n p t d", t=KT, p=P)
        if n == 0:
            sp.wait_ge(r.spare_free, 1)
        sp.dma_start(r.x1[:, n], x[n]).then_inc(r.loaded[n % 2], 16)

    def store(r, sp, n, out):
        if n >= 2:
            sp.wait_ge(r.y_mm, (n - 1) * KT)
        for h in range(G):
            sp.dma_start(r.aT[LATE + h * DH:LATE + (h + 1) * DH, n % 2, 1], out[32 * h:32 * h + DH]).then_inc(r.late[n % 2], 16)


    def pe_setup(r, pe, bank):
        pe.wait_ge(r.const, 16 * r.CONSTANTS)
        pe.wait_ge(r.ones_done, 1)
        for i in range(2):
            for c in range(2):
                pe.matmul(bank[:, i * E:(i + 1) * E], r.wpn[:, c, i * P:(i + 1) * P], r.wg[:, c, :],
                          start=(c == 0), stop=(c == 1))
        for c in range(2):
            mm = pe.matmul(bank[:, 2 * E:3 * E], r.ones_f[:], r.wg[:, c, :], start=(c == 0), stop=(c == 1))
        mm.then_inc(r.setup_mm, 1)

    def pe_step(r, pe, step, banks):
        if step is None:
            return
        what, n = step
        u = n % 2

        def tile(s, out):
            for c in range(2):
                mm = pe.matmul(out, r.aT[:, u, c, s * P:(s + 1) * P], r.wp[:, c, :], start=(c == 0), stop=(c == 1))
            mm.then_inc(r.y_mm, 1)

        if what == "project":
            pe.wait_ge(r.loaded[u], 48 * (n // 2 + 1))
            pe.wait_ge(r.late[u], 64 * (n // 2 + 1))
            if n == 0:
                pe.wait_ge(r.setup_done, 2)
            else:
                pe.wait_ge(r.placed, n)
            for s in range(2):
                tile(s, banks[:, s, 0:D + E])
        elif what == "project_last":
            for s in range(2, KT):
                pe.wait_ge(r.summed, n * KT + s - 1)
                pe.wait_ge(r.logits_out, n * KT + s - 1)
                tile(s, banks[:, s % 2, 0:D + E])
        else:
            pe.wait_ge(r.count_done, n + 1)
            out = banks[:, 0, 0:KT * E]
            pe.matmul(out, r.before[:], r.counts[:].rearrange("p s e -> p (s e)"), start=True, stop=False)
            pe.matmul(out, r.ones[:], r.ahead[:].rearrange("p s e -> p (s e)"), start=False, stop=True).then_inc(r.c_mm, 1)


    def dve_constants(r, dve, v_sb):
        dve.tensor_copy(r.xg[:], v_sb[:, :, D:D + E]).then_inc(r.xg_done, 1)
        dve.memset(r.ones_f[:], 1.0).then_inc(r.ones_done, 1)
        dve.memset(r.run[:], 0.0).then_inc(r.ones_done, 1)
        dve.wait_ge(r.const, 16 * r.CONSTANTS)
        dve.wait_ge(r.xg_done, 1)

    def dve_setup(r, dve, bank):
        dve.wait_ge(r.setup_mm, 1)
        dve.tensor_copy(r.wp[:, :, D:], bank[:, 0:2 * E].rearrange("p (c e) -> p c e", c=2)).then_inc(r.setup_done, 1)
        dve.tensor_copy(r.wsum[:], bank[:, 2 * E:3 * E]).then_inc(r.setup_done, 1)

    def dve_step(r, dve, step, banks):
        if step is None:
            return
        what, n = step
        if what != "count":
            for s in (range(2) if what == "project" else range(2, KT)):
                dve.wait_ge(r.y_mm, n * KT + s + 1)
                dve.tensor_tensor(r.slogit[:, s], banks[:, s % 2, D:D + E], r.xg[:, n * KT + s], ALU.add).then_inc(r.logits_out, 1)
                dve.tensor_tensor(r.x1[:, n, s], banks[:, s % 2, 0:D], r.x1[:, n, s], ALU.add).then_inc(r.summed, 1)
        if what == "project_last":
            r.choose(dve, n)
        if what == "count":
            r.places(dve, n, banks)

    def choose(r, dve, n):
        c = Chain(dve, r.step, n * r.STEPS, r.STEPS)
        r.chain = c
        layernorm_stats(c, lambda s: dve.wait_ge(r.summed, n * KT + (s + 1)), lambda s: r.x1[:, n, s], r.stats, r.mv)
        rsqrt(c, r.mv[:, :, 1], [r.tmp[:, k] for k in range(5)], r.rstd[:])
        for s in range(KT):
            dve.tensor_scalar(r.x1[:, n, s], r.x1[:, n, s], r.mv[:, s, 0:1], r.rstd[:, s:s + 1],
                              ALU.subtract, ALU.mult).then_inc(r.x1_done, 1)
        mean = r.mv[:, :, 0:1].broadcast_to([P, KT, E])
        c.did(dve.tensor_tensor(r.shiftl[:], mean, r.wsum[:].unsqueeze(1).broadcast_to([P, KT, E]), ALU.mult))
        c.wait()
        dve.wait_ge(r.logits_out, (n + 1) * KT)
        c.did(dve.tensor_tensor(r.clogit[:], r.slogit[:], r.shiftl[:], ALU.subtract))
        c.wait()
        c.did(dve.tensor_tensor(r.logit[:], r.clogit[:], r.rstd[:].unsqueeze(2).broadcast_to([P, KT, E]), ALU.mult))
        c.wait()
        for s in range(KT):
            c.did(dve.max(r.top[:, s], r.logit[:, s]))
        c.wait()
        for s in range(KT):
            c.did(dve.max_index(r.topi[:, s], r.top[:, s], r.logit[:, s]))
        c.wait()
        c.did(dve.tensor_copy(r.chosen[:], r.topi[:, :, 0:2]))
        c.wait()
        c.did(dve.tensor_tensor(r.hot[:], r.iota[:], r.chosen[:].unsqueeze(3).broadcast_to([P, KT, 2, E]), ALU.is_equal))
        c.wait()
        c.did(dve.tensor_tensor(r.counts[:], r.hot[:, :, 0], r.hot[:, :, 1], ALU.add))
        if n == 0:
            dve.wait_ge(r.ones_done, 2)
        c.did(dve.tensor_copy(r.ahead[:, 0], r.run[:]))
        c.wait()
        for s in range(1, KT):
            c.did(dve.tensor_tensor(r.ahead[:, s], r.ahead[:, s - 1], r.counts[:, s - 1], ALU.add))
            c.wait()
        dve.tensor_tensor(r.run[:], r.ahead[:, KT - 1], r.counts[:, KT - 1], ALU.add).then_inc(r.count_done, 1)
        c.did(dve.tensor_tensor(r.gap_all[:, n], r.top[:, :, 1], r.top[:, :, 0], ALU.subtract))
        if n >= 1:
            dve.wait_ge(r.scattered, n * KT * 2 * 16)
        dve.tensor_copy(r.xsplit[:, :, D:D + 1], r.number2[:, n].unsqueeze(2)).then_inc(r.tags, 1)
        dve.tensor_copy(r.xsplit[:, :, D + 1:D + 2], r.chosen[:, :, 0:1]).then_inc(r.tags, 1)

    def places(r, dve, n, banks):
        c = r.chain
        dve.wait_ge(r.c_mm, n + 1)
        ahead = banks[:, 0, 0:KT * E].rearrange("p (s e) -> p s e", s=KT)
        dve.tensor_tensor(r.place[:], r.hot[:], ahead.unsqueeze(2).broadcast_to([P, KT, 2, E]), ALU.mult).then_inc(r.placed, 1)
        dve.wait_ge(r.placed, n + 1)
        c.did(dve.tensor_reduce(r.pos[:], r.place[:].rearrange("p s k e -> p (s k) e"), AX.X, ALU.add))
        c.wait()
        c.did(dve.tensor_scalar(r.keep_all[:, n], r.pos[:], float(CAP), None, ALU.is_lt))
        c.did(dve.scalar_tensor_tensor(out=r.row[:], in0=r.chosen[:].rearrange("p s k -> p (s k)"),
                                       scalar=float(CAP), in1=r.pos[:], op0=ALU.mult, op1=ALU.add))
        c.wait()
        c.did(dve.scalar_tensor_tensor(out=r.row2[:], in0=r.row[:], scalar=-float(DROPPED), in1=r.keep_all[:, n],
                                       op0=ALU.add, op1=ALU.mult))
        c.wait()
        dve.tensor_scalar(r.dest_all[:, n], r.row2[:], float(DROPPED), None, ALU.add).then_inc(r.dest_done, 1)
        c.end()

    def cleared(r, pool):
        pool.sem_inc(r.spare_free, 1)

    def split(r, pool, n):
        pool.wait_ge(r.x1_done, (n + 1) * KT)
        if n >= 1:
            pool.wait_ge(r.scattered, n * KT * 2 * 16)
        pool.tensor_copy(r.high, r.x1[:, n]).then_inc(r.split_high, 1)
        r.split_rest(pool, n)

    def split_rest(r, pool, n):
        pool.wait_ge(r.split_high, n + 1)
        pool.tensor_tensor(r.low, r.x1[:, n], r.high, ALU.subtract).then_inc(r.split_low, 1)

    def scatter(r, pool, n, m):
        if m == 0:
            pool.wait_ge(r.dest_done, n + 1)
            pool.wait_ge(r.split_low, n + 1)
            pool.wait_ge(r.tags, 2 * n + 2)
            alone(pool)
        pool.indirect_dma_start(
            out=r.slots_x, out_offset=bass.IndirectOffsetOnAxis(ap=r.dest_all[:, n, m:m + 1], axis=0),
            in_=r.xsplit[:, m // 2], in_offset=None, bounds_check=SLOTS - 1,
            oob_is_err=False).then_inc(r.scattered, 16)

    def pool_end(r, pool):
        pool.wait_ge(r.scattered, (NB - 1) * KT * 2 * 16)

    def act_gates(r, act):
        act.wait_ge(r.step, NB * r.STEPS)
        act.activation(r.gexp[:], r.gap_all[:], ACT.Exp).then_inc(r.gexp_done, 1)

    def dve_gates(r, dve):
        c = Chain(dve, r.g_step, 0, 3)
        dve.wait_ge(r.gexp_done, 1)
        c.did(dve.tensor_scalar(r.gsum[:], r.gexp[:], 1.0, None, ALU.add))
        c.wait()
        c.did(dve.reciprocal(r.gate[:, :, :, 0], r.gsum[:]))
        c.wait()
        c.did(dve.tensor_tensor(r.gate[:, :, :, 1], r.gexp[:], r.gate[:, :, :, 0], ALU.mult))
        c.wait()
        c.end()
        dve.tensor_tensor(r.weight_all[:], r.gate[:].rearrange("p n s k -> p n (s k)"), r.keep_all[:],
                          ALU.mult).then_inc(r.weights, 1)


def route_last(nc, io, psum, r, ex):
    n = NB - 1
    with ExitStack() as st:
        banks = psum("ps_r", [P, 2, QB], F32, st)
        with nc.Block() as block:
            @block.sync
            def _(sp):
                ex.load_weights(sp, io, 0, 0)
                ex.load_constants(sp, io)
                ex.load_weights(sp, io, 1, 1)

            @block.tensor
            def _(pe):
                for what in ("project", "project_last", "count"):
                    r.pe_step(pe, (what, n), banks)

            @block.vector
            def _(dve):
                for what in ("project", "project_last", "count"):
                    r.dve_step(dve, (what, n), banks)
                r.dve_gates(dve)

            @block.scalar
            def _(act):
                for k in range(2):
                    ex.weights_high(act, 0, 0, 0, k)
                act.wait_ge(r.x1_done, NB * KT)
                act.wait_ge(r.scattered, n * KT * 2 * 16)
                act.activation(r.high, r.x1[:, n], ACT.Identity).then_inc(r.split_high, 1)
                r.act_gates(act)

            @block.gpsimd
            def _(pool):
                ex.weights_low(pool, 0, 0, 0)
                r.split_rest(pool, n)
                for m in range(2 * KT):
                    r.scatter(pool, n, m)
                pool.wait_ge(r.scattered, NB * KT * 2 * 16)


def layernorm_stats(c, ready, src, stats, mv):
    dve = c.eng
    for s in range(KT):
        ready(s)
        c.did(dve.bn_stats(stats[:, s], src(s)))
    c.wait()
    alone(dve)
    for s in range(KT):
        c.did(dve.bn_aggr(mv[:, s], stats[:, s]))
    c.wait()



SB = [(0, 3), (3, 6), (6, ST)]


class Experts:

    def __init__(x, sb, sem):
        x.sb, x.sem = sb, sem
        x.w1 = sb("w1", [P, 2, 2, HID], F32)
        x.w2 = sb("w2", [P, 2, HC, D], F32)
        x.w1s = sb("w1s", [P, 2, 2, 2, HID], BF16)
        x.w2s = sb("w2s", [P, 2, 2, HC, D], BF16)
        x.b1 = sb("b1", [P, E, HC], F32)
        x.b2 = sb("b2", [P, E, D], F32)
        x.expert = sb("expert_no", [P, E, ST], F32)
        x.ident = sb("ident5", [P, P], BF16)
        x.const = sem("e_const")
        x.w_loaded = [sem(f"we_loaded{u}") for u in range(2)]
        x.ye_mm = sem("ye_mm")
        x.wh = sem("w_high")
        x.ws = sem("w_split")

    def load_constants(x, sp, io):
        sp.dma_start(x.ident[:], io["ident_b"]).then_inc(x.const, 16)
        sp.dma_start(x.b1[:], io["b1T"]).then_inc(x.const, 16)
        sp.dma_start(x.expert[:], io["expert_no"]).then_inc(x.const, 16)
        for e in range(E):
            sp.dma_start(x.b2[:, e], io["b2"][e:e + 1].broadcast_to([P, D])).then_inc(x.const, 16)

    def load_weights(x, sp, io, u, e):
        sp.dma_start(x.w1[:, u], io["W1"][e].rearrange("(c p) h -> p c h", p=P)).then_inc(x.w_loaded[u], 16)
        sp.dma_start(x.w2[:, u], io["W2"][e].rearrange("(c p) d -> p c d", p=P)).then_inc(x.w_loaded[u], 16)

    def weights_high(x, act, e, i, u, k):
        act.wait_ge(x.w_loaded[u], i * 32 + 32)
        if not (isinstance(e, int) and e < 2):
            act.wait_ge(x.ye_mm, (e - 1) * ST)
        src, dst = ((x.w1, x.w1s), (x.w2, x.w2s))[k]
        act.activation(dst[:, u, 0], src[:, u], ACT.Identity).then_inc(x.wh, 1)

    def weights_low(x, pool, e, u, k):
        src, dst = ((x.w1, x.w1s), (x.w2, x.w2s))[k]
        pool.wait_ge(x.wh, e * 2 + (k + 1))
        alone(pool)
        pool.tensor_tensor(dst[:, u, 1], src[:, u], dst[:, u, 0], ALU.subtract).then_inc(x.ws, 1)


def experts(nc, io, psum, slots_x, entries_y, X):
    sb, sem = X.sb, X.sem
    w1s, w2s, b1, b2, ident, ws, ye_mm = X.w1s, X.w2s, X.b1, X.b2, X.ident, X.ws, X.ye_mm
    with ExitStack() as st:
        warm = sb("warm5", [1, 1], F32)
        xe = sb("xe", [P, 2, ST, ROW], F32)
        other = sb("other", [P, ST], F32)
        entry = sb("entry", [P, 2, ST], U32)
        xs = sb("xs", [P, 2, 2, 2, ST * P], BF16)
        hid = sb("hid", [P, 4, 3 * P], F32)
        hs = sb("hs", [P, 2, 2, HC, 3 * P], BF16)
        y = sb("y", [P, 3, D], F32)
        ps_h = psum("ps_h", [P, 4, QB], F32, st)
        ps_y = psum("ps_y5", [P, 2, QB], F32, st)
        ps_x = psum("ps_x", [P, 2, 2 * QB], BF16, st)

        x_first = [sem(f"xe_first{u}") for u in range(2)]
        x_loaded = [sem(f"xe_loaded{u}") for u in range(2)]
        x_mm = sem("x_mm")
        x_out = sem("x_out")
        h_mm = sem("h_mm")
        gelu = sem("gelu")
        h_high = sem("h_high")
        h_low = sem("h_low")
        y_out = sem("y_out")
        tag_read = sem("tag_read")
        entry_done = sem("entry_done")
        y_stored = [sem(f"y_stored{k}") for k in range(3)]

        nc.sync.sem_inc(x_out, 2)
        nc.sync.sem_inc(h_low, 4)
        nc.sync.sem_inc(ye_mm, 2 * ST)
        nc.sync.sem_inc(h_mm, 2 * 24)
        nc.sync.sem_inc(y_out, 2)
        nc.sync.sem_inc(gelu, 4)

        def width(sbk):
            a, z = SB[sbk]
            return min(z * P, CAP) - a * P

        def rows_of(k):
            return LAST if k == ST - 1 else P

        def over_experts(eng, one):
            for u in range(2):
                one(u, 0, u, True)
            with eng.Fori(1, E // 2 - 1) as i:
                for u in range(2):
                    one(2 * i + u, i, u, True)
            for u in range(2):
                one(E - 2 + u, E // 2 - 1, u, u == 0)

        xs_d = slots_x[0:SLOTS].rearrange("(e r) d -> e r d", e=E)
        with nc.Block() as block:
            @block.sync
            def _(sp):
                def load(u, e):
                    z = SB[0][1]
                    sp.dma_start(xe[:, u, 0:z], xs_d[e, 0:z * P].rearrange("(k p) d -> p k d", p=P)).then_inc(x_first[u], 16)
                    sp.dma_start(xe[:, u, z:ST - 1], xs_d[e, z * P:(ST - 1) * P].rearrange("(k p) d -> p k d", p=P)).then_inc(x_loaded[u], 16)
                    sp.dma_start(xe[0:LAST, u, ST - 1], xs_d[e, (ST - 1) * P:CAP]).then_inc(x_loaded[u], 16)

                load(0, 0)
                load(1, 1)
                with sp.Fori(0, E // 2 - 1) as i:
                    for u in range(2):
                        e = 2 * i + u
                        sp.wait_ge(ws, e * 2 + 2)
                        sp.wait_ge(x_mm, e * ST + ST)
                        sp.wait_ge(entry_done, e * 2 + 2)
                        X.load_weights(sp, io, u, e + 2)
                        load(u, e + 2)

            @block.gpsimd
            def _(pool):
                def scatter(e, u, k):
                    n = rows_of(k)
                    pool.wait_ge(y_out, e * ST + (k + 1 + 2))
                    if k == 0:
                        pool.wait_ge(entry_done, e * 2 + 2)
                    alone(pool)
                    pool.indirect_dma_start(
                        out=entries_y, out_offset=bass.IndirectOffsetOnAxis(ap=entry[0:n, u, k:k + 1], axis=0),
                        in_=y[0:n, k % 3], in_offset=None, bounds_check=2 * T - 1,
                        oob_is_err=False).then_inc(y_stored[k % 3], 16)

                def one(e, i, u, ahead):
                    for k in range(2):
                        if ahead:
                            X.weights_low(pool, e + 1, 1 - u, k)
                        for t in range(*((SB[0], (SB[1][0], ST))[k])):
                            scatter(e, u, t)

                X.weights_low(pool, 0, 0, 1)
                over_experts(pool, one)
                for k in range(3):
                    pool.wait_ge(y_stored[k], 16 * (E * ST // 3))

            @block.tensor
            def _(pe):
                pe.wait_ge(X.const, 16 * (E + 3))

                def transpose(e, i, u, k):
                    if k == 0:
                        pe.wait_ge(x_first[u], i * 16 + 16)
                    if k == SB[0][1]:
                        pe.wait_ge(x_loaded[u], i * 32 + 32)
                    pe.wait_ge(x_out, e * ST + (k + 1))
                    alone(pe)
                    n = rows_of(k)
                    rows = xe[0:n, u, k, 0:D].bitcast(BF16)
                    for c in range(4):
                        mm = pe.transpose(ps_x[:, (ST * u + k) % 2, c * P:c * P + n], rows[:, c * P:(c + 1) * P],
                                          ident[0:n, 0:n])
                    mm.then_inc(x_mm, 1)

                def up(e, u, sbk, m):
                    w = width(sbk)
                    q = sbk * HC + m
                    pe.wait_ge(gelu, e * 24 + (q + 1))
                    a = SB[sbk][0] * P
                    terms = [(0, 0), (0, 1), (1, 0)]
                    for t, (i1, i2) in enumerate(terms):
                        for c in range(2):
                            mm = pe.matmul(ps_h[:, q % 4, 0:w], w1s[:, u, i1, c, m * P:(m + 1) * P], xs[:, u, i2, c, a:a + w],
                                           start=(t == 0 and c == 0), stop=(t == 2 and c == 1))
                    mm.then_inc(h_mm, 1)

                def down(e, i, u, sbk, ahead):
                    for k in range(*SB[sbk]):
                        if ahead:
                            transpose(e + 1, i + u, 1 - u, k)
                        n = rows_of(k)
                        o = (k - SB[sbk][0]) * P
                        pe.wait_ge(y_out, e * ST + (k + 1))
                        pe.wait_ge(h_low, e * 24 + (sbk + 1) * HC + 4)
                        for t, (i1, i2) in enumerate([(0, 0), (0, 1), (1, 0)]):
                            for m in range(HC):
                                mm = pe.matmul(ps_y[0:n, (ST * u + k) % 2, 0:D], hs[:, (3 * u + sbk) % 2, i1, m, o:o + n],
                                               w2s[:, u, i2, m, :], start=(t == 0 and m == 0), stop=(t == 2 and m == HC - 1))
                        mm.then_inc(ye_mm, 1)

                def one(e, i, u, ahead):
                    pe.wait_ge(ws, e * 2 + 2)
                    first = isinstance(e, int) and e == 0
                    pe.wait_ge(x_out, e * ST + (SB[0][1] if first else ST) + 2)
                    for m in range(HC):
                        up(e, u, 0, m)
                        if first and SB[0][1] + m < ST:
                            transpose(0, 0, 0, SB[0][1] + m)
                    if first:
                        pe.wait_ge(x_out, ST + 2)
                    for m in range(HC):
                        up(e, u, 1, m)
                    down(e, i, u, 0, ahead)
                    for m in range(HC):
                        up(e, u, 2, m)
                    down(e, i, u, 1, ahead)
                    down(e, i, u, 2, ahead)

                for k in range(*SB[0]):
                    transpose(0, 0, 0, k)
                over_experts(pe, one)

            @block.scalar
            def _(act):
                act.wait_ge(X.const, 16 * (E + 3))
                act.activation(warm[:], b1[0:1, 0, 0:1], ACT.Gelu_apprx_tanh)

                def tokens(e, u, k):
                    act.wait_ge(x_mm, e * ST + (k + 1))
                    act.wait_ge(h_mm, e * 24 + 24)
                    n = rows_of(k)
                    src = ps_x[:, (ST * u + k) % 2, 0:4 * P].rearrange("p (c n) -> p c n", c=4)
                    act.activation(xs[:, u, :, :, k * P:k * P + n].rearrange("p a c n -> p (a c) n"), src[:, :, 0:n],
                                   ACT.Identity).then_inc(x_out, 1)

                def one(e, i, u, ahead):
                    def hidden(q):
                        w = width(q // HC)
                        act.wait_ge(h_mm, e * 24 + (q + 1 + 48))
                        act.wait_ge(h_low, e * 24 + (q + 1))
                        alone(act)
                        act.activation(hid[:, q % 4, 0:w], ps_h[:, q % 4, 0:w], ACT.Gelu_apprx_tanh,
                                       bias=b1[:, e, q % HC:q % HC + 1]).then_inc(gelu, 1)

                    first = isinstance(e, int) and e == 0
                    for q in range(2 * HC):
                        hidden(q)
                        if first and SB[0][1] + q < ST:
                            tokens(0, 0, SB[0][1] + q)
                        if ahead and q in (5, 13):
                            X.weights_high(act, e + 1, i + u, 1 - u, q // HC)
                    if ahead:
                        for k in range(*SB[0]):
                            tokens(e + 1, 1 - u, k)
                    for q in range(2 * HC, 3 * HC):
                        hidden(q)
                    if ahead:
                        for k in range(SB[1][0], ST):
                            tokens(e + 1, 1 - u, k)

                for k in range(*SB[0]):
                    tokens(0, 0, k)
                over_experts(act, one)

            @block.vector
            def _(dve):
                def out(e, u, k):
                    n = rows_of(k)
                    dve.wait_ge(ye_mm, e * ST + (k + 1 + 2 * ST))
                    if not (isinstance(e, int) and e == 0 and k < 3):
                        dve.wait_ge(y_stored[k % 3], e * (16 * ST // 3) + (k // 3) * 16)
                    bias = b2[0:n, bass.ds(e, 1)].rearrange("p o d -> p (o d)")
                    dve.tensor_tensor(y[0:n, k % 3], ps_y[0:n, (ST * u + k) % 2, 0:D], bias, ALU.add).then_inc(y_out, 1)

                def split(e, u, q):
                    w = width(q // HC)
                    sl = (3 * u + q // HC) % 2
                    dve.wait_ge(gelu, e * 24 + (q + 1 + 4))
                    if q % HC == 0:
                        dve.wait_ge(ye_mm, e * ST + (ends(q // HC - 2)) + 2 * ST)
                    dve.tensor_copy(hs[:, sl, 0, q % HC, 0:w], hid[:, q % 4, 0:w]).then_inc(h_high, 1)
                    dve.wait_ge(h_high, e * 24 + (q + 1))
                    dve.tensor_tensor(hs[:, sl, 1, q % HC, 0:w], hid[:, q % 4, 0:w], hs[:, sl, 0, q % HC, 0:w],
                                      ALU.subtract).then_inc(h_low, 1)

                def ends(sbk):
                    return SB[sbk][1] if sbk >= 0 else SB[sbk % 3][1] - ST

                def entries(e, i, u):
                    dve.wait_ge(x_first[u], i * 16 + 16)
                    dve.wait_ge(x_loaded[u], i * 32 + 32)
                    if not (isinstance(e, int) and e < 2):
                        for k in range(3):
                            dve.wait_ge(y_stored[k], (e - 1) * (16 * ST // 3))
                    if isinstance(e, int) and e == 0:
                        dve.wait_ge(X.const, 16 * (E + 3))
                    parts = [(P, slice(0, ST - 1)), (LAST, slice(ST - 1, ST))]
                    for q, (n, ks) in enumerate(parts):
                        mine = X.expert[0:n, bass.ds(e, 1), ks].rearrange("p o k -> p (o k)")
                        dve.tensor_tensor(other[0:n, ks], xe[0:n, u, ks, D + 1], mine, ALU.not_equal).then_inc(tag_read, 1)
                    for q, (n, ks) in enumerate(parts):
                        dve.wait_ge(tag_read, e * 2 + q + 1)
                        dve.tensor_tensor(entry[0:n, u, ks], xe[0:n, u, ks, D], other[0:n, ks], ALU.add).then_inc(entry_done, 1)

                def one(e, i, u, ahead):
                    entries(e, i, u)
                    for q in range(2 * HC):
                        split(e, u, q)
                    for k in range(ST):
                        if k >= 1:
                            out(e, u, k - 1)
                        if k == SB[0][1] - 1:
                            for q in range(2 * HC, 3 * HC):
                                split(e, u, q)
                    out(e, u, ST - 1)

                over_experts(dve, one)



def combine(nc, io, sb, psum, sem, x1_all, entries_y, weight_all):
    with ExitStack() as st:
        ye = sb("ye", [P, 4, KT, 2, D], F32, st)
        z = sb("z", [P, 4, KT, D], F32, st)
        half = sb("half", [P, 2, KT, D], F32, st)
        sum1 = sb("sum1", [P, 2, KT, D], F32, st)
        stats = sb("statsc", [P, 2, KT, 6], F32, st)
        mv = sb("mvc", [P, 2, KT, 2], F32, st)
        tmp = sb("tmpc", [P, 5, 2, KT], F32, st)
        nmr = sb("nmr", [P, 2, KT], F32, st)
        rstd = sb("rstdc", [P, 2, KT], F32, st)
        ye_loaded = [sem(f"ye_loaded{v}") for v in range(4)]
        half_done = sem("half_done")
        sum1_done = sem("sum1_done")
        z_done = sem("z_done")
        c_step = sem("c_step")
        scales = sem("scales")
        applied = sem("applied")
        out_done = [sem(f"out_done{v}") for v in range(4)]

        ye_v = entries_y[0:2 * T].rearrange("(n s p k) d -> n p s (k d)", s=KT, p=P, k=2)
        out_v = io["out"].rearrange("o (n t p) d -> (o n) p t d", t=KT, p=P)
        with nc.Block() as block:
            @block.sync
            def _(sp):
                def store(n):
                    sp.wait_ge(applied, (n + 1) * KT)
                    sp.dma_start(out_v[n], z[:, n % 4]).then_inc(out_done[n % 4], 16)

                for n in range(NB):
                    if n >= 4:
                        sp.wait_ge(z_done, (n - 3) * KT)
                    sp.dma_start(ye[:, n % 4].rearrange("p s k d -> p s (k d)"), ye_v[n]).then_inc(ye_loaded[n % 4], 16)
                    if n >= 4 and n % 2 == 1:
                        store(n - 5)
                        store(n - 4)
                for n in range(NB - 4, NB):
                    store(n)
                for v in range(4):
                    sp.wait_ge(out_done[v], 16 * (NB // 4))

            @block.scalar
            def _(act):
                def weigh(n):
                    act.wait_ge(ye_loaded[n % 4], 16 * (n // 4 + 1))
                    if n >= 2:
                        act.wait_ge(sum1_done, (n - 1) * KT)
                    for s in range(KT):
                        act.activation(half[:, n % 2, s], ye[:, n % 4, s, 0], ACT.Identity,
                                       scale=weight_all[:, n, 2 * s:2 * s + 1]).then_inc(half_done, 1)

                def apply(i):
                    act.wait_ge(scales, i + 1)
                    for v in range(2):
                        for s in range(KT):
                            act.activation(z[:, (2 * i + v) % 4, s], z[:, (2 * i + v) % 4, s], ACT.Identity,
                                           scale=rstd[:, v, s:s + 1], bias=nmr[:, v, s:s + 1]).then_inc(applied, 1)

                for i in range(NB // 2):
                    for v in range(2):
                        weigh(2 * i + v)
                    if i >= 1:
                        apply(i - 1)
                apply(NB // 2 - 1)

            @block.gpsimd
            def _(pool):
                for n in range(NB):
                    for s in range(KT):
                        pool.wait_ge(half_done, n * KT + s + 1)
                        if n >= 2:
                            pool.wait_ge(z_done, (n - 2) * KT + s + 1)
                        pool.tensor_tensor(sum1[:, n % 2, s], half[:, n % 2, s], x1_all[:, n, s], ALU.add).then_inc(sum1_done, 1)

            @block.vector
            def _(dve):
                for i in range(NB // 2):
                    steps = 4 * KT + RSQRT_STEPS
                    c = Chain(dve, c_step, i * steps, steps)

                    def add(n, s):
                        dve.wait_ge(sum1_done, n * KT + s + 1)
                        if n >= 4 and s == 0:
                            dve.wait_ge(out_done[n % 4], 16 * (n // 4))
                        dve.scalar_tensor_tensor(out=z[:, n % 4, s], in0=ye[:, n % 4, s, 1], scalar=weight_all[:, n, 2 * s + 1:2 * s + 2],
                                                 in1=sum1[:, n % 2, s], op0=ALU.mult, op1=ALU.add).then_inc(z_done, 1)

                    def spread(n, s):
                        dve.wait_ge(z_done, n * KT + s + 1)
                        c.did(dve.bn_stats(stats[:, n % 2, s], z[:, n % 4, s]))

                    tiles = [(2 * i + v, s) for v in range(2) for s in range(KT)]
                    add(*tiles[0])
                    for q in range(1, len(tiles)):
                        add(*tiles[q])
                        spread(*tiles[q - 1])
                    spread(*tiles[-1])
                    c.wait()
                    for v in range(2):
                        for s in range(KT):
                            c.did(dve.bn_aggr(mv[:, v, s], stats[:, v, s]))
                    c.wait()
                    if i >= 1:
                        dve.wait_ge(applied, i * 2 * KT)
                    rsqrt(c, mv[:, :, :, 1], [tmp[:, k] for k in range(5)], rstd[:])
                    c.end()
                    dve.scalar_tensor_tensor(out=nmr[:], in0=mv[:, :, :, 0], scalar=-1.0, in1=rstd[:],
                                             op0=ALU.mult, op1=ALU.mult).then_inc(scales, 1)



def constants():
    bf = mybir.dt.np(BF16)
    start = 2.0 ** (-2.0 ** (-(math.log2(H) - 3)))
    slopes = np.array([start * start ** i for i in range(H)], np.float32)
    rest = -slopes[:, None] * np.arange(T, dtype=np.float32)[None, :]
    key_const = np.ones((H, 6, T), bf)
    for a in range(3):
        key_const[:, a] = rest.astype(bf)
        rest = rest - key_const[:, a].astype(np.float32)
    p = np.arange(P)
    wide = np.where(np.arange(T + QB - P)[None, :] - (T - P) > p[:, None], MASKED, 0.0)
    t = np.arange(T).reshape(NB, KT, P).transpose(2, 0, 1)
    return {
        "number2": np.ascontiguousarray(2.0 * t, dtype=np.float32),
        "expert_no": np.ascontiguousarray(np.broadcast_to(np.arange(E, dtype=np.float32)[None, :, None], (P, E, ST))),
        "key_const": key_const,
        "q_const": np.ones((3, G, QB), bf),
        "no_shift": np.zeros((H, 3 * T), bf),
        "cmask": np.where(p[:, None] > p[None, :], MASKED, 0.0).astype(bf),
        "wide": wide.astype(bf),
        "ident_b": np.eye(P, dtype=bf),
        "ident": np.eye(P, dtype=np.float32),
        "headsel": (p[:, None] // DH == np.arange(8)[None, :]).astype(bf),
        "before": (p[:, None] < p[None, :]).astype(bf),
        "ones": np.ones((P, P), bf),
        "iota": np.ascontiguousarray(np.broadcast_to(np.arange(E, dtype=np.float32), (P, KT, 2, E))),
    }


def kernel(**inputs):
    import concourse.bacc as bacc
    from concourse.bass_utils import run_bass_kernel_spmd as run

    a = {k[3:]: np.asarray(v) for k, v in inputs.items()}
    arrays = {
        "x": a["attn_x"][0], "xT": a["attn_x"][0].T, "WpT": a["attn_Wp"].T, "Wp": a["attn_Wp"], "Wg": a["ffn_Wg"],
        "W1": a["ffn_W1"], "W2": a["ffn_W2"], "b2": a["ffn_b2"],
        "b1T": a["ffn_b1"].reshape(E, HC, P).transpose(2, 0, 1),
    }
    for w in "qkv":
        arrays["W" + w] = a["attn_W" + w].T
        arrays["A" + w] = a["attn_A" + w].T
        arrays["B" + w] = a["attn_B" + w]
    arrays.update(constants())
    arrays = {k: np.ascontiguousarray(v) for k, v in arrays.items()}
    nc = bacc.Bacc("TRN2", target_bir_lowering=False, num_devices=1)
    io = {k: nc.dram_tensor("in_" + k, v.shape, mybir.dt.from_np(v.dtype), kind="ExternalInput").ap()
          for k, v in arrays.items()}
    io["out"] = nc.dram_tensor("out_0", (1, T, D), F32, kind="ExternalOutput").ap()
    build(nc, io)
    r = run(nc, [{"in_" + k: v for k, v in arrays.items()}], core_ids=[0])
    return r.results[0]["out_0"]
```
